# Optimizing a Trainium2 kernel written in Bass

```python
import numpy as np
import jax
import jax.numpy as jnp

def _softmax(x, axis=-1):
    return jax.nn.softmax(x, axis=axis)

def _gelu(x):
    return jax.nn.gelu(x, approximate=True)

def _silu(x):
    return jax.nn.silu(x)

def _sigmoid(x):
    return jax.nn.sigmoid(x)

def _layernorm(x, axis=-1, eps=1e-05):
    m = jnp.mean(x, axis=axis, keepdims=True)
    v = jnp.var(x, axis=axis, keepdims=True)
    return (x - m) / jnp.sqrt(v + eps)

def _scatter_add(tgt, idx, src, axis=0):
    return tgt.at[idx].add(src)

def _segment_sum(src, seg, n):
    return jax.ops.segment_sum(src, seg, n)
kernel_name = 'mk_flamingo_gated_d4_seqx_r8_aca9c9'

def setup_inputs(seed: int=0):
    np.random.seed(seed)
    _w = jnp.asarray

    def _rec_inputs():
        import jax
        import jax.numpy as jnp
        _rk = jax.random.key(seed)
        x = -0.000125 + 0.9999 * jax.random.normal(jax.random.fold_in(_rk, 1), (16, 128, 128), jnp.float32)
        _lenS = 128 - jax.random.randint(jax.random.fold_in(_rk, 7), (16,), 0, max(1, 128 // 4) + 1, jnp.int32)
        _lenS2 = 77 - jax.random.randint(jax.random.fold_in(_rk, 8), (16,), 0, max(1, 77 // 4) + 1, jnp.int32)
        _ctx_768P = jax.random.normal(jax.random.fold_in(_rk, 11), (16, 16, 96), jnp.float32)
        _ctx_768c = jax.random.dirichlet(jax.random.fold_in(_rk, 511), 0.3 * jnp.ones((16,), jnp.float32), (16, 77))
        _ctx_768t = jnp.einsum('bsk,bkd->bsd', _ctx_768c, _ctx_768P)
        _ctx_768t = _ctx_768t * jax.lax.rsqrt(jnp.mean(jnp.square(_ctx_768t)) + 1e-12) * 0.953939
        ctx_768 = 0.00272024 + 0.999456 * (_ctx_768t + 0.3 * jax.random.normal(jax.random.fold_in(_rk, 611), (16, 77, 96), jnp.float32))
        _g = jax.random.normal(jax.random.fold_in(_rk, 9001), (2, 4), jnp.float32)
        _g = jnp.sign(_g) * jnp.maximum(jnp.abs(_g), 1.0) + (_g == 0) * 1.0
        g_xattn = _g[0]
        g_ffn = _g[1]
        return (x, ctx_768, g_xattn, g_ffn)
    x, ctx_768, g_xattn, g_ffn = _rec_inputs()

    def _L0_xattn_setup():
        import jax, jax.numpy as jnp
        import numpy as np
        N_HEADS = 16
        DIM_EMBED = 128
        DIM_CROSS = 96
        DIM_HEAD = DIM_EMBED // N_HEADS
        key = jax.random.key(seed)
        ks = jax.random.split(key, 10)
        B, Sq, Sk = (8, 512, 77)
        s_e = 1.0 / np.sqrt(DIM_EMBED)
        s_c = 1.0 / np.sqrt(DIM_CROSS)
        return {'x': jax.random.normal(ks[0], (B, Sq, DIM_EMBED), jnp.float32), 'y': jax.random.normal(ks[1], (B, Sk, DIM_CROSS), jnp.float32), 'wq': jax.random.normal(ks[2], (DIM_EMBED, DIM_EMBED), jnp.float32) * s_e, 'bq': jax.random.normal(ks[3], (DIM_EMBED,), jnp.float32) * 0.01, 'wk': jax.random.normal(ks[4], (DIM_CROSS, DIM_EMBED), jnp.float32) * s_c, 'bk': jax.random.normal(ks[5], (DIM_EMBED,), jnp.float32) * 0.01, 'wv': jax.random.normal(ks[6], (DIM_CROSS, DIM_EMBED), jnp.float32) * s_c, 'bv': jax.random.normal(ks[7], (DIM_EMBED,), jnp.float32) * 0.01, 'wo': jax.random.normal(ks[8], (DIM_EMBED, DIM_EMBED), jnp.float32) * s_e, 'bo': jax.random.normal(ks[9], (DIM_EMBED,), jnp.float32) * 0.01}
    _L0_xattn_all = _L0_xattn_setup()
    _L0_xattn_in = {k: v for k, v in _L0_xattn_all.items() if k in ('wq', 'bq', 'wk', 'bk', 'wv', 'bv', 'wo', 'bo')}
    del _L0_xattn_all

    def _L0_ffn_setup():
        import jax, jax.numpy as jnp
        import numpy as np
        from jax import lax
        LOKAL_GRUP = 7
        TOP_K = 2
        EPS = 1e-08
        CACHE_BONUS = 0.1

        def _route(tokens, uzman_embeddings, onbellek_durumu):
            sim = tokens @ uzman_embeddings.T
            _, local_idx = lax.top_k(sim, LOKAL_GRUP)
            t_norm = tokens / (jnp.linalg.norm(tokens, axis=-1, keepdims=True) + EPS)
            e_norm = uzman_embeddings / (jnp.linalg.norm(uzman_embeddings, axis=-1, keepdims=True) + EPS)
            local_embs = e_norm[local_idx]
            scores = jnp.einsum('nld,nd->nl', local_embs, t_norm)
            scores = scores + CACHE_BONUS * onbellek_durumu[local_idx]
            top_scores, top_local = lax.top_k(scores, TOP_K)
            global_idx = jnp.take_along_axis(local_idx, top_local, axis=1)
            weights = jax.nn.softmax(top_scores, axis=-1)
            return (global_idx, lax.stop_gradient(weights))
        key = jax.random.key(seed)
        ks = jax.random.split(key, 6)
        B, S, D, E, H = (2, 256, 128, 8, 512)
        return {'x': jax.random.normal(ks[0], (B, S, D), jnp.float32), 'uzman_embeddings': jax.random.normal(ks[1], (E, D), jnp.float32) * 0.01, 'W1': jax.random.normal(ks[2], (E, D, H), jnp.float32) * 0.02, 'b1': jax.random.normal(ks[3], (E, H), jnp.float32) * 0.02, 'W2': jax.random.normal(ks[4], (E, H, D), jnp.float32) * 0.02, 'b2': jax.random.normal(ks[5], (E, D), jnp.float32) * 0.02, 'onbellek_durumu': jnp.ones((E,), jnp.float32)}
    _L0_ffn_all = _L0_ffn_setup()
    _L0_ffn_in = {k: v for k, v in _L0_ffn_all.items() if k in ('uzman_embeddings', 'W1', 'b1', 'W2', 'b2', 'onbellek_durumu')}
    del _L0_ffn_all

    def _L1_xattn_setup():
        import jax, jax.numpy as jnp
        import numpy as np
        HEADS = 16
        DIM_HEAD = 64
        SCALE = DIM_HEAD ** (-0.5)
        QUERY_DIM = 128
        CONTEXT_DIM = 96
        INNER_DIM = HEADS * DIM_HEAD
        key = jax.random.key(seed)
        ks = jax.random.split(key, 7)
        B, Nq, Nk = (8, 512, 77)
        x = jax.random.normal(ks[0], (B, Nq, QUERY_DIM), dtype=jnp.float32)
        context = jax.random.normal(ks[1], (B, Nk, CONTEXT_DIM), dtype=jnp.float32)
        Wq = jax.random.normal(ks[2], (QUERY_DIM, INNER_DIM), dtype=jnp.float32) * QUERY_DIM ** (-0.5)
        Wk = jax.random.normal(ks[3], (CONTEXT_DIM, INNER_DIM), dtype=jnp.float32) * CONTEXT_DIM ** (-0.5)
        Wv = jax.random.normal(ks[4], (CONTEXT_DIM, INNER_DIM), dtype=jnp.float32) * CONTEXT_DIM ** (-0.5)
        Wo = jax.random.normal(ks[5], (INNER_DIM, QUERY_DIM), dtype=jnp.float32) * INNER_DIM ** (-0.5)
        bo = jnp.zeros((QUERY_DIM,), dtype=jnp.float32)
        return {'x': x, 'context': context, 'Wq': Wq, 'Wk': Wk, 'Wv': Wv, 'Wo': Wo, 'bo': bo}
    _L1_xattn_all = _L1_xattn_setup()
    _L1_xattn_in = {k: v for k, v in _L1_xattn_all.items() if k in ('Wq', 'Wk', 'Wv', 'Wo', 'bo')}
    del _L1_xattn_all

    def _L1_ffn_setup():
        import jax, jax.numpy as jnp
        import numpy as np
        THRESHOLD = 0.1
        key = jax.random.key(seed)
        k1, k2, k3 = jax.random.split(key, 3)
        B, S, D, E = (4, 512, 128, 8)
        inputs = jax.random.normal(k1, (B, S, D), dtype=jnp.float32)
        gate_w = jax.random.normal(k2, (D, E), dtype=jnp.float32) * 0.02
        gate_b = jnp.zeros((E,), dtype=jnp.float32)
        expert_w = jax.random.normal(k3, (E, D, D), dtype=jnp.float32) * 0.02
        expert_b = jnp.zeros((E, D), dtype=jnp.float32)
        return {'inputs': inputs, 'gate_w': gate_w, 'gate_b': gate_b, 'expert_w': expert_w, 'expert_b': expert_b}
    _L1_ffn_all = _L1_ffn_setup()
    _L1_ffn_in = {k: v for k, v in _L1_ffn_all.items() if k in ('gate_w', 'gate_b', 'expert_w', 'expert_b')}
    del _L1_ffn_all

    def _L2_xattn_setup():
        import jax, jax.numpy as jnp
        import numpy as np
        B, LQ, LK = (4, 256, 256)
        D1, D2, H = (128, 96, 128)
        key = jax.random.key(seed)
        ks = jax.random.split(key, 9)
        s1, s2, sh = (1.0 / np.sqrt(D1), 1.0 / np.sqrt(D2), 1.0 / np.sqrt(H))
        return {'query': jax.random.normal(ks[0], (B, LQ, D1), jnp.float32), 'key': jax.random.normal(ks[1], (B, LK, D2), jnp.float32), 'value': jax.random.normal(ks[2], (B, LK, D2), jnp.float32), 'Wq': jax.random.normal(ks[3], (D1, H), jnp.float32) * s1, 'bq': jax.random.normal(ks[4], (H,), jnp.float32) * s1, 'Wk': jax.random.normal(ks[5], (D2, H), jnp.float32) * s2, 'bk': jax.random.normal(ks[6], (H,), jnp.float32) * s2, 'Wv': jax.random.normal(ks[7], (D2, H), jnp.float32) * s2, 'bv': jax.random.normal(ks[8], (H,), jnp.float32) * s2}
    _L2_xattn_all = _L2_xattn_setup()
    _L2_xattn_in = {k: v for k, v in _L2_xattn_all.items() if k in ('Wq', 'bq', 'Wk', 'bk', 'Wv', 'bv')}
    del _L2_xattn_all

    def _L2_ffn_setup():
        import jax, jax.numpy as jnp
        import numpy as np
        B, T, D, F, E = (2, 128, 128, 512, 8)
        EPS = 1e-06
        key = jax.random.key(seed)
        k = jax.random.split(key, 5)
        scale = 0.02
        return {'x': jax.random.normal(k[0], (B, T, D), dtype=jnp.float32), 'rms_w': jnp.ones((D,), dtype=jnp.float32), 'gate_w': jax.random.normal(k[1], (E, D), dtype=jnp.float32) * scale, 'W1': jax.random.normal(k[2], (E, D, F), dtype=jnp.float32) * scale, 'b1': jnp.zeros((E, F), dtype=jnp.float32), 'W2': jax.random.normal(k[3], (E, F, D), dtype=jnp.float32) * scale, 'b2': jnp.zeros((E, D), dtype=jnp.float32)}
    _L2_ffn_all = _L2_ffn_setup()
    _L2_ffn_in = {k: v for k, v in _L2_ffn_all.items() if k in ('rms_w', 'gate_w', 'W1', 'b1', 'W2', 'b2')}
    del _L2_ffn_all

    def _L3_xattn_setup():
        import math
        import jax, jax.numpy as jnp
        import numpy as np
        B, SQ, SKV = (4, 256, 256)
        D_EMBED, D_CROSS, D_ATT, N_HEADS = (128, 96, 128, 16)
        D_HEAD = D_ATT // N_HEADS

        def _split_heads(t):
            b, s, _ = t.shape
            return t.reshape(b, s, N_HEADS, D_HEAD).transpose(0, 2, 1, 3)
        key = jax.random.key(seed)
        ks = jax.random.split(key, 10)
        s_e = 1.0 / math.sqrt(D_EMBED)
        s_c = 1.0 / math.sqrt(D_CROSS)
        s_a = 1.0 / math.sqrt(D_ATT)
        return {'x': jax.random.normal(ks[0], (B, SQ, D_EMBED), jnp.float32), 'y': jax.random.normal(ks[1], (B, SKV, D_CROSS), jnp.float32), 'Wq': jax.random.normal(ks[2], (D_EMBED, D_ATT), jnp.float32) * s_e, 'bq': jax.random.normal(ks[3], (D_ATT,), jnp.float32) * 0.01, 'Wk': jax.random.normal(ks[4], (D_CROSS, D_ATT), jnp.float32) * s_c, 'bk': jax.random.normal(ks[5], (D_ATT,), jnp.float32) * 0.01, 'Wv': jax.random.normal(ks[6], (D_CROSS, D_ATT), jnp.float32) * s_c, 'bv': jax.random.normal(ks[7], (D_ATT,), jnp.float32) * 0.01, 'Wo': jax.random.normal(ks[8], (D_ATT, D_EMBED), jnp.float32) * s_a, 'bo': jax.random.normal(ks[9], (D_EMBED,), jnp.float32) * 0.01}
    _L3_xattn_all = _L3_xattn_setup()
    _L3_xattn_in = {k: v for k, v in _L3_xattn_all.items() if k in ('Wq', 'bq', 'Wk', 'bk', 'Wv', 'bv', 'Wo', 'bo')}
    del _L3_xattn_all

    def _L3_ffn_setup():
        import jax, jax.numpy as jnp
        import numpy as np
        EPS = 1e-06
        LN_EPS = 1e-05

        def _absmean_core(W):
            gamma = jnp.mean(jnp.abs(W)) + EPS
            Ws = W / gamma
            Wq = jnp.sign(Ws) * jnp.minimum(jnp.round(jnp.abs(Ws)), 1.0)
            return (Wq, gamma)

        @jax.custom_vjp
        def absmean(W):
            return _absmean_core(W)[0]

        def _absmean_fwd(W):
            Wq, gamma = _absmean_core(W)
            return (Wq, gamma)

        def _absmean_bwd(gamma, g):
            return (g / gamma,)
        absmean.defvjp(_absmean_fwd, _absmean_bwd)

        def layernorm(x, w, b, eps=LN_EPS):
            mu = jnp.mean(x, axis=-1, keepdims=True)
            var = jnp.mean((x - mu) ** 2, axis=-1, keepdims=True)
            return (x - mu) * jax.lax.rsqrt(var + eps) * w + b
        key = jax.random.key(seed)
        k1, k2, k3 = jax.random.split(key, 3)
        d, h = (128, 512)
        B, T = (8, 256)
        return {'x': jax.random.normal(k1, (B, T, d), jnp.float32), 'W_fc': jax.random.normal(k2, (h, d), jnp.float32), 'ln_w': jnp.ones((h,), jnp.float32), 'ln_b': jnp.zeros((h,), jnp.float32), 'W_proj': jax.random.normal(k3, (d, h), jnp.float32)}
    _L3_ffn_all = _L3_ffn_setup()
    _L3_ffn_in = {k: v for k, v in _L3_ffn_all.items() if k in ('W_fc', 'ln_w', 'ln_b', 'W_proj')}
    del _L3_ffn_all
    return {'x': x, 'ctx_768': ctx_768, 'g_xattn': g_xattn, 'g_ffn': g_ffn, 'L0_xattn_wq': _L0_xattn_in['wq'], 'L0_xattn_bq': _L0_xattn_in['bq'], 'L0_xattn_wk': _L0_xattn_in['wk'], 'L0_xattn_bk': _L0_xattn_in['bk'], 'L0_xattn_wv': _L0_xattn_in['wv'], 'L0_xattn_bv': _L0_xattn_in['bv'], 'L0_xattn_wo': _L0_xattn_in['wo'], 'L0_xattn_bo': _L0_xattn_in['bo'], 'L0_ffn_uzman_embeddings': _L0_ffn_in['uzman_embeddings'], 'L0_ffn_W1': _L0_ffn_in['W1'], 'L0_ffn_b1': _L0_ffn_in['b1'], 'L0_ffn_W2': _L0_ffn_in['W2'], 'L0_ffn_b2': _L0_ffn_in['b2'], 'L0_ffn_onbellek_durumu': _L0_ffn_in['onbellek_durumu'], 'L1_xattn_Wq': _L1_xattn_in['Wq'], 'L1_xattn_Wk': _L1_xattn_in['Wk'], 'L1_xattn_Wv': _L1_xattn_in['Wv'], 'L1_xattn_Wo': _L1_xattn_in['Wo'], 'L1_xattn_bo': _L1_xattn_in['bo'], 'L1_ffn_gate_w': _L1_ffn_in['gate_w'], 'L1_ffn_gate_b': _L1_ffn_in['gate_b'], 'L1_ffn_expert_w': _L1_ffn_in['expert_w'], 'L1_ffn_expert_b': _L1_ffn_in['expert_b'], 'L2_xattn_Wq': _L2_xattn_in['Wq'], 'L2_xattn_bq': _L2_xattn_in['bq'], 'L2_xattn_Wk': _L2_xattn_in['Wk'], 'L2_xattn_bk': _L2_xattn_in['bk'], 'L2_xattn_Wv': _L2_xattn_in['Wv'], 'L2_xattn_bv': _L2_xattn_in['bv'], 'L2_ffn_rms_w': _L2_ffn_in['rms_w'], 'L2_ffn_gate_w': _L2_ffn_in['gate_w'], 'L2_ffn_W1': _L2_ffn_in['W1'], 'L2_ffn_b1': _L2_ffn_in['b1'], 'L2_ffn_W2': _L2_ffn_in['W2'], 'L2_ffn_b2': _L2_ffn_in['b2'], 'L3_xattn_Wq': _L3_xattn_in['Wq'], 'L3_xattn_bq': _L3_xattn_in['bq'], 'L3_xattn_Wk': _L3_xattn_in['Wk'], 'L3_xattn_bk': _L3_xattn_in['bk'], 'L3_xattn_Wv': _L3_xattn_in['Wv'], 'L3_xattn_bv': _L3_xattn_in['bv'], 'L3_xattn_Wo': _L3_xattn_in['Wo'], 'L3_xattn_bo': _L3_xattn_in['bo'], 'L3_ffn_W_fc': _L3_ffn_in['W_fc'], 'L3_ffn_ln_w': _L3_ffn_in['ln_w'], 'L3_ffn_ln_b': _L3_ffn_in['ln_b'], 'L3_ffn_W_proj': _L3_ffn_in['W_proj']}

def reference(x, ctx_768, g_xattn, g_ffn, L0_xattn_wq, L0_xattn_bq, L0_xattn_wk, L0_xattn_bk, L0_xattn_wv, L0_xattn_bv, L0_xattn_wo, L0_xattn_bo, L0_ffn_uzman_embeddings, L0_ffn_W1, L0_ffn_b1, L0_ffn_W2, L0_ffn_b2, L0_ffn_onbellek_durumu, L1_xattn_Wq, L1_xattn_Wk, L1_xattn_Wv, L1_xattn_Wo, L1_xattn_bo, L1_ffn_gate_w, L1_ffn_gate_b, L1_ffn_expert_w, L1_ffn_expert_b, L2_xattn_Wq, L2_xattn_bq, L2_xattn_Wk, L2_xattn_bk, L2_xattn_Wv, L2_xattn_bv, L2_ffn_rms_w, L2_ffn_gate_w, L2_ffn_W1, L2_ffn_b1, L2_ffn_W2, L2_ffn_b2, L3_xattn_Wq, L3_xattn_bq, L3_xattn_Wk, L3_xattn_bk, L3_xattn_Wv, L3_xattn_bv, L3_xattn_Wo, L3_xattn_bo, L3_ffn_W_fc, L3_ffn_ln_w, L3_ffn_ln_b, L3_ffn_W_proj):
    import jax
    import jax.numpy as jnp

    def _L0_xattn_ref(x, y, wq, bq, wk, bk, wv, bv, wo, bo):
        import jax, jax.numpy as jnp
        import numpy as np
        N_HEADS = 16
        DIM_EMBED = 128
        DIM_CROSS = 96
        DIM_HEAD = DIM_EMBED // N_HEADS
        B, Sq, E = x.shape
        H, D = (N_HEADS, DIM_HEAD)
        q = (x @ wq + bq).reshape(B, Sq, H, D).transpose(0, 2, 1, 3)
        k = (y @ wk + bk).reshape(B, -1, H, D).transpose(0, 2, 1, 3)
        v = (y @ wv + bv).reshape(B, -1, H, D).transpose(0, 2, 1, 3)
        scores = jnp.einsum('bhqd,bhkd->bhqk', q, k) / jnp.sqrt(jnp.asarray(D, x.dtype))
        attn = jax.nn.softmax(scores, axis=-1)
        out = jnp.einsum('bhqk,bhkd->bhqd', attn, v)
        out = out.transpose(0, 2, 1, 3).reshape(B, Sq, E)
        return out @ wo + bo

    def _L0_ffn_ref(x, uzman_embeddings, W1, b1, W2, b2, onbellek_durumu):
        import jax, jax.numpy as jnp
        import numpy as np
        from jax import lax
        LOKAL_GRUP = 7
        TOP_K = 2
        EPS = 1e-08
        CACHE_BONUS = 0.1

        def _route(tokens, uzman_embeddings, onbellek_durumu):
            sim = tokens @ uzman_embeddings.T
            _, local_idx = lax.top_k(sim, LOKAL_GRUP)
            t_norm = tokens / (jnp.linalg.norm(tokens, axis=-1, keepdims=True) + EPS)
            e_norm = uzman_embeddings / (jnp.linalg.norm(uzman_embeddings, axis=-1, keepdims=True) + EPS)
            local_embs = e_norm[local_idx]
            scores = jnp.einsum('nld,nd->nl', local_embs, t_norm)
            scores = scores + CACHE_BONUS * onbellek_durumu[local_idx]
            top_scores, top_local = lax.top_k(scores, TOP_K)
            global_idx = jnp.take_along_axis(local_idx, top_local, axis=1)
            weights = jax.nn.softmax(top_scores, axis=-1)
            return (global_idx, lax.stop_gradient(weights))
        B, S, D = x.shape
        tokens = x.reshape(-1, D)
        global_idx, weights = _route(tokens, uzman_embeddings, onbellek_durumu)
        h = jnp.einsum('nd,edh->enh', tokens, W1) + b1[:, None, :]
        h = jax.nn.gelu(h, approximate=False)
        out_all = jnp.einsum('enh,ehd->end', h, W2) + b2[:, None, :]
        N = tokens.shape[0]
        out_sel = out_all[global_idx, jnp.arange(N)[:, None]]
        out = jnp.sum(weights[..., None] * out_sel, axis=1)
        return out.reshape(B, S, D)

    def _L1_xattn_ref(x, context, Wq, Wk, Wv, Wo, bo):
        import jax, jax.numpy as jnp
        import numpy as np
        HEADS = 16
        DIM_HEAD = 64
        SCALE = DIM_HEAD ** (-0.5)
        QUERY_DIM = 128
        CONTEXT_DIM = 96
        INNER_DIM = HEADS * DIM_HEAD
        B, Nq, _ = x.shape
        Nk = context.shape[1]
        q = x @ Wq
        k = context @ Wk
        v = context @ Wv
        q = q.reshape(B, Nq, HEADS, DIM_HEAD).transpose(0, 2, 1, 3)
        k = k.reshape(B, Nk, HEADS, DIM_HEAD).transpose(0, 2, 1, 3)
        v = v.reshape(B, Nk, HEADS, DIM_HEAD).transpose(0, 2, 1, 3)
        sim = jnp.einsum('bhid,bhjd->bhij', q, k) * SCALE
        attn = jax.nn.softmax(sim, axis=-1)
        out = jnp.einsum('bhij,bhjd->bhid', attn, v)
        out = out.transpose(0, 2, 1, 3).reshape(B, Nq, INNER_DIM)
        return out @ Wo + bo

    def _L1_ffn_ref(inputs, gate_w, gate_b, expert_w, expert_b):
        import jax, jax.numpy as jnp
        import numpy as np
        THRESHOLD = 0.1
        d = inputs.shape[-1]
        x = inputs.reshape(-1, d)
        gate_logits = jax.nn.softmax(x @ gate_w + gate_b, axis=-1)
        selected = (gate_logits >= THRESHOLD).astype(x.dtype)
        weights = gate_logits * selected
        wsum = jnp.sum(weights, axis=-1, keepdims=True)
        weights = weights / jnp.where(wsum == 0, jnp.ones_like(wsum), wsum)
        E = expert_w.shape[0]
        out = jnp.zeros((x.shape[0], expert_w.shape[-1]), dtype=x.dtype)
        for e in range(E):
            out = out + weights[:, e:e + 1] * (x @ expert_w[e] + expert_b[e])
        return out.reshape(*inputs.shape[:-1], out.shape[-1])

    def _L2_xattn_ref(query, key, value, Wq, bq, Wk, bk, Wv, bv):
        import jax, jax.numpy as jnp
        import numpy as np
        B, LQ, LK = (4, 256, 256)
        D1, D2, H = (128, 96, 128)
        q = jnp.einsum('bqd,dh->bqh', query, Wq) + bq
        k = jnp.einsum('bkd,dh->bkh', key, Wk) + bk
        v = jnp.einsum('bkd,dh->bkh', value, Wv) + bv
        scores = jnp.einsum('bqh,bkh->bqk', q, k)
        weights = jax.nn.softmax(scores, axis=-1)
        return jnp.einsum('bqk,bkh->bqh', weights, v)

    def _L2_ffn_ref(x, rms_w, gate_w, W1, b1, W2, b2):
        import jax, jax.numpy as jnp
        import numpy as np
        B, T, D, F, E = (2, 128, 128, 512, 8)
        EPS = 1e-06
        ms = jnp.mean(x * x, axis=-1, keepdims=True)
        xn = x * jax.lax.rsqrt(ms + EPS) * rms_w
        logits = jnp.einsum('btd,ed->bte', xn, gate_w)
        scores = jax.nn.softmax(logits, axis=-1)
        top1_idx = jnp.argmax(scores, axis=-1)
        top1_score = jnp.max(scores, axis=-1)
        out = jnp.zeros_like(xn)
        for e in range(E):
            h = jax.nn.silu(jnp.einsum('btd,df->btf', xn, W1[e]) + b1[e])
            ye = jnp.einsum('btf,fd->btd', h, W2[e]) + b2[e]
            out = jnp.where((top1_idx == e)[..., None], ye, out)
        return out * top1_score[..., None]

    def _L3_xattn_ref(x, y, Wq, bq, Wk, bk, Wv, bv, Wo, bo):
        import math
        import jax, jax.numpy as jnp
        import numpy as np
        B, SQ, SKV = (4, 256, 256)
        D_EMBED, D_CROSS, D_ATT, N_HEADS = (128, 96, 128, 16)
        D_HEAD = D_ATT // N_HEADS

        def _split_heads(t):
            b, s, _ = t.shape
            return t.reshape(b, s, N_HEADS, D_HEAD).transpose(0, 2, 1, 3)
        q = _split_heads(x @ Wq + bq)
        k = _split_heads(y @ Wk + bk)
        v = _split_heads(y @ Wv + bv)
        scale = 1.0 / math.sqrt(D_HEAD)
        scores = jnp.einsum('bhqd,bhkd->bhqk', q, k) * scale
        weights = jax.nn.softmax(scores, axis=-1)
        out = jnp.einsum('bhqk,bhkd->bhqd', weights, v)
        out = out.transpose(0, 2, 1, 3).reshape(x.shape[0], x.shape[1], D_ATT)
        return out @ Wo + bo

    def _L3_ffn_ref(x, W_fc, ln_w, ln_b, W_proj):
        import jax, jax.numpy as jnp
        import numpy as np
        EPS = 1e-06
        LN_EPS = 1e-05

        def _absmean_core(W):
            gamma = jnp.mean(jnp.abs(W)) + EPS
            Ws = W / gamma
            Wq = jnp.sign(Ws) * jnp.minimum(jnp.round(jnp.abs(Ws)), 1.0)
            return (Wq, gamma)

        @jax.custom_vjp
        def absmean(W):
            return _absmean_core(W)[0]

        def _absmean_fwd(W):
            Wq, gamma = _absmean_core(W)
            return (Wq, gamma)

        def _absmean_bwd(gamma, g):
            return (g / gamma,)
        absmean.defvjp(_absmean_fwd, _absmean_bwd)

        def layernorm(x, w, b, eps=LN_EPS):
            mu = jnp.mean(x, axis=-1, keepdims=True)
            var = jnp.mean((x - mu) ** 2, axis=-1, keepdims=True)
            return (x - mu) * jax.lax.rsqrt(var + eps) * w + b
        h = jnp.einsum('btd,hd->bth', x, absmean(W_fc))
        h = jax.nn.gelu(h, approximate=False)
        h = layernorm(h, ln_w, ln_b)
        return jnp.einsum('bth,dh->btd', h, absmean(W_proj))
    x = x + jnp.tanh(g_xattn[0]) * _L0_xattn_ref(_layernorm(x, axis=-1), ctx_768, L0_xattn_wq, L0_xattn_bq, L0_xattn_wk, L0_xattn_bk, L0_xattn_wv, L0_xattn_bv, L0_xattn_wo, L0_xattn_bo)
    x = x + jnp.tanh(g_ffn[0]) * _L0_ffn_ref(_layernorm(x, axis=-1), L0_ffn_uzman_embeddings, L0_ffn_W1, L0_ffn_b1, L0_ffn_W2, L0_ffn_b2, L0_ffn_onbellek_durumu)
    x = x + jnp.tanh(g_xattn[1]) * _L1_xattn_ref(_layernorm(x, axis=-1), ctx_768, L1_xattn_Wq, L1_xattn_Wk, L1_xattn_Wv, L1_xattn_Wo, L1_xattn_bo)
    x = x + jnp.tanh(g_ffn[1]) * _L1_ffn_ref(_layernorm(x, axis=-1), L1_ffn_gate_w, L1_ffn_gate_b, L1_ffn_expert_w, L1_ffn_expert_b)
    x = x + jnp.tanh(g_xattn[2]) * _L2_xattn_ref(_layernorm(x, axis=-1), ctx_768, ctx_768, L2_xattn_Wq, L2_xattn_bq, L2_xattn_Wk, L2_xattn_bk, L2_xattn_Wv, L2_xattn_bv)
    x = x + jnp.tanh(g_ffn[2]) * _L2_ffn_ref(_layernorm(x, axis=-1), L2_ffn_rms_w, L2_ffn_gate_w, L2_ffn_W1, L2_ffn_b1, L2_ffn_W2, L2_ffn_b2)
    x = x + jnp.tanh(g_xattn[3]) * _L3_xattn_ref(_layernorm(x, axis=-1), ctx_768, L3_xattn_Wq, L3_xattn_bq, L3_xattn_Wk, L3_xattn_bk, L3_xattn_Wv, L3_xattn_bv, L3_xattn_Wo, L3_xattn_bo)
    x = x + jnp.tanh(g_ffn[3]) * _L3_ffn_ref(_layernorm(x, axis=-1), L3_ffn_W_fc, L3_ffn_ln_w, L3_ffn_ln_b, L3_ffn_W_proj)
    return x

_drawn_inputs = setup_inputs


def setup_inputs(seed=0):
    import zlib

    import numpy as np

    out = dict(_drawn_inputs(seed))
    spreads = {'L0_ffn_onbellek_durumu': (1.0, 0.545),
     'L1_xattn_bo': (0.0, 0.1),
     'L1_ffn_gate_b': (0.0, 0.1),
     'L1_ffn_expert_b': (0.0, 0.1),
     'L2_ffn_rms_w': (1.0, 0.6),
     'L2_ffn_b1': (0.0, 0.8),
     'L2_ffn_b2': (0.0, 0.672),
     'L3_ffn_ln_w': (1.0, 0.2),
     'L3_ffn_ln_b': (0.0, 0.1)}
    factors = {'L0_xattn_bq': 8.0,
     'L0_xattn_bk': 64.0,
     'L0_xattn_bv': 4.207,
     'L0_xattn_bo': 3.504,
     'L0_ffn_b1': 8.0,
     'L0_ffn_b2': 3.08,
     'L2_xattn_bk': 64.0,
     'L2_ffn_gate_w': 4.442,
     'L2_ffn_W1': 8.0,
     'L2_ffn_W2': 8.0,
     'L3_xattn_bq': 64.0,
     'L3_xattn_bk': 64.0,
     'L3_xattn_bv': 8.0,
     'L3_xattn_bo': 7.411}
    for name, (base, spread) in spreads.items():
        noise = np.random.default_rng([zlib.crc32(name.encode()), seed]).standard_normal(out[name].shape)
        drawn = base * np.exp(spread * noise) if base else spread * noise
        out[name] = jnp.asarray(drawn.astype(out[name].dtype))
    for name, factor in factors.items():
        out[name] = (out[name] * factor).astype(out[name].dtype)
    return out
```

```python
from contextlib import ExitStack

import concourse.bass as bass
import numpy as np
from concourse import mybir

F32 = mybir.dt.float32
F32R = mybir.dt.float32r
ALU = mybir.AluOpType
ACT = mybir.ActivationFunctionType
AX = mybir.AxisListType

P = 128
B = 16
D = 128
SK = 77
SP = 78
DC = 96
GB = 4
NG = B // GB
GT = GB * P
H = 16
D8 = 8
HG = 4
D64 = 64
INNER = H * D64
C1 = INNER // P
E = 8
HID = 512
NC_HID = HID // P
WCH = 2048
ROUNDS = ((0, 6), (6, 11), (11, 16))

C_ID = 0
C_CQ, C_MQ, C_CK, C_MK = 128, 129, 130, 131
C_MASK = 132
C_NA = 136
C_NB = C_NA + 33
C_UP = C_NB + 33
C_DOWN = C_UP + E
C_HALF = C_DOWN + E
C_TM = C_HALF + GB
C_KIND = C_TM + GB
C_ONE = C_KIND + H * HG
C_PLUS = C_ONE + P
C_SELB = C_PLUS + GB
NCONST = C_SELB + GB * SK


def constants():
    c = np.zeros((P, NCONST), np.float32)
    c[:, C_ID:C_ID + P] = np.eye(P)
    role = (np.arange(P) % 32) // D8
    c[:, C_CQ] = np.where(role == 1, -1, 1)
    c[:, C_MQ] = role == 1
    c[:, C_CK] = np.where(role == 2, -1, 1)
    c[:, C_MK] = role == 2
    for j in range(HG):
        c[32 * j:32 * j + 32, C_MASK + j] = 1
    c[:, C_NA:C_NA + 33] = 1.0
    c[:, C_NB:C_NB + 33] = 1e-5
    c[:, C_NA + 20:C_NA + 24] = 1.0 + 1e-6
    c[:, C_NB + 20:C_NB + 24] = 1e-11
    c[:, C_UP:C_UP + E] = np.arange(1, E + 1)
    c[:, C_DOWN:C_DOWN + E] = np.arange(E, 0, -1)
    c[:, C_HALF:C_HALF + GB] = -0.5
    for t in range(GB):
        c[E * t:E * t + E, C_TM + t] = 1
        c[t, C_SELB + t * SK:C_SELB + t * SK + SK] = 1
    for h in range(H):
        c[DC, C_KIND + h * HG + h // HG] = 1
    c[:, C_ONE:C_ONE + P] = 1
    c[:, C_PLUS:C_PLUS + GB] = 0.5
    return c


def selectors():
    s = np.zeros((P, H, SK), np.float32)
    for h in range(H):
        s[h, h] = 1
        s[64 + h, h] = 1
    return s


def build(nc, a, out):
    ctx = ExitStack()
    with ctx:
        def sem(name):
            return ctx.enter_context(nc.semaphore(name))

        def sems(prefix, *names):
            return type(prefix, (), {n: sem(f"{prefix}_{n}") for n in names})

        ps = ctx.enter_context(nc.psum_tensor("banks", [P, 8, 512], F32))

        top = [(nc.sbuf_base + 63) // 64 * 64]

        def place(name, shape, dt=F32, at=None):
            size = int(np.prod(shape[1:])) * 4
            offset = top[0] if at is None else at[0]
            t = nc.alloc_sbuf_tensor_at(name, shape, dt, offset=offset)
            size = (size + 63) // 64 * 64
            if at is None:
                top[0] += size
            else:
                at[0] += size
                at[1] = max(at[1], at[0])
            return t

        const = place("const", [P, NCONST])
        x = place("x", [P, B, D])
        xn = place("xn", [P, GB, D])
        xhi = place("xhi", [P, GT], F32R)
        xlo = place("xlo", [P, GT], F32R)
        ctxT = place("ctxT", [P, B, SP])
        chi = place("chi", [P, GB, SP], F32R)
        clo = place("clo", [P, GB, SP], F32R)
        tg = place("tg", [P, 2, 4])
        st = place("st", [P, GB, 6])
        mv = place("mv", [P, GB, 2])
        vv = place("vv", [P, GB])
        rstd = place("rstd", [P, GB])
        fs = place("fs", [P, 5, GB])
        mh = place("mh", [P, 2, GB])
        scal = place("scal", [P, 8])
        ones2 = place("ones2", [64, GT], F32R)
        idn = const[:, C_ID:C_ID + P]

        a_raw = place("a_raw", [P, 4, P])
        a_bq = place("a_bq", [64, P])
        a_bo = place("a_bo", [1, P])
        wq = [place("wq_hi", [P, H, 4, D8], F32R), place("wq_lo", [P, H, 4, D8], F32R)]
        wk = [place("wk_hi", [P, H, 4, D8], F32R), place("wk_lo", [P, H, 4, D8], F32R)]
        wv = [place("wv_hi", [P, P], F32R), place("wv_lo", [P, P], F32R)]
        wo = place("wo", [P, P])
        bo = place("bo", [1, P])
        bq2 = place("bq2", [64, H, 4, D8], F32R)
        b_raw = place("b_raw", [P, 3, P])
        w2 = [place("w2_hi", [P, 3, P], F32R), place("w2_lo", [P, 3, P], F32R)]
        b_bq = place("b_bq", [64, P])
        b_bq2 = place("b_bq2", [64, P], F32R)
        rraw = place("rraw", [P, 16])
        rwt = [place("rw_hi", [P, 16], F32R), place("rw_lo", [P, 16], F32R)]
        emb = place("emb", [E, 3, D])
        emb_s = place("emb_s", [E, 4])
        rowb = place("rowb", [P, E])
        b2rep = place("b2rep", [GB * E, D])
        b2m = place("b2m", [GB * E, GB, D])
        b1 = place("b1", [P, E * NC_HID])
        rmsw = place("rmsw", [P, 1])
        cw = place("cw", [P, GB, E])
        cT = place("cT", [GB * E, P])
        rt = place("rt", [P, 12, GB, E])
        rs = place("rs", [P, 12, GB])
        raw = [place("raw0", [P, WCH // 2]), place("raw1", [P, WCH // 2])]
        l1w = [place("l1w_hi", [P, 4, INNER], F32R), place("l1w_lo", [P, 4, INNER], F32R)]

        wregion = [top[0], top[0]]
        wb = [place("wb_hi", [P, 8, WCH // 2], F32R, wregion), place("wb_lo", [P, 8, WCH // 2], F32R, wregion)]
        wend = wregion[1]
        wregion = [top[0], wend]
        wo1 = place("wo1", [P, C1, D], F32, wregion)
        sel1 = place("sel1", [P, H, SK], F32, wregion)
        q1 = place("q1", [P, C1, GT], F32, wregion)
        k1 = place("k1", [P, C1, GB, SP], F32, wregion)
        v1 = place("v1", [SK, GB, H, D64 + 1], F32, wregion)
        nm1 = place("nm1", [P, P], F32, wregion)
        nT = place("nT", [P, P], F32, wregion)
        assert wregion[0] <= wend
        wregion = [top[0], wend]
        wf = place("wf", [P, 4, P], F32R, wregion)
        wp = place("wp", [P, 4, P], F32, wregion)
        wfr = place("wfr", [P, 4, P], F32, wregion)
        wpr = place("wpr", [P, 4, P], F32, wregion)
        lnw = place("lnw", [P, 4], F32, wregion)
        lnb = place("lnb", [P, 4], F32, wregion)
        ta = place("ta", [P, 16], F32, wregion)
        top[0] = wend

        rden = place("rden", [P, H])
        s0 = top[0]
        s = [s0, s0]
        prob = [place("prob0", [SK, 4, 512], F32, s), place("prob1", [SK, 4, 512], F32, s)]
        sa = s[0]
        ctok = place("ctok", [SK, B, DC], F32, s)
        s = [sa, s[1]]
        q = place("q", [P, HG, GB, P], F32R, s)
        k = place("k", [P, HG, GB, SP], F32R, s)
        kbd = [place("kbd0", [P, HG, HG, SP], F32R, s), place("kbd1", [P, HG, HG, SP], F32R, s)]
        v = place("v", [SK, GB, H, D8 + 1], F32, s)
        nm = place("nm", [P, 4, 32], F32, s)
        on8 = place("on8", [P, P], F32, s)
        oT8 = place("oT8", [P, P], F32, s)
        s = [sa, s[1]]
        on = place("on", [P, INNER], F32, s)
        oT = place("oT", [P, C1, P], F32, s)
        s = [sa, s[1]]
        q2 = [place("q2_hi", [P, GT], F32R, s), place("q2_lo", [P, GT], F32R, s)]
        k2 = [place("k2_hi", [P, GB, SP], F32R, s), place("k2_lo", [P, GB, SP], F32R, s)]
        v2 = place("v2", [SK, GB, D + 1], F32, s)
        nm2 = place("nm2", [P, GB], F32, s)
        nT2 = place("nT2", [GB, P], F32, s)
        s = [s0, s[1]]
        hf = place("hf", [P, 4, 512], F32, s)
        hhi = [place("hhi0", [P, 4, 512], F32R, s), place("hhi1", [P, 4, 512], F32R, s)]
        hlo = [place("hlo0", [P, 4, 512], F32R, s), place("hlo1", [P, 4, 512], F32R, s)]
        s = [s0, s[1]]
        hg = place("hg", [P, GB, HID], F32, s)
        hgT = place("hgT", [P, 2, 4, P], F32, s)
        assert s[1] <= nc.sbuf_usable_end, (s[1], nc.sbuf_usable_end)

        ld = sems("loaded", "const", "x", "xrest", "ctx", "gate", "a", "r", "raw0", "raw1", "l1raw", "l1", "b", "l3")
        su = sems("setup", "braw", "zero", "dve", "tanh", "pe", "scratch", "plink", "vlink")
        fr = sems("front", "link", "var", "rstd", "xn", "xt", "hi", "lo")
        h8 = sems("heads8", "w", "ctx", "mm", "hi", "lo", "v_mm", "v", "kbd", "s", "max", "t", "shift",
                  "st", "exp", "o", "on", "oT_mm", "oT", "y", "x", "link")
        ff = sems("experts", "w_mm", "w_ss", "w_rt", "w", "r", "nn", "rn", "d", "tanh", "c", "ct_mm", "ct", "b_mm", "xb",
                  "h", "act", "split", "o", "x", "link", "link1")
        h64 = sems("heads64", "ctx", "qmm", "kmm", "vmm", "q", "k", "v", "s", "max", "t", "nT", "st", "exp",
                   "o", "on", "oT_mm", "oT", "y", "x", "link", "nm")
        h1 = sems("head128", "w", "ctx", "qmm", "qhi", "q", "kmm", "khi", "k", "vmm", "v", "s", "max", "t", "nT",
                  "st", "exp", "o", "x", "big", "link")
        mx = sems("mixed", "w", "r", "d", "e", "c", "ct_mm", "ct", "b_mm", "xb", "o", "half", "x", "link")
        tn = sems("ternary", "sum", "gamma", "w", "wT_mm", "wT", "h", "act", "var", "rstd", "norm", "t_mm", "t",
                  "y", "x", "link")
        wr = sems("split", "big", "l1")
        stored = sem("stored")

        block = ctx.enter_context(nc.Block())

        def row(ap):
            return ap.rearrange("(o n) -> o n", o=1)

        def f32(ap):
            return ap.bitcast(F32)

        def done(kind):
            return {"h8": (h8.x, B), "ff": (ff.x, NG * E), "h64": (h64.x, B), "mx": (mx.half, 8 * NG),
                    "h1": (h1.x, NG), "tn": (tn.x, NG)}[kind]

        def wait_done(eng, kind, runs):
            s_, n_ = done(kind)
            eng.wait_ge(s_, n_ * runs)

        def next_group(g):
            return 0 if isinstance(g, int) else (g + 1) % NG

        class Link:

            def __init__(self, eng, s_, per, step=0):
                self.eng, self.sem, self.per, self.step, self.n = eng, s_, per, step, 0

            def mark(self, ins):
                self.n += 1
                ins.then_inc(self.sem, 1)

            def wait(self, back=0):
                assert self.n > back
                self.eng.wait_ge(self.sem, self.step * self.per + self.n - back)

            def link(self, ins):
                self.mark(ins)
                self.wait()

            def end(self):
                assert self.n == self.per, (self.n, self.per)

        N_A = 9

        @block.sync
        def _(sp):
            def load_heads8(layer):
                n = f"L{layer}_xattn_"
                c = "w" if layer == 0 else "W"
                sp.dma_start(a_raw[:, 0, :], a[n + c + "q"]).then_inc(ld.a, 16)
                sp.dma_start(a_raw[0:DC, 1, :], a[n + c + "k"]).then_inc(ld.a, 16)
                sp.dma_start(a_raw[DC:DC + 1, 1, :], row(a[n + "bk"])).then_inc(ld.a, 16)
                sp.dma_start(a_raw[0:DC, 2, :], a[n + c + "v"]).then_inc(ld.a, 16)
                sp.dma_start(a_raw[DC:DC + 1, 2, :], row(a[n + "bv"])).then_inc(ld.a, 16)
                sp.dma_start(a_raw[:, 3, :], a[n + c + "o"]).then_inc(ld.a, 16)
                sp.dma_start(a_bq[0:1, :], row(a[n + "bq"])).then_inc(ld.a, 16)
                sp.dma_start(a_bq[32:33, :], row(a[n + "bq"])).then_inc(ld.a, 16)
                sp.dma_start(a_bo[:, :], row(a[n + "bo"])).then_inc(ld.a, 16)

            def load_experts(layer, i):
                w1 = a[f"L{layer}_ffn_W1"].rearrange("e d h -> d e h")
                w2 = a[f"L{layer}_ffn_W2"].rearrange("e (c p) d -> p (e c) d", p=P)
                src = w1[:, 2 * i:2 * i + 2, :] if i < 4 else w2[:, 8 * i - 32:8 * i - 24, :]
                n = 2 if i < 4 else 8
                sp.dma_start(raw[i % 2][:, :].rearrange("p (e h) -> p e h", e=n), src)\
                  .then_inc((ld.raw0, ld.raw1)[i % 2], 16)

            def load_b2(name):
                for t in range(GB):
                    sp.dma_start(b2rep[E * t:E * t + E, :], a[name]).then_inc(ld.r, 16)

            sp.dma_start(const[:, :], a["const"]).then_inc(ld.const, 16)
            xd = a["x"].rearrange("b t d -> t b d")
            sp.dma_start(x[:, 0:GB, :], xd[:, 0:GB, :]).then_inc(ld.x, 16)
            sp.dma_start(ctok[:, :, :], a["ctx_768"].rearrange("b s d -> s b d")).then_inc(ld.ctx, 16)
            sp.wait_ge(su.braw, 1)
            load_heads8(0)
            sp.dma_start(x[:, GB:B, :], xd[:, GB:B, :]).then_inc(ld.xrest, 16)
            sp.dma_start(tg[:, 0, :], row(a["g_xattn"]).to_broadcast([P, 4])).then_inc(ld.gate, 16)
            sp.dma_start(tg[:, 1, :], row(a["g_ffn"]).to_broadcast([P, 4])).then_inc(ld.gate, 16)
            sp.dma_start(emb[:, 0, :], a["L0_ffn_uzman_embeddings"]).then_inc(ld.r, 16)
            sp.dma_start(rowb[:, :], row(a["L0_ffn_onbellek_durumu"]).to_broadcast([P, E])).then_inc(ld.r, 16)
            sp.dma_start(b1[:, :], a["L0_b1"]).then_inc(ld.r, 16)
            load_b2("L0_ffn_b2")
            for i in range(8):
                if i >= 2:
                    sp.wait_ge(wr.big, i - 1)
                load_experts(0, i)
            sp.wait_ge(wr.big, 7)
            sp.dma_start(raw[0][:, :], a["L1_xattn_Wq"]).then_inc(ld.l1raw, 16)
            for i, n in enumerate(("L1_xattn_Wk", "L1_xattn_Wv")):
                sp.wait_ge(wr.l1, i + 1)
                sp.dma_start(raw[0][0:DC, :], a[n]).then_inc(ld.l1raw, 16)
            sp.wait_ge(wr.l1, 3)
            sp.dma_start(raw[0][:, :].rearrange("p (e h) -> p e h", e=E),
                         a["L1_ffn_expert_w"].rearrange("e d h -> d e h")).then_inc(ld.l1raw, 16)
            wait_done(sp, "ff", 1)
            sp.dma_start(wo1[:, :, :], a["L1_xattn_Wo"].rearrange("(c p) d -> p c d", p=P)).then_inc(ld.l1, 16)
            sp.dma_start(sel1[:, :, :], a["sel"]).then_inc(ld.l1, 16)
            sp.dma_start(bo[:, :], row(a["L1_xattn_bo"])).then_inc(ld.l1, 16)
            sp.dma_start(rraw[:, 0:E], a["L1_ffn_gate_w"]).then_inc(ld.r, 16)
            sp.dma_start(rowb[:, :], row(a["L1_ffn_gate_b"]).to_broadcast([P, E])).then_inc(ld.r, 16)
            load_b2("L1_ffn_expert_b")
            sp.dma_start(b_raw[:, 0, :], a["L2_xattn_Wq"]).then_inc(ld.b, 16)
            for j, n in ((1, "k"), (2, "v")):
                sp.dma_start(b_raw[0:DC, j, :], a["L2_xattn_W" + n]).then_inc(ld.b, 16)
                sp.dma_start(b_raw[DC:DC + 1, j, :], row(a["L2_xattn_b" + n])).then_inc(ld.b, 16)
            sp.dma_start(b_bq[0:1, :], row(a["L2_xattn_bq"])).then_inc(ld.b, 16)
            sp.dma_start(b_bq[32:33, :], row(a["L2_xattn_bq"])).then_inc(ld.b, 16)
            load_heads8(3)
            sp.dma_start(rmsw[:, :], a["L2_ffn_rms_w"].rearrange("(p o) -> p o", o=1)).then_inc(ld.b, 16)
            sp.wait_ge(wr.l1, 4)
            for i in range(8):
                if i >= 2:
                    sp.wait_ge(h1.big, i - 1)
                if i == 2:
                    wait_done(sp, "mx", 1)
                    sp.dma_start(emb[:, 0, :], a["L2_ffn_gate_w"]).then_inc(ld.r, 16)
                    sp.dma_start(b1[:, :], a["L2_b1"]).then_inc(ld.r, 16)
                    load_b2("L2_ffn_b2")
                load_experts(2, i)
            wait_done(sp, "ff", 2)
            sp.dma_start(wfr[:, :, :], a["L3_ffn_W_fc"].rearrange("(c p) d -> p c d", p=P)).then_inc(ld.l3, 16)
            sp.dma_start(wpr[:, :, :], a["L3_ffn_W_proj"].rearrange("d (c p) -> d c p", p=P)).then_inc(ld.l3, 16)
            sp.dma_start(lnw[:, :], a["ln_w"]).then_inc(ld.l3, 16)
            sp.dma_start(lnb[:, :], a["ln_b"]).then_inc(ld.l3, 16)
            od = out.rearrange("b t d -> t b d")
            for g in range(NG):
                sp.wait_ge(tn.x, g + 1)
                sp.dma_start(od[:, GB * g:GB * g + GB, :], x[:, GB * g:GB * g + GB, :]).then_inc(stored, 16)
            sp.wait_ge(stored, 16 * NG)

        @block.gpsimd
        def _(pool):
            def rsqrt_front(n):
                pool.wait_ge(fr.var, n + 1)
                pool.tensor_tensor(rstd[:, :], vv[:, :], const[:, C_HALF:C_HALF + GB], ALU.pow).then_inc(fr.rstd, 1)

            def split_chunk(src, rows, hi, lo, links, done_, count):
                pool.tensor_copy(hi, src).then_inc(su.plink, 1)
                pool.wait_ge(su.plink, links)
                pool.tensor_tensor(lo, src, f32(hi), ALU.subtract).then_inc(done_, 1)

            def keys(G, b):
                if b == 0:
                    pool.wait_ge(h8.lo, 8 * G + 8)
                if b >= 2:
                    pool.wait_ge(h8.st, 2 * (4 * G + b - 1))
                kb = f32(k[:, :, b, :]).unsqueeze(2).to_broadcast([P, HG, HG, SP])
                m = const[:, C_MASK:C_MASK + HG].unsqueeze(1).unsqueeze(3).to_broadcast([P, HG, HG, SP])
                pool.tensor_tensor(kbd[b % 2][:, :, :, :], kb, m, ALU.mult).then_inc(h8.kbd, 1)

            def heads8_scratch():
                pool.memset(v[:, :, :, D8:D8 + 1], 1.0).then_inc(su.scratch, 1)
                pool.memset(nm[:, :, :], 0.0).then_inc(su.scratch, 1)

            pool.memset(a_bq[:, :], 0.0).then_inc(su.braw, 1)
            pool.memset(b_bq[:, :], 0.0).then_inc(su.zero, 1)
            pool.memset(ctxT[0:DC, :, SK:SP], 0.0).then_inc(su.zero, 1)
            pool.wait_ge(su.zero, 2)
            pool.memset(ctxT[DC:DC + 1, :, :], 1.0).then_inc(su.zero, 1)
            pool.wait_ge(su.zero, 3)
            for t in (*wq, *wk):
                pool.memset(f32(t[:, :, :, :]), 0.0).then_inc(su.zero, 1)
            pool.memset(f32(bq2[:, :, :, :]), 0.0).then_inc(su.zero, 1)
            pool.memset(f32(ones2[:, :]), 1.0).then_inc(su.zero, 1)
            heads8_scratch()
            pool.wait_ge(ld.const, 16)
            rsqrt_front(0)
            for g in range(NG):
                rsqrt_front(g + 1)
                for b in range(GB):
                    keys(g, b)
                    if b < 2:
                        i = 2 * g + b
                        pool.wait_ge((ld.raw0, ld.raw1)[b], 16 * (g + 1))
                        split_chunk(raw[b][:, :], P, wb[0][:, i, :], wb[1][:, i, :], i + 1, wr.big, i + 1)
            pool.wait_ge(ff.w_ss, 1)
            pool.tensor_tensor(emb_s[:, 1:2], emb_s[:, 0:1], const[0:E, C_PLUS:C_PLUS + 1], ALU.pow).then_inc(ff.w_rt, 1)
            for g in range(NG):
                pool.wait_ge(ff.nn, g + 1)
                pool.tensor_tensor(rs[:, 1, :], rs[:, 0, :], const[:, C_PLUS:C_PLUS + GB], ALU.pow).then_inc(ff.rn, 1)
                rsqrt_front(NG + g + 1)
                rows = DC if g in (1, 2) else P
                pool.wait_ge(ld.l1raw, 16 * (g + 1))
                split_chunk(raw[0][0:rows, :], rows, l1w[0][0:rows, g, :], l1w[1][0:rows, g, :], 8 + g + 1, wr.l1, g + 1)
            wait_done(pool, "ff", 1)
            pool.memset(v1[:, :, :, D64:D64 + 1], 1.0).then_inc(su.scratch, 1)
            pool.memset(nm1[:, :], 0.0).then_inc(su.scratch, 1)
            with pool.Fori(0, NG) as g:
                rsqrt_front(g + 2 * NG + 1)
            with pool.Fori(0, NG) as g:
                rsqrt_front(g + 3 * NG + 1)
            wait_done(pool, "h64", 1)
            pool.memset(v2[:, :, D:D + 1], 1.0).then_inc(su.scratch, 1)
            with pool.Fori(0, NG) as g:
                rsqrt_front(g + 4 * NG + 1)
            with pool.Fori(0, NG) as g:
                rsqrt_front(g + 5 * NG + 1)
            wait_done(pool, "ff", 2)
            heads8_scratch()
            with pool.Fori(0, NG) as g:
                rsqrt_front(g + 6 * NG + 1)
                for b in range(GB):
                    keys(g + NG, b)
            with pool.Fori(0, NG) as g:
                rsqrt_front(g + 7 * NG + 1)
                pool.wait_ge(tn.var, g + 1)
                pool.tensor_tensor(ta[:, 4:8], ta[:, 0:4], const[:, C_HALF:C_HALF + GB], ALU.pow).then_inc(tn.rstd, 1)

        @block.scalar
        def _(act):
            def copy(o_, i_, **kw):
                return act.activation(o_, i_, ACT.Copy, **kw)

            def front(n):
                act.wait_ge(fr.xt, n + 1)
                copy(xhi[:, :], ps[:, 7, :]).then_inc(fr.hi, 1)

            def heads8(run, phase):
                with act.Fori(0, NG) as g:
                    G = g + NG * run
                    for u in range(8):
                        act.wait_ge(h8.mm, 8 * G + u + 1)
                        bank = ps[:, u % 6, :]
                        if u < 4:
                            copy(q[:, u, :, :].rearrange("p b t -> p (b t)"), bank,
                                 scale=const[:, C_CQ:C_CQ + 1]).then_inc(h8.hi, 1)
                        else:
                            copy(k[:, u - 4, :, :].rearrange("p b t -> p (b t)"), bank[:, 0:GB * SP],
                                 scale=const[:, C_CK:C_CK + 1]).then_inc(h8.hi, 1)
                    front(g + NG * phase + 1)
                    act.wait_ge(h8.v_mm, G + 1)
                    for b in range(GB):
                        ins = copy(v[:, b, :, 0:D8], ps[0:SK, 6, b * P:b * P + P].rearrange("p (h d) -> p h d", h=H))
                    ins.then_inc(h8.v, 1)
                    for b in range(GB + 1):
                        if b >= 1:
                            act.wait_ge(h8.oT_mm, 4 * G + b)
                            copy(oT8[:, :], ps[:, 6, 0:P]).then_inc(h8.oT, 1)
                        if b < GB:
                            for half in range(2):
                                act.wait_ge(h8.st, 2 * (4 * G + b) + half + 1)
                                act.activation(prob[b % 2][:, 2 * half:2 * half + 2, :],
                                               ps[0:SK, 2 + 2 * half:4 + 2 * half, :], ACT.Exp,
                                               scale=D8 ** -0.5).then_inc(h8.exp, 1)

            def experts(run, phase, func):
                with act.Fori(0, NG) as g:
                    G = g + NG * run
                    if run:
                        act.wait_ge(ff.d, G + 1)
                        act.activation(rt[:, 3, :, :], rt[:, 2, :, :], ACT.Tanh, scale=0.5).then_inc(ff.tanh, 1)
                    else:
                        act.wait_ge(ff.d, G + 1)
                        act.activation(rs[:, 9, :], rs[:, 8, :], ACT.Tanh, scale=0.5).then_inc(ff.tanh, 1)
                    for u in range(E * NC_HID):
                        if u >= 4:
                            act.wait_ge(ff.split, 32 * G + u - 3)
                        act.wait_ge(ff.h, 32 * G + u + 1)
                        act.activation(hf[:, u % 4, :], ps[:, u % 4, :], func, bias=b1[:, u:u + 1])\
                           .then_inc(ff.act, 1)
                    front(g + NG * phase + 1)

            def heads64():
                with act.Fori(0, NG) as g:
                    for c in range(C1):
                        act.wait_ge(h64.qmm, 8 * g + c + 1)
                        copy(q1[:, c, :], ps[:, c % 4, :]).then_inc(h64.q, 1)
                    for i in range(2 * GB):
                        act.wait_ge(h64.vmm, 8 * g + i + 1)
                        copy(v1[:, i // 2, 8 * (i % 2):8 * (i % 2) + 8, 0:D64],
                             ps[0:SK, i % 4, :].rearrange("p (h d) -> p h d", h=8)).then_inc(h64.v, 1)
                    front(g + 2 * NG + 1)
                    for b in range(GB + 1):
                        if b < GB:
                            for half in range(2):
                                act.wait_ge(h64.st, 2 * (4 * g + b) + half + 1)
                                act.activation(prob[b % 2][:, 2 * half:2 * half + 2, :],
                                               ps[0:SK, 2 + 2 * half:4 + 2 * half, :], ACT.Exp,
                                               scale=D64 ** -0.5).then_inc(h64.exp, 1)
                        if b >= 1:
                            for half in range(2):
                                act.wait_ge(h64.oT_mm, 2 * (4 * g + b - 1) + half + 1)
                                copy(oT[:, 4 * half:4 * half + 4, :].rearrange("p c t -> p (c t)"), ps[:, 6 + half, :])\
                                    .then_inc(h64.oT, 1)

            def mixed():
                with act.Fori(0, NG) as g:
                    act.wait_ge(mx.d, g + 1)
                    act.activation(rt[:, 3, :, :], rt[:, 2, :, :], ACT.Exp).then_inc(mx.e, 1)
                    front(g + 3 * NG + 1)

            def head128():
                with act.Fori(0, NG) as g:
                    act.wait_ge(h1.qmm, g + 1)
                    copy(q2[0][:, :], ps[:, 0, :]).then_inc(h1.qhi, 1)
                    act.wait_ge(h1.kmm, g + 1)
                    copy(k2[0][:, :, :].rearrange("p b t -> p (b t)"), ps[:, 1, 0:GB * SP]).then_inc(h1.khi, 1)
                    act.wait_ge(h1.vmm, g + 1)
                    copy(v2[:, :, 0:D], ps[0:SK, 2, :].rearrange("p (b d) -> p b d", b=GB)).then_inc(h1.v, 1)
                    front(g + 4 * NG + 1)
                    act.wait_ge(h1.st, g + 1)
                    act.activation(prob[0][:, 0, :], ps[0:SK, 5, :], ACT.Exp).then_inc(h1.exp, 1)

            def ternary():
                with act.Fori(0, NG) as g:
                    for t in range(GB):
                        act.wait_ge(tn.h, 4 * g + t + 1)
                        act.activation(hg[:, t, :], ps[:, t, :], ACT.Gelu).then_inc(tn.act, 1)
                    front(g + 7 * NG + 1)
                    for t in range(GB):
                        act.wait_ge(tn.t_mm, 4 * g + t + 1)
                        for c in range(NC_HID):
                            ins = act.activation(hgT[:, t % 2, c, :], ps[:, 4 + t % 2, c * P:c * P + P], ACT.Identity,
                                                 scale=lnw[:, c:c + 1], bias=lnb[:, c:c + 1])
                        ins.then_inc(tn.t, 1)

            act.wait_ge(ld.gate, 32)
            act.activation(tg[:, :, :], tg[:, :, :], ACT.Tanh).then_inc(su.tanh, 1)
            front(0)
            heads8(0, 0)
            act.wait_ge(ld.r, 16 * 7)
            experts(0, 1, ACT.Gelu)
            heads64()
            mixed()
            head128()
            act.wait_ge(ld.r, 16 * 19)
            experts(1, 5, ACT.Silu)
            heads8(1, 6)
            act.wait_ge(ld.l3, 64)
            ternary()

        @block.tensor
        def _(pe):
            def split3(o_, w_, m_, stop=True):
                pe.matmul(o_, w_[0], m_[0], start=True, stop=False)
                pe.matmul(o_, w_[1], m_[0], start=False, stop=False)
                return pe.matmul(o_, w_[0], m_[1], start=False, stop=stop)

            xT = (xhi[:, :], xlo[:, :])

            def front(n):
                pe.wait_ge(fr.xn, n + 1)
                for t in range(GB):
                    ins = pe.transpose(ps[:, 7, t * P:t * P + P], xn[:, t, :], idn)
                ins.then_inc(fr.xt, 1)

            def tokens(src, t):
                return tuple(p_[:, t * P:t * P + P] for p_ in src)

            def heads8(run, phase):
                wait_done(pe, "ff", 2) if run else None
                pe.wait_ge(h8.w, run + 1)
                with pe.Fori(0, NG) as g:
                    G = g + NG * run
                    pe.wait_ge(fr.lo, g + NG * phase + 1)
                    pe.wait_ge(h8.ctx, G + 1)
                    for u in range(8):
                        if u >= 6:
                            pe.wait_ge(h8.lo, 8 * G + u - 5)
                        cols = slice(4 * (u % 4), 4 * (u % 4) + 4)
                        if u < 4:
                            o_ = ps[:, u % 6, :]
                            wt = tuple(w_[:, cols, :, :].rearrange("p h r d -> p (h r d)") for w_ in wq)
                            split3(o_, wt, xT, stop=False)
                            pe.matmul(o_, bq2[:, cols, :, :].rearrange("p h r d -> p (h r d)"), ones2[:, :],
                                      start=False, stop=True).then_inc(h8.mm, 1)
                        else:
                            wt = tuple(w_[0:DC + 1, cols, :, :].rearrange("p h r d -> p (h r d)") for w_ in wk)
                            split3(ps[:, u % 6, 0:GB * SP], wt,
                                   tuple(c_[0:DC + 1, :, :].rearrange("p b t -> p (b t)") for c_ in (chi, clo)))\
                                .then_inc(h8.mm, 1)
                    front(g + NG * phase + 1)
                    for b in range(GB):
                        ins = split3(ps[0:SK, 6, b * P:b * P + P], tuple(c_[0:DC + 1, b, 0:SK] for c_ in (chi, clo)),
                                     tuple(w_[0:DC + 1, :] for w_ in wv))
                    ins.then_inc(h8.v_mm, 1)
                    pe.wait_ge(h8.lo, 8 * G + 8)
                    for b in range(GB + 1):
                        if b < GB:
                            pe.wait_ge(h8.kbd, 4 * G + b + 1)
                            for j in range(HG):
                                if j >= 2:
                                    pe.wait_ge(h8.max, 4 * (4 * G + b) + j - 1)
                                pe.matmul(ps[:, j % 2, 0:HG * SP], q[:, j, b, :],
                                          kbd[b % 2][:, j, :, :].rearrange("p h t -> p (h t)"),
                                          start=True, stop=True).then_inc(h8.s, 1)
                        if b >= 1:
                            if b == 1:
                                pe.wait_ge(h8.v, G + 1)
                            if b >= 2:
                                pe.wait_ge(h8.x, 4 * G + b - 1)
                            pe.wait_ge(h8.exp, 2 * (4 * G + b))
                            for h in range(H):
                                ins = pe.matmul(ps[:, 6, h * (D8 + 1):(h + 1) * (D8 + 1)],
                                                prob[(b - 1) % 2][:, h // 4, (h % 4) * P:(h % 4) * P + P],
                                                v[:, b - 1, h, :], start=True, stop=True)
                            ins.then_inc(h8.o, 1)
                        if b < GB:
                            if b == 0:
                                pe.wait_ge(fr.lo, g + NG * phase + 2)
                            pe.wait_ge(h8.max, 4 * (4 * G + b) + 4)
                            pe.transpose(ps[:, 7, 0:P], nm[:, :, :].rearrange("p j r -> p (j r)"), idn)\
                                .then_inc(h8.t, 1)
                        if b >= 1:
                            pe.wait_ge(h8.on, 4 * G + b)
                            pe.transpose(ps[:, 6, 0:P], on8[:, :], idn).then_inc(h8.oT_mm, 1)
                        if b < GB:
                            pe.wait_ge(h8.shift, 4 * G + b + 1)
                            for j in range(HG):
                                for i in range(HG):
                                    ins = pe.matmul(ps[0:SK, 2 + j, i * P:i * P + P], kbd[b % 2][:, j, i, 0:SK],
                                                    q[:, j, b, :], start=True, stop=True)
                                if j % 2:
                                    ins.then_inc(h8.st, 1)
                        if b >= 1:
                            pe.wait_ge(h8.oT, 4 * G + b)
                            pe.matmul(ps[:, 6, 0:P], oT8[:, :], wo[:, :], start=True, stop=False)
                            pe.matmul(ps[:, 6, 0:P], const[0:1, C_ONE:C_ONE + P], bo[:, :], start=False, stop=True)\
                                .then_inc(h8.y, 1)

            def mix_rows(s_c, s_ct_mm, s_ct, s_b_mm, G, between):
                pe.wait_ge(s_c, G + 1)
                pe.transpose(ps[0:GB * E, 6, 0:P], cw[:, :, :].rearrange("p t e -> p (t e)"), idn).then_inc(s_ct_mm, 1)
                between()
                pe.wait_ge(s_ct, G + 1)
                pe.matmul(ps[:, 6, :], cT[:, :], b2m[:, :, :].rearrange("p t d -> p (t d)"), start=True, stop=True)\
                    .then_inc(s_b_mm, 1)

            def experts(run, phase):
                wait_done(pe, "h1" if run else "h8", 1)
                if run:
                    pe.wait_ge(ld.r, 16 * 19)
                else:
                    pe.wait_ge(ff.w_ss, 2)
                for j in range(1 if run else 2):
                    ins = pe.transpose(ps[:, 6, 8 * j:8 * j + E], emb[:, 2 * j, :], const[0:E, C_ID:C_ID + E])
                ins.then_inc(ff.w_mm, 1)
                pe.wait_ge(ff.w, run + 1)
                if run:
                    pe.wait_ge(h1.big, 8)
                else:
                    pe.wait_ge(wr.big, 8)
                with pe.Fori(0, NG) as g:
                    G = g + NG * run
                    pe.wait_ge(fr.lo, g + NG * phase + 1)
                    n = E if run else 2 * E
                    for t in range(GB):
                        ins = split3(ps[:, 6, t * 16:t * 16 + n], tokens(xT, t), tuple(w_[:, 0:n] for w_ in rwt))
                    ins.then_inc(ff.r, 1)

                    def up(e):
                        for c in range(NC_HID):
                            u = e * NC_HID + c
                            if u >= 4:
                                pe.wait_ge(ff.act, 32 * G + u - 3)
                            split3(ps[:, u % 4, :],
                                   tuple(w_[:, e // 2, (u % 8) * P:(u % 8) * P + P] for w_ in wb), xT)\
                                .then_inc(ff.h, 1)

                    def down(e):
                        pe.wait_ge(ff.split, 32 * G + 4 * e + 4)
                        if e >= 2:
                            pe.wait_ge(ff.x, 8 * G + e - 1)
                        for t in range(GB):
                            o_ = ps[:, 4 + e % 2, t * P:t * P + P]
                            for c in range(NC_HID):
                                hh = hhi[e % 2][:, c, t * P:t * P + P]
                                hl = hlo[e % 2][:, c, t * P:t * P + P]
                                w_ = [z[:, 4 + e // 2, (4 * (e % 2) + c) * P:(4 * (e % 2) + c) * P + P] for z in wb]
                                pe.matmul(o_, hh, w_[0], start=(c == 0), stop=False)
                                pe.matmul(o_, hh, w_[1], start=False, stop=False)
                                ins = pe.matmul(o_, hl, w_[0], start=False, stop=(c == NC_HID - 1))
                        ins.then_inc(ff.o, 1)

                    up(0)
                    mix_rows(ff.c, ff.ct_mm, ff.ct, ff.b_mm, G, lambda: up(1))
                    down(0)
                    for e in range(2, E):
                        up(e)
                        if e < E - 1:
                            down(e - 1)
                    front(g + NG * phase + 1)
                    down(E - 2)
                    down(E - 1)

            def heads64():
                wait_done(pe, "ff", 1)
                pe.wait_ge(ld.l1, 48)
                pe.wait_ge(wr.l1, 4)
                pe.wait_ge(su.scratch, 4)
                with pe.Fori(0, NG) as g:
                    pe.wait_ge(fr.lo, g + 2 * NG + 1)
                    pe.wait_ge(h64.ctx, g + 1)
                    ct = tuple(c_[0:DC, :, :].rearrange("p b t -> p (b t)") for c_ in (chi, clo))
                    for c in range(C1):
                        if c >= 4:
                            pe.wait_ge(h64.q, 8 * g + c - 3)
                        split3(ps[:, c % 4, :], tuple(w_[:, 0, c * P:c * P + P] for w_ in l1w), xT).then_inc(h64.qmm, 1)
                        if c >= 2:
                            pe.wait_ge(h64.k, 8 * g + c - 1)
                        split3(ps[:, 4 + c % 2, 0:GB * SP], tuple(w_[0:DC, 1, c * P:c * P + P] for w_ in l1w), ct)\
                            .then_inc(h64.kmm, 1)
                    front(g + 2 * NG + 1)
                    for i in range(2 * GB):
                        if i < 4:
                            pe.wait_ge(h64.q, 8 * g + 5 + i)
                        else:
                            pe.wait_ge(h64.v, 8 * g + i - 3)
                        split3(ps[0:SK, i % 4, :], tuple(c_[0:DC, i // 2, 0:SK] for c_ in (chi, clo)),
                               tuple(w_[0:DC, 2, 512 * (i % 2):512 * (i % 2) + 512] for w_ in l1w)).then_inc(h64.vmm, 1)
                    pe.wait_ge(h64.k, 8 * g + 8)
                    pe.wait_ge(h64.v, 8 * g + 8)
                    pe.wait_ge(fr.lo, g + 2 * NG + 2)
                    for b in range(GB + 1):
                        if b < GB:
                            if b:
                                pe.wait_ge(h64.nT, 4 * g + b)
                            for u in range(4):
                                half, par = u // 2, u % 2
                                if u >= 2:
                                    pe.wait_ge(h64.max, 4 * (4 * g + b) + u - 1)
                                for i in range(4):
                                    c = 4 * half + i
                                    ins = pe.matmul(ps[:, par, i * SP:i * SP + SK],
                                                    q1[64 * par:64 * par + 64, c, b * P:b * P + P],
                                                    k1[64 * par:64 * par + 64, c, b, 0:SK], start=True, stop=True)
                                ins.then_inc(h64.s, 1)
                        if b >= 1:
                            if b >= 2:
                                pe.wait_ge(h64.x, 4 * g + b - 1)
                            pe.wait_ge(h64.exp, 2 * (4 * g + b))
                            for r_, (h0, h1_) in enumerate(ROUNDS):
                                if r_ == 2:
                                    pe.wait_ge(h64.on, 3 * (4 * g + b - 1) + 1)
                                for h in range(h0, h1_):
                                    slot, i = 2 * (h // 8) + h % 2, (h % 8) // 2
                                    ins = pe.matmul(ps[:, 6 + r_ % 2, (h - h0) * (D64 + 1):(h - h0 + 1) * (D64 + 1)],
                                                    prob[(b - 1) % 2][:, slot, i * P:i * P + P],
                                                    v1[:, b - 1, h, :], start=True, stop=True)
                                ins.then_inc(h64.o, 1)
                        if b < GB:
                            pe.wait_ge(h64.max, 4 * (4 * g + b) + 5 - 1)
                            pe.wait_ge(h64.nm, 4 * g + b + 1)
                            pe.transpose(ps[:, 0, 0:P], nm1[:, :], idn).then_inc(h64.t, 1)
                            pe.wait_ge(h64.nT, 4 * g + b + 1)
                            for half in range(2):
                                for i in range(4):
                                    for par in range(2):
                                        c, r0 = 4 * half + i, 64 * par
                                        h = 2 * c + par
                                        o_ = ps[0:SK, 2 + 2 * half + par, i * P:i * P + P]
                                        pe.matmul(o_, k1[r0:r0 + 64, c, b, 0:SK],
                                                  q1[r0:r0 + 64, c, b * P:b * P + P], start=True, stop=False)
                                        ins = pe.matmul(o_, sel1[r0:r0 + H, h, :], nT[r0:r0 + H, :],
                                                        start=False, stop=True)
                                ins.then_inc(h64.st, 1)
                        if b >= 1:
                            for half in range(2):
                                pe.wait_ge(h64.on, 3 * (4 * g + b - 1) + 3)
                                for c in range(4):
                                    ins = pe.transpose(ps[:, 6 + half, c * P:c * P + P],
                                                       on[:, (4 * half + c) * P:(4 * half + c + 1) * P], idn)
                                ins.then_inc(h64.oT_mm, 1)
                            pe.wait_ge(h64.oT, 2 * (4 * g + b))
                            for c in range(C1):
                                pe.matmul(ps[:, 6, 0:P], oT[:, c, :], wo1[:, c, :], start=(c == 0), stop=False)
                            pe.matmul(ps[:, 6, 0:P], const[0:1, C_ONE:C_ONE + P], bo[:, :], start=False, stop=True)\
                                .then_inc(h64.y, 1)

            def mixed():
                wait_done(pe, "h64", 1)
                pe.wait_ge(mx.w, 1)
                with pe.Fori(0, NG) as g:
                    pe.wait_ge(fr.lo, g + 3 * NG + 1)
                    for t in range(GB):
                        ins = split3(ps[:, 6, t * 16:t * 16 + E], tokens(xT, t), tuple(w_[:, 0:E] for w_ in rwt))
                    ins.then_inc(mx.r, 1)

                    def half_(i):
                        for t in range(GB):
                            if i:
                                pe.wait_ge(mx.half, 8 * g + t + 1)
                            split3(ps[:, t, :], tokens(xT, t),
                                   tuple(w_[:, 3, 512 * i:512 * i + 512] for w_ in l1w)).then_inc(mx.o, 1)

                    mix_rows(mx.c, mx.ct_mm, mx.ct, mx.b_mm, g, lambda: half_(0))
                    half_(1)
                    front(g + 3 * NG + 1)

            def head128():
                wait_done(pe, "mx", 1)
                pe.wait_ge(h1.w, 1)
                pe.wait_ge(su.scratch, 5)
                with pe.Fori(0, NG) as g:
                    pe.wait_ge(fr.lo, g + 4 * NG + 1)
                    pe.wait_ge(h1.ctx, g + 1)
                    split3(ps[:, 0, :], tuple(w_[:, 0, :] for w_ in w2), xT, stop=False)
                    pe.matmul(ps[:, 0, :], b_bq2[:, :], ones2[:, :], start=False, stop=True).then_inc(h1.qmm, 1)
                    split3(ps[:, 1, 0:GB * SP], tuple(w_[0:DC + 1, 1, :] for w_ in w2),
                           tuple(c_[0:DC + 1, :, :].rearrange("p b t -> p (b t)") for c_ in (chi, clo)))\
                        .then_inc(h1.kmm, 1)
                    for b in range(GB):
                        ins = split3(ps[0:SK, 2, b * P:b * P + P], tuple(c_[0:DC + 1, b, 0:SK] for c_ in (chi, clo)),
                                     tuple(w_[0:DC + 1, 2, :] for w_ in w2))
                    ins.then_inc(h1.vmm, 1)
                    front(g + 4 * NG + 1)
                    pe.wait_ge(h1.q, g + 1)
                    pe.wait_ge(h1.k, g + 1)
                    for b in range(GB):
                        ins = split3(ps[:, 3, b * SP:b * SP + SP], tokens([q_[:, :] for q_ in q2], b),
                                     tuple(k_[:, b, :] for k_ in k2))
                    ins.then_inc(h1.s, 1)
                    pe.wait_ge(h1.max, g + 1)
                    pe.transpose(ps[0:GB, 4, 0:P], nm2[:, :], idn).then_inc(h1.t, 1)
                    pe.wait_ge(h1.nT, g + 1)
                    for b in range(GB):
                        o_ = ps[0:SK, 5, b * P:b * P + P]
                        split3(o_, tuple(k_[:, b, 0:SK] for k_ in k2), tokens([q_[:, :] for q_ in q2], b), stop=False)
                        ins = pe.matmul(o_, const[0:GB, C_SELB + b * SK:C_SELB + b * SK + SK], nT2[:, :],
                                        start=False, stop=True)
                    ins.then_inc(h1.st, 1)
                    pe.wait_ge(h1.exp, g + 1)
                    pe.wait_ge(h1.v, g + 1)
                    for b in range(GB):
                        ins = pe.matmul(ps[:, (6, 0)[b // 2], (b % 2) * (D + 1):(b % 2 + 1) * (D + 1)],
                                        prob[0][:, 0, b * P:b * P + P], v2[:, b, :], start=True, stop=True)
                        if b % 2:
                            ins.then_inc(h1.o, 1)

            def ternary():
                wait_done(pe, "h8", 2)
                pe.wait_ge(tn.sum, 1)
                pe.matmul(ps[:, 2, 0:2], const[:, C_ONE:C_ONE + P], ta[:, 8:10], start=True, stop=True)\
                    .then_inc(tn.gamma, 1)
                pe.wait_ge(tn.w, 1)
                for j, w_ in enumerate((wfr, wpr)):
                    for c in range(4):
                        ins = pe.transpose(ps[:, j, c * P:c * P + P], w_[:, c, :], idn)
                    ins.then_inc(tn.wT_mm, 1)
                pe.wait_ge(tn.wT, 2)
                with pe.Fori(0, NG) as g:
                    pe.wait_ge(fr.lo, g + 7 * NG + 1)
                    for t in range(GB):
                        w_ = wf[:, :, :].rearrange("p c h -> p (c h)")
                        pe.matmul(ps[:, t, :], xhi[:, t * P:t * P + P], w_, start=True, stop=False)
                        pe.matmul(ps[:, t, :], xlo[:, t * P:t * P + P], w_, start=False, stop=True).then_inc(tn.h, 1)
                    front(g + 7 * NG + 1)
                    for t in range(GB + 1):
                        if t < GB:
                            pe.wait_ge(tn.norm, 4 * g + t + 1)
                            if t >= 2:
                                pe.wait_ge(tn.t, 4 * g + t - 1)
                            for c in range(NC_HID):
                                ins = pe.transpose(ps[:, 4 + t % 2, c * P:c * P + P], hg[:, t, c * P:c * P + P], idn)
                            ins.then_inc(tn.t_mm, 1)
                        if t >= 1:
                            pe.wait_ge(tn.t, 4 * g + t)
                            for c in range(NC_HID):
                                ins = pe.matmul(ps[:, 6, (t - 1) * P:t * P], hgT[:, (t - 1) % 2, c, :], wp[:, c, :],
                                                start=(c == 0), stop=(c == NC_HID - 1))
                    ins.then_inc(tn.y, 1)

            pe.wait_ge(ld.const, 16)
            pe.wait_ge(ld.ctx, 16)
            for b in range(B):
                ins = pe.transpose(ps[0:DC, b // 4, (b % 4) * SP:(b % 4) * SP + SK], ctok[:, b, :],
                                   const[0:SK, C_ID:C_ID + SK])
            ins.then_inc(su.pe, 1)
            front(0)
            pe.wait_ge(su.dve, 4)
            pe.wait_ge(su.zero, 9)
            pe.wait_ge(su.scratch, 2)
            heads8(0, 0)
            experts(0, 1)
            heads64()
            mixed()
            head128()
            experts(1, 5)
            heads8(1, 6)
            ternary()

        @block.vector
        def _(dve):
            def over(ap, n=E):
                return ap.unsqueeze(2).to_broadcast([P, GB, n])

            def along(col, n=E):
                return const[:, col:col + n].unsqueeze(1).to_broadcast([P, GB, n])

            def group(t_, g, w=1):
                return t_[:, bass.ds(g, w), :]

            def variance(lk, s_, n, mean, var):
                lk.wait()
                lk.mark(dve.tensor_tensor(fs[:, 0, :], s_[:, :, 1], s_[:, :, 4], ALU.add))
                lk.mark(dve.tensor_tensor(fs[:, 1, :], s_[:, :, 1], s_[:, :, 4], ALU.subtract))
                lk.mark(dve.tensor_tensor(fs[:, 2, :], s_[:, :, 2], s_[:, :, 5], ALU.add))
                lk.wait()
                lk.mark(dve.tensor_scalar(mean, fs[:, 0, :], 0.5, None, ALU.mult))
                lk.mark(dve.tensor_tensor(fs[:, 3, :], fs[:, 1, :], fs[:, 1, :], ALU.mult))
                lk.mark(dve.tensor_scalar(fs[:, 4, :], fs[:, 2, :], 1.0 / n, None, ALU.mult))
                lk.wait()
                lk.link(dve.scalar_tensor_tensor(out=var, in0=fs[:, 3, :], scalar=0.25, in1=fs[:, 4, :],
                                                 op0=ALU.mult, op1=ALU.add))

            def front_a(gn, n):
                lk = Link(dve, fr.link, 11, n)
                for t in range(GB):
                    lk.mark(dve.bn_stats(st[:, t, :], x[:, bass.ds(gn * GB + t, 1), :].rearrange("p o d -> p (o d)")))
                variance(lk, st, D, mv[:, :, 0], mv[:, :, 1])
                dve.tensor_scalar(vv[:, :], mv[:, :, 1], const[:, bass.ds(n + C_NA, 1)], const[:, bass.ds(n + C_NB, 1)],
                                  ALU.mult, ALU.add).then_inc(fr.var, 1)
                lk.end()

            def front_b(gn, n):
                dve.wait_ge(fr.rstd, n + 1)
                for t in range(GB):
                    ins = dve.tensor_scalar(xn[:, t, :], x[:, bass.ds(gn * GB + t, 1), :].rearrange("p o d -> p (o d)"),
                                            mv[:, t, 0:1], rstd[:, t:t + 1], ALU.subtract, ALU.mult)
                ins.then_inc(fr.xn, 1)

            def front_c(n):
                dve.wait_ge(fr.hi, n + 1)
                dve.tensor_tensor(xlo[:, :], ps[:, 7, :], f32(xhi[:, :]), ALU.subtract).then_inc(fr.lo, 1)

            def stage(lk, g, rows, s_):
                c_ = ctxT[0:rows, bass.ds(g * GB, GB), :]
                lk.mark(dve.tensor_copy(chi[0:rows, :, :], c_))
                lk.wait()
                dve.tensor_tensor(clo[0:rows, :, :], c_, f32(chi[0:rows, :, :]), ALU.subtract).then_inc(s_, 1)

            sl = Link(dve, su.vlink, 0)

            def add_to_x(tile_, w, in_, scalar, s_):
                xt = x[:, bass.ds(tile_, w), :].rearrange("p o d -> p (o d)")
                dve.scalar_tensor_tensor(out=xt, in0=in_, scalar=scalar, in1=xt, op0=ALU.mult, op1=ALU.add).then_inc(s_, 1)

            def heads8_weights(run):
                def rep(ap, rows):
                    return ap[0:rows, :].rearrange("p (h d) -> p h d", h=H).unsqueeze(2).to_broadcast([rows, H, 3, D8])
                dve.wait_ge(ld.a, 16 * N_A * (run + 1))
                dve.wait_ge(su.zero, 9)
                K1 = DC + 1
                sl.mark(dve.tensor_copy(wq[0][:, :, 0:3, :], rep(a_raw[:, 0, :], P)))
                sl.mark(dve.tensor_copy(wk[0][0:K1, :, 0:3, :], rep(a_raw[:, 1, :], K1)))
                sl.mark(dve.tensor_copy(wv[0][0:K1, :], a_raw[0:K1, 2, :]))
                sl.mark(dve.tensor_copy(bq2[:, :, 0:3, :], rep(a_bq[:, :], 64)))
                sl.mark(dve.tensor_copy(wk[0][DC:K1, :, 3, 0:HG],
                                        const[DC:K1, C_KIND:C_KIND + H * HG].rearrange("p (h k) -> p h k", h=H)))
                sl.mark(dve.tensor_copy(wo[:, :], a_raw[:, 3, :]))
                sl.mark(dve.tensor_copy(bo[:, :], a_bo[:, :]))
                sl.wait()
                dve.tensor_tensor(wq[1][:, :, 0:3, :], rep(a_raw[:, 0, :], P), f32(wq[0][:, :, 0:3, :]), ALU.subtract)
                dve.tensor_tensor(wk[1][0:K1, :, 0:3, :], rep(a_raw[:, 1, :], K1), f32(wk[0][0:K1, :, 0:3, :]),
                                  ALU.subtract)
                dve.tensor_tensor(wv[1][0:K1, :], a_raw[0:K1, 2, :], f32(wv[0][0:K1, :]), ALU.subtract)
                dve.tensor_tensor(bq2[32:64, :, 0:3, :], rep(a_bq[:, :], 64)[32:64], f32(bq2[32:64, :, 0:3, :]),
                                  ALU.subtract).then_inc(h8.w, 1)

            def heads8(run, phase):
                layer = 3 * run
                heads8_weights(run)
                with dve.Fori(0, NG) as g:
                    G = g + NG * run
                    n = g + NG * phase + 1
                    gn = next_group(g)
                    lk = Link(dve, h8.link, 5, G)
                    stage(lk, g, DC + 1, h8.ctx)
                    front_a(gn, n)
                    for u in range(8):
                        dve.wait_ge(h8.hi, 8 * G + u + 1)
                        t_, m, w = (q, C_MQ, GT) if u < 4 else (k, C_MK, GB * SP)
                        t_ = t_[:, u % 4, :, :].rearrange("p b t -> p (b t)")
                        dve.scalar_tensor_tensor(out=t_, in0=ps[:, u % 6, 0:w], scalar=const[:, m:m + 1], in1=f32(t_),
                                                 op0=ALU.mult, op1=ALU.add).then_inc(h8.lo, 1)
                        if u == 3:
                            front_b(gn, n)
                    front_c(n)
                    for b in range(GB + 1):
                        if b < GB:
                            for j in range(HG):
                                dve.wait_ge(h8.s, 4 * (4 * G + b) + j + 1)
                                s_ = ps[:, j % 2, 0:HG * SP].rearrange("p (h t) -> p h t", h=HG)[:, :, 0:SK]
                                dve.tensor_reduce(nm[:, :, 24 + j:25 + j], s_, AX.X, ALU.max, negate=True)\
                                   .then_inc(h8.max, 1)
                        if b >= 1:
                            dve.wait_ge(h8.o, 4 * G + b)
                            o_ = ps[:, 6, 0:H * (D8 + 1)].rearrange("p (h d) -> p h d", h=H)
                            lk.link(dve.reciprocal(rden[:, :].unsqueeze(2), o_[:, :, D8:D8 + 1]))
                            dve.tensor_tensor(on8[:, :].rearrange("p (h d) -> p h d", h=H), o_[:, :, 0:D8],
                                              rden[:, :].unsqueeze(2).to_broadcast([P, H, D8]), ALU.mult)\
                               .then_inc(h8.on, 1)
                        if b < GB:
                            dve.wait_ge(h8.t, 4 * G + b + 1)
                            dve.tensor_tensor(q[:, :, b, :], f32(q[:, :, b, :]),
                                              ps[:, 7, 0:P].unsqueeze(1).to_broadcast([P, HG, P]), ALU.add)\
                               .then_inc(h8.shift, 1)
                        if b >= 1:
                            dve.wait_ge(h8.y, 4 * G + b)
                            add_to_x(g * GB + b - 1, 1, ps[:, 6, 0:P], tg[:, 0, layer:layer + 1], h8.x)
                    lk.end()

            def second_biases(s_):
                dve.tensor_tensor(b2m[:, :, :], b2rep[:, :].unsqueeze(1).to_broadcast([GB * E, GB, D]),
                                  const[0:GB * E, C_TM:C_TM + GB].unsqueeze(2).to_broadcast([GB * E, GB, D]),
                                  ALU.mult).then_inc(s_, 1)

            def split_small(hi, lo, src):
                sl.link(dve.tensor_copy(hi, src))
                return dve.tensor_tensor(lo, src, f32(hi), ALU.subtract)

            def first_best(lk, s_, best, hit, tie, one):
                lk.link(dve.tensor_reduce(best, s_, AX.X, ALU.max))
                lk.link(dve.tensor_tensor(hit, s_, over(best), ALU.is_equal))
                lk.link(dve.tensor_tensor(hit, hit, along(C_DOWN), ALU.mult))
                lk.link(dve.tensor_reduce(tie, hit, AX.X, ALU.max))
                lk.link(dve.tensor_tensor(one, hit, over(tie), ALU.is_equal))

            def route_top2(lk, G, gate):
                R = [rt[:, i, :, :] for i in range(12)]
                S = [rs[:, i, :] for i in range(12)]
                dve.wait_ge(ff.rn, G + 1)
                lk.link(dve.tensor_scalar(S[4], S[1], 1e-8, None, ALU.add))
                lk.link(dve.reciprocal(S[5], S[4]))
                dve.wait_ge(ff.r, G + 1)
                o_ = ps[:, 6, 0:GB * 16].rearrange("p (t e) -> p t e", e=16)
                lk.mark(dve.tensor_tensor(R[0], o_[:, :, E:2 * E], over(S[5]), ALU.mult))
                lk.mark(dve.tensor_copy(R[2], o_[:, :, 0:E]))
                lk.wait()
                lk.mark(dve.tensor_tensor(R[1], R[0], rowb[:, :].unsqueeze(1).to_broadcast([P, GB, E]), ALU.add))
                lk.link(dve.tensor_reduce(S[6], R[2], AX.X, ALU.min))
                lk.link(dve.tensor_tensor(R[3], R[2], over(S[6]), ALU.is_equal))
                lk.link(dve.tensor_tensor(R[4], R[3], along(C_UP), ALU.mult))
                lk.link(dve.tensor_reduce(S[7], R[4], AX.X, ALU.max))
                lk.link(dve.tensor_tensor(R[5], R[4], over(S[7]), ALU.is_equal))
                lk.link(dve.scalar_tensor_tensor(out=R[6], in0=R[5], scalar=-1e30, in1=R[1], op0=ALU.mult, op1=ALU.add))
                first_best(lk, R[6], S[10], R[7], S[11], R[9])
                lk.link(dve.scalar_tensor_tensor(out=R[10], in0=R[9], scalar=-3e30, in1=R[6], op0=ALU.mult, op1=ALU.add))
                first_best(lk, R[10], S[6], R[3], S[7], R[11])
                dve.tensor_tensor(S[8], S[6], S[10], ALU.subtract).then_inc(ff.d, 1)
                dve.wait_ge(ff.tanh, G + 1)
                lk.mark(dve.tensor_scalar(S[2], S[9], 0.5, 0.5, ALU.mult, ALU.add))
                lk.link(dve.tensor_scalar(S[3], S[9], -0.5, 0.5, ALU.mult, ALU.add))
                lk.mark(dve.tensor_tensor(R[7], R[9], over(S[3]), ALU.mult))
                lk.link(dve.tensor_tensor(R[8], R[11], over(S[2]), ALU.mult))
                lk.link(dve.tensor_tensor(R[0], R[7], R[8], ALU.add))
                dve.tensor_scalar(cw[:, :, :], R[0], gate, None, ALU.mult).then_inc(ff.c, 1)

            def route_top1(lk, G, gate):
                R = [rt[:, i, :, :] for i in range(12)]
                S = [rs[:, i, :] for i in range(12)]
                dve.wait_ge(ff.r, G + 1)
                o_ = ps[:, 6, 0:GB * 16].rearrange("p (t e) -> p t e", e=16)
                lk.link(dve.tensor_copy(R[0], o_[:, :, 0:E]))
                first_best(lk, R[0], S[0], R[1], S[1], R[5])
                dve.tensor_tensor(R[2], R[0], over(S[0]), ALU.subtract).then_inc(ff.d, 1)
                dve.wait_ge(ff.tanh, G + 1)
                lk.mark(dve.tensor_scalar(R[6], R[3], 1.0, None, ALU.add))
                lk.link(dve.tensor_scalar(R[7], R[3], -1.0, 1.0, ALU.mult, ALU.add))
                lk.link(dve.reciprocal(R[8], R[7]))
                lk.link(dve.tensor_tensor(R[9], R[6], R[8], ALU.mult))
                lk.link(dve.tensor_reduce(S[2], R[9], AX.X, ALU.add))
                lk.link(dve.reciprocal(S[3], S[2]))
                lk.link(dve.tensor_tensor(R[10], R[5], over(S[3]), ALU.mult))
                dve.tensor_scalar(cw[:, :, :], R[10], gate, None, ALU.mult).then_inc(ff.c, 1)

            def experts(run, phase):
                layer = 2 * run
                LK2, LK1 = 60, 45
                gate = tg[:, 1, layer:layer + 1]
                dve.wait_ge(ld.r, 16 * (19 if run else 7))
                n_ = E if run else 2 * E
                if not run:
                    sl.link(dve.tensor_tensor(emb[:, 1, :], emb[:, 0, :], emb[:, 0, :], ALU.mult))
                    dve.tensor_reduce(emb_s[:, 0:1], emb[:, 1, :], AX.X, ALU.add).then_inc(ff.w_ss, 1)
                    dve.wait_ge(ff.w_rt, 1)
                    sl.link(dve.tensor_scalar(emb_s[:, 2:3], emb_s[:, 1:2], 1e-8, None, ALU.add))
                    sl.link(dve.reciprocal(emb_s[:, 3:4], emb_s[:, 2:3]))
                    dve.tensor_scalar(emb[:, 2, :], emb[:, 0, :], emb_s[:, 3:4], None, ALU.mult).then_inc(ff.w_ss, 1)
                    sl.link(dve.tensor_scalar(rowb[:, :], rowb[:, :], 0.1, None, ALU.mult))
                dve.wait_ge(ff.w_mm, run + 1)
                if run:
                    sl.link(dve.tensor_scalar(rraw[:, 0:n_], ps[:, 6, 0:n_], rmsw[:, 0:1], None, ALU.mult))
                else:
                    sl.link(dve.tensor_copy(rraw[:, 0:n_], ps[:, 6, 0:n_]))
                split_small(rwt[0][:, 0:n_], rwt[1][:, 0:n_], rraw[:, 0:n_])
                second_biases(ff.w)
                with dve.Fori(0, NG) as g:
                    G = g + NG * run
                    n = g + NG * phase + 1
                    gn = next_group(g)
                    lk = Link(dve, (ff.link, ff.link1)[run], (LK2, LK1)[run], g)
                    if not run:
                        lk.link(dve.tensor_tensor(rs[:, 2, :], mv[:, :, 1], rstd[:, :], ALU.mult))
                        dve.scalar_tensor_tensor(out=rs[:, 0, :], in0=rs[:, 2, :], scalar=float(D), in1=rstd[:, :],
                                                 op0=ALU.mult, op1=ALU.mult).then_inc(ff.nn, 1)
                    front_a(gn, n)
                    (route_top1 if run else route_top2)(lk, G, gate)

                    def split(e):
                        if e >= 2:
                            dve.wait_ge(ff.o, 8 * G + e - 1)
                        for c in range(NC_HID + 1):
                            u = NC_HID * e + c
                            if c < NC_HID:
                                dve.wait_ge(ff.act, 32 * G + u + 1)
                                lk.mark(dve.tensor_copy(hhi[e % 2][:, c, :], hf[:, u % 4, :]))
                            if c:
                                lk.wait(back=1 if c < NC_HID else 0)
                                dve.tensor_tensor(hlo[e % 2][:, c - 1, :], hf[:, (u - 1) % 4, :],
                                                  f32(hhi[e % 2][:, c - 1, :]), ALU.subtract).then_inc(ff.split, 1)

                    def add(e):
                        dve.wait_ge(ff.o, 8 * G + e + 1)
                        if e:
                            dve.wait_ge(ff.x, 8 * G + e)
                        else:
                            dve.wait_ge(ff.xb, G + 1)
                        for t in range(GB):
                            xt = x[:, bass.ds(g * GB + t, 1), :].rearrange("p o d -> p (o d)")
                            ins = dve.scalar_tensor_tensor(out=xt, in0=ps[:, 4 + e % 2, t * P:t * P + P],
                                                           scalar=cw[:, t, e:e + 1], in1=xt, op0=ALU.mult, op1=ALU.add)
                        ins.then_inc(ff.x, 1)

                    split(0)
                    dve.wait_ge(ff.ct_mm, G + 1)
                    dve.tensor_copy(cT[:, :], ps[0:GB * E, 6, 0:P]).then_inc(ff.ct, 1)
                    split(1)
                    add_rows(g, ff.b_mm, G, ff.xb)
                    front_b(gn, n)
                    add(0)
                    for e in range(2, E):
                        split(e)
                        if e == E - 1:
                            front_c(n)
                        add(e - 1)
                    add(E - 1)
                    lk.end()

            def add_rows(g, s_mm, G, s_):
                dve.wait_ge(s_mm, G + 1)
                xt = x[:, bass.ds(g * GB, GB), :].rearrange("p t d -> p (t d)")
                dve.tensor_tensor(xt, xt, ps[:, 6, :], ALU.add).then_inc(s_, 1)

            def heads64():
                with dve.Fori(0, NG) as g:
                    n = g + 2 * NG + 1
                    gn = next_group(g)
                    lk = Link(dve, h64.link, 13, g)
                    stage(lk, g, DC, h64.ctx)
                    front_a(gn, n)
                    for c in range(C1):
                        dve.wait_ge(h64.kmm, 8 * g + c + 1)
                        dve.tensor_copy(k1[:, c, :, :].rearrange("p b t -> p (b t)"), ps[:, 4 + c % 2, 0:GB * SP])\
                           .then_inc(h64.k, 1)
                        if c == 1:
                            front_b(gn, n)
                    front_c(n)
                    for b in range(GB + 1):
                        if b < GB:
                            for u in range(4):
                                half, par = u // 2, u % 2
                                dve.wait_ge(h64.s, 4 * (4 * g + b) + u + 1)
                                s_ = ps[:, par, 0:4 * SP].rearrange("p (h t) -> p h t", h=4)[:, :, 0:SK]
                                o_ = nm1[:, 0:H].rearrange("p (f i r) -> p f i r", f=2, i=4)[:, half, :, par:par + 1]
                                dve.tensor_reduce(o_, s_, AX.X, ALU.max, negate=True).then_inc(h64.max, 1)
                            dve.wait_ge(h64.max, 4 * (4 * g + b) + 4)
                            dve.tensor_copy(nm1[:, 64:64 + H], nm1[:, 0:H]).then_inc(h64.nm, 1)
                        if b >= 1:
                            for r_, (h0, h1_) in enumerate(ROUNDS):
                                dve.wait_ge(h64.o, 3 * (4 * g + b - 1) + r_ + 1)
                                nh = h1_ - h0
                                o_ = ps[:, 6 + r_ % 2, 0:nh * (D64 + 1)].rearrange("p (h d) -> p h d", h=nh)
                                lk.link(dve.reciprocal(rden[:, h0:h1_].unsqueeze(2), o_[:, :, D64:D64 + 1]))
                                dve.tensor_tensor(on[:, h0 * D64:h1_ * D64].rearrange("p (h d) -> p h d", h=nh),
                                                  o_[:, :, 0:D64],
                                                  rden[:, h0:h1_].unsqueeze(2).to_broadcast([P, nh, D64]), ALU.mult)\
                                   .then_inc(h64.on, 1)
                        if b < GB:
                            dve.wait_ge(h64.t, 4 * g + b + 1)
                            dve.tensor_copy(nT[:, :], ps[:, 0, 0:P]).then_inc(h64.nT, 1)
                        if b >= 1:
                            dve.wait_ge(h64.y, 4 * g + b)
                            add_to_x(g * GB + b - 1, 1, ps[:, 6, 0:P], tg[:, 0, 1:2], h64.x)
                    lk.end()

            def mixed():
                dve.wait_ge(ld.r, 16 * 13)
                split_small(rwt[0][:, 0:E], rwt[1][:, 0:E], rraw[:, 0:E])
                second_biases(mx.w)
                R = [rt[:, i, :, :] for i in range(12)]
                S = [rs[:, i, :] for i in range(12)]
                with dve.Fori(0, NG) as g:
                    n = g + 3 * NG + 1
                    gn = next_group(g)
                    lk = Link(dve, mx.link, 36, g)
                    front_a(gn, n)
                    dve.wait_ge(mx.r, g + 1)
                    o_ = ps[:, 6, 0:GB * 16].rearrange("p (t e) -> p t e", e=16)[:, :, 0:E]
                    lk.link(dve.tensor_tensor(R[0], o_, rowb[:, :].unsqueeze(1).to_broadcast([P, GB, E]), ALU.add))
                    lk.link(dve.tensor_reduce(S[0], R[0], AX.X, ALU.max))
                    dve.tensor_tensor(R[2], R[0], over(S[0]), ALU.subtract).then_inc(mx.d, 1)
                    front_b(gn, n)
                    dve.wait_ge(mx.e, g + 1)
                    lk.link(dve.tensor_reduce(S[1], R[3], AX.X, ALU.add))
                    lk.link(dve.reciprocal(S[2], S[1]))
                    lk.link(dve.tensor_tensor(R[4], R[3], over(S[2]), ALU.mult))
                    lk.link(dve.tensor_scalar(R[5], R[4], 0.1, None, ALU.is_ge))
                    lk.link(dve.tensor_tensor(R[6], R[4], R[5], ALU.mult))
                    lk.link(dve.tensor_reduce(S[3], R[6], AX.X, ALU.add))
                    lk.link(dve.tensor_scalar(S[4], S[3], 0.0, None, ALU.is_equal))
                    lk.link(dve.tensor_tensor(S[5], S[3], S[4], ALU.add))
                    lk.link(dve.reciprocal(S[6], S[5]))
                    lk.link(dve.tensor_tensor(R[7], R[6], over(S[6]), ALU.mult))
                    dve.tensor_scalar(cw[:, :, :], R[7], tg[:, 1, 1:2], None, ALU.mult).then_inc(mx.c, 1)
                    dve.wait_ge(mx.ct_mm, g + 1)
                    dve.tensor_copy(cT[:, :], ps[0:GB * E, 6, 0:P]).then_inc(mx.ct, 1)
                    add_rows(g, mx.b_mm, g, mx.xb)
                    for i in range(2):
                        for e in range(4):
                            for t in range(GB):
                                if e == 0:
                                    dve.wait_ge(mx.o, 8 * g + 4 * i + t + 1)
                                    if i:
                                        dve.wait_ge(mx.half, 8 * g + t + 1)
                                    else:
                                        dve.wait_ge(mx.xb, g + 1)
                                else:
                                    lk.wait(back=3 - t if e == 3 else 3)
                                xt = x[:, bass.ds(g * GB + t, 1), :].rearrange("p o d -> p (o d)")
                                ins = dve.scalar_tensor_tensor(out=xt, in0=ps[:, t, e * P:e * P + P],
                                                               scalar=cw[:, t, 4 * i + e:4 * i + e + 1], in1=xt,
                                                               op0=ALU.mult, op1=ALU.add)
                                if e < 3:
                                    lk.mark(ins)
                                else:
                                    ins.then_inc(mx.half, 1)
                    front_c(n)
                    lk.end()

            def head128():
                dve.wait_ge(ld.b, 16 * 8)
                K1 = DC + 1
                sl.mark(dve.tensor_copy(w2[0][:, 0, :], b_raw[:, 0, :]))
                sl.mark(dve.tensor_copy(w2[0][0:K1, 1:3, :], b_raw[0:K1, 1:3, :]))
                sl.mark(dve.tensor_copy(b_bq2[:, :], b_bq[:, :]))
                sl.link(dve.memset(scal[:, :], 1.0))
                sl.mark(dve.tensor_copy(scal[:, 0:4], rmsw[:, 0:1].to_broadcast([P, 4])))
                dve.tensor_tensor(w2[1][:, 0, :], b_raw[:, 0, :], f32(w2[0][:, 0, :]), ALU.subtract)
                dve.tensor_tensor(w2[1][0:K1, 1:3, :], b_raw[0:K1, 1:3, :], f32(w2[0][0:K1, 1:3, :]), ALU.subtract)
                dve.tensor_tensor(b_bq2[32:64, :], b_bq[32:64, :], f32(b_bq2[32:64, :]), ALU.subtract).then_inc(h1.w, 1)
                sl.wait()
                with dve.Fori(0, NG) as g:
                    n = g + 4 * NG + 1
                    gn = next_group(g)
                    lk = Link(dve, h1.link, 8, g)
                    stage(lk, g, K1, h1.ctx)
                    front_a(gn, n)
                    dve.wait_ge(h1.qhi, g + 1)
                    dve.tensor_tensor(q2[1][:, :], ps[:, 0, :], f32(q2[0][:, :]), ALU.subtract).then_inc(h1.q, 1)
                    dve.wait_ge(h1.khi, g + 1)
                    dve.tensor_tensor(k2[1][:, :, :].rearrange("p b t -> p (b t)"), ps[:, 1, 0:GB * SP],
                                      f32(k2[0][:, :, :]).rearrange("p b t -> p (b t)"), ALU.subtract).then_inc(h1.k, 1)
                    front_b(gn, n)
                    dve.wait_ge(h1.s, g + 1)
                    dve.tensor_reduce(nm2[:, :].unsqueeze(2),
                                      ps[:, 3, 0:GB * SP].rearrange("p (b t) -> p b t", b=GB)[:, :, 0:SK],
                                      AX.X, ALU.max, negate=True).then_inc(h1.max, 1)
                    dve.wait_ge(h1.t, g + 1)
                    dve.tensor_copy(nT2[:, :], ps[0:GB, 4, 0:P]).then_inc(h1.nT, 1)
                    front_c(n)
                    for b in range(2):
                        i = g * 2 + b
                        hi, lo = (t_[:, bass.ds(i, 1), :].rearrange("p o n -> p (o n)") for t_ in wb)
                        dve.wait_ge((ld.raw0, ld.raw1)[b], 16 * (g + NG + 1))
                        lk.link(dve.tensor_scalar(raw[b][:, :], raw[b][:, :], scal[:, bass.ds(i, 1)], None, ALU.mult))
                        lk.link(dve.tensor_scalar(hi, raw[b][:, :], 1.0, None, ALU.mult))
                        dve.tensor_tensor(lo, raw[b][:, :], f32(hi), ALU.subtract).then_inc(h1.big, 1)
                    for i in range(2):
                        dve.wait_ge(h1.o, 2 * g + i + 1)
                        lk.mark(dve.reciprocal(rden[:, 2 * i:2 * i + 2].unsqueeze(2),
                                               ps[:, (6, 0)[i], 0:2 * (D + 1)].rearrange("p (b d) -> p b d", b=2)[:, :, D:D + 1]))
                    lk.wait()
                    lk.link(dve.tensor_scalar(rden[:, 4:8], rden[:, 0:4], tg[:, 0, 2:3], None, ALU.mult))
                    for b in range(GB):
                        xt = x[:, bass.ds(g * GB + b, 1), :].rearrange("p o d -> p (o d)")
                        o_ = ps[:, (6, 0)[b // 2], (b % 2) * (D + 1):(b % 2) * (D + 1) + D]
                        ins = dve.scalar_tensor_tensor(out=xt, in0=o_, scalar=rden[:, 4 + b:5 + b], in1=xt,
                                                       op0=ALU.mult, op1=ALU.add)
                    ins.then_inc(h1.x, 1)
                    lk.end()

            def ternary():
                dve.wait_ge(ld.l3, 64)
                for j, w_ in enumerate((wfr, wpr)):
                    ins = dve.tensor_reduce(ta[:, 8 + j:9 + j], w_[:, :, :].rearrange("p c d -> p (c d)"), AX.X, ALU.add,
                                            apply_absolute_value=True)
                ins.then_inc(tn.sum, 1)
                dve.wait_ge(tn.gamma, 1)
                sl.link(dve.tensor_scalar(ta[:, 10:12], ps[:, 2, 0:2], 1.0 / (HID * D), 1e-6, ALU.mult, ALU.add))
                sl.mark(dve.tensor_scalar(ta[:, 12:14], ta[:, 10:12], 0.5, None, ALU.mult))
                sl.link(dve.tensor_scalar(ta[:, 14:16], ta[:, 10:12], -0.5, None, ALU.mult))
                for j, w_ in enumerate((wfr, wpr)):
                    wv_ = w_[:, :, :].rearrange("p c d -> p (c d)")
                    sl.link(dve.tensor_scalar(hg[:, j, :], wv_, ta[:, 14 + j:15 + j], None, ALU.is_lt))
                    ins = dve.scalar_tensor_tensor(out=wv_, in0=wv_, scalar=ta[:, 12 + j:13 + j], in1=hg[:, j, :],
                                                   op0=ALU.is_gt, op1=ALU.subtract)
                ins.then_inc(tn.w, 1)
                dve.wait_ge(tn.wT_mm, 1)
                dve.tensor_copy(wf[:, :, :].rearrange("p c h -> p (c h)"), ps[:, 0, :]).then_inc(tn.wT, 1)
                dve.wait_ge(tn.wT_mm, 2)
                dve.tensor_copy(wp[:, :, :].rearrange("p c h -> p (c h)"), ps[:, 1, :]).then_inc(tn.wT, 1)
                with dve.Fori(0, NG) as g:
                    n = g + 7 * NG + 1
                    gn = next_group(g)
                    lk = Link(dve, tn.link, 11, g)
                    front_a(gn, n)
                    front_b(gn, n)
                    for t in range(GB):
                        dve.wait_ge(tn.act, 4 * g + t + 1)
                        lk.mark(dve.bn_stats(st[:, t, :], hg[:, t, :]))
                    variance(lk, st, HID, mh[:, 0, :], mh[:, 1, :])
                    dve.tensor_scalar(ta[:, 0:4], mh[:, 1, :], 1e-5, None, ALU.add).then_inc(tn.var, 1)
                    dve.wait_ge(tn.rstd, g + 1)
                    for t in range(GB):
                        dve.tensor_scalar(hg[:, t, :], hg[:, t, :], mh[:, 0, t:t + 1], ta[:, 4 + t:5 + t],
                                          ALU.subtract, ALU.mult).then_inc(tn.norm, 1)
                    front_c(n)
                    dve.wait_ge(tn.y, g + 1)
                    add_to_x(g * GB, GB, ps[:, 6, :], tg[:, 1, 3:4], tn.x)
                    lk.end()

            dve.wait_ge(ld.const, 16)
            dve.wait_ge(ld.x, 16)
            front_a(0, 0)
            front_b(0, 0)
            dve.wait_ge(su.zero, 4)
            dve.wait_ge(su.pe, 1)
            for i in range(4):
                o_ = ps[0:DC, i, 0:GB * SP].rearrange("p (b t) -> p b t", b=GB)[:, :, 0:SK]
                dve.tensor_copy(ctxT[0:DC, GB * i:GB * i + GB, 0:SK], o_).then_inc(su.dve, 1)
            front_c(0)
            dve.wait_ge(su.dve, 4)
            dve.wait_ge(ld.xrest, 16)
            dve.wait_ge(su.tanh, 1)
            heads8(0, 0)
            experts(0, 1)
            heads64()
            mixed()
            head128()
            experts(1, 5)
            heads8(1, 6)
            ternary()


_PASS = ["x", "ctx_768", "g_xattn", "g_ffn",
         "L0_xattn_wq", "L0_xattn_bq", "L0_xattn_wk", "L0_xattn_bk", "L0_xattn_wv", "L0_xattn_bv", "L0_xattn_wo",
         "L0_xattn_bo", "L0_ffn_uzman_embeddings", "L0_ffn_W1", "L0_ffn_b1", "L0_ffn_W2", "L0_ffn_b2",
         "L0_ffn_onbellek_durumu", "L1_xattn_Wq", "L1_xattn_Wk", "L1_xattn_Wv", "L1_xattn_Wo", "L1_xattn_bo",
         "L1_ffn_gate_w", "L1_ffn_gate_b", "L1_ffn_expert_w", "L1_ffn_expert_b", "L2_xattn_Wq", "L2_xattn_bq",
         "L2_xattn_Wk", "L2_xattn_bk", "L2_xattn_Wv", "L2_xattn_bv", "L2_ffn_rms_w", "L2_ffn_gate_w", "L2_ffn_W1",
         "L2_ffn_b1", "L2_ffn_W2", "L2_ffn_b2", "L3_xattn_Wq", "L3_xattn_bq", "L3_xattn_Wk", "L3_xattn_bk",
         "L3_xattn_Wv", "L3_xattn_bv", "L3_xattn_Wo", "L3_xattn_bo", "L3_ffn_W_fc", "L3_ffn_ln_w", "L3_ffn_ln_b",
         "L3_ffn_W_proj"]


def kernel(**inputs):
    import concourse.bacc as bacc
    import concourse.bass_utils as bass_utils

    nc = bacc.Bacc("TRN2", target_bir_lowering=False, num_devices=1)
    arrays, args = {}, {}
    given = {n: np.ascontiguousarray(inputs[n]) for n in _PASS}
    for n, src in (("L0_b1", "L0_ffn_b1"), ("L2_b1", "L2_ffn_b1"), ("ln_w", "L3_ffn_ln_w"), ("ln_b", "L3_ffn_ln_b")):
        given[n] = np.ascontiguousarray(np.asarray(inputs[src]).reshape(-1, P).T)
    given["const"] = constants()
    given["sel"] = selectors()
    for n, v in given.items():
        arrays[f"in_{n}"] = v
        args[n] = nc.dram_tensor(f"in_{n}", v.shape, mybir.dt.from_np(v.dtype), kind="ExternalInput").ap()
    o = nc.dram_tensor("out_0", (B, P, D), F32, kind="ExternalOutput").ap()
    build(nc, args, o)
    r = bass_utils.run_bass_kernel_spmd(nc, [arrays], core_ids=[0])
    return r.results[0]["out_0"]
```

```python
from contextlib import ExitStack

import concourse.bass as bass
import numpy as np
from concourse import mybir

F32 = mybir.dt.float32
F32R = mybir.dt.float32r
ALU = mybir.AluOpType
ACT = mybir.ActivationFunctionType
AX = mybir.AxisListType

P = 128
B = 16
D = 128
SK = 77
SP = 78
DC = 96
GB = 4
NG = B // GB
GT = GB * P
H = 16
D8 = 8
HG = 4
D64 = 64
INNER = H * D64
C1 = INNER // P
E = 8
HID = 512
NC_HID = HID // P
WCH = 2048

C_ID = 0
C_CQ, C_MQ, C_CK, C_MK = 128, 129, 130, 131
C_MASK = 132
C_NA = 136
C_NB = C_NA + 33
C_UP = C_NB + 33
C_DOWN = C_UP + E
C_HALF = C_DOWN + E
C_TM = C_HALF + GB
C_ONE = C_TM + GB
C_PLUS = C_ONE + P
C_SELB = C_PLUS + GB
NCONST = C_SELB + GB * SK


def constants():
    c = np.zeros((P, NCONST), np.float32)
    c[:, C_ID:C_ID + P] = np.eye(P)
    role = (np.arange(P) % 32) // D8
    c[:, C_CQ] = np.where(role == 1, -1, 1)
    c[:, C_MQ] = role == 1
    c[:, C_CK] = np.where(role == 2, -1, 1)
    c[:, C_MK] = role == 2
    for j in range(HG):
        c[32 * j:32 * j + 32, C_MASK + j] = 1
    c[:, C_NA:C_NA + 33] = 1.0
    c[:, C_NB:C_NB + 33] = 1e-5
    c[:, C_NA + 20:C_NA + 24] = 1.0 + 1e-6
    c[:, C_NB + 20:C_NB + 24] = 1e-11
    c[:, C_UP:C_UP + E] = np.arange(1, E + 1)
    c[:, C_DOWN:C_DOWN + E] = np.arange(E, 0, -1)
    c[:, C_HALF:C_HALF + GB] = -0.5
    for t in range(GB):
        c[E * t:E * t + E, C_TM + t] = 1
        c[t, C_SELB + t * SK:C_SELB + t * SK + SK] = 1
    c[:, C_ONE:C_ONE + P] = 1
    c[:, C_PLUS:C_PLUS + GB] = 0.5
    return c


def build(nc, a, out):
    ctx = ExitStack()
    with ctx:
        def sem(name):
            return ctx.enter_context(nc.semaphore(name))

        def sems(prefix, *names):
            return type(prefix, (), {n: sem(f"{prefix}_{n}") for n in names})

        ps = ctx.enter_context(nc.psum_tensor("banks", [P, 8, 512], F32))

        top = [(nc.sbuf_base + 63) // 64 * 64]

        def place(name, shape, dt=F32, at=None):
            size = int(np.prod(shape[1:])) * 4
            offset = top[0] if at is None else at[0]
            t = nc.alloc_sbuf_tensor_at(name, shape, dt, offset=offset)
            size = (size + 63) // 64 * 64
            if at is None:
                top[0] += size
            else:
                at[0] += size
                at[1] = max(at[1], at[0])
            return t

        const = place("const", [P, NCONST])
        x = place("x", [P, B, D])
        xn = place("xn", [P, GB, D])
        xhi = place("xhi", [P, GT], F32R)
        xlo = place("xlo", [P, GT], F32R)
        ctxT = place("ctxT", [P, B, SP])
        chi = place("chi", [P, GB, SP], F32R)
        clo = place("clo", [P, GB, SP], F32R)
        tg = place("tg", [P, 2, 4])
        st = place("st", [P, GB, 6])
        mv = place("mv", [P, GB, 2])
        vv = place("vv", [P, GB])
        rstd = place("rstd", [P, GB])
        fs = place("fs", [P, 5, GB])
        mh = place("mh", [P, 2, GB])
        scal = place("scal", [P, 8])
        ones2 = place("ones2", [64, GT], F32R)
        idn = const[:, C_ID:C_ID + P]

        a_raw = place("a_raw", [P, 4, P])
        a_bq = place("a_bq", [64, P])
        a_bo = place("a_bo", [1, P])
        wq = [place("wq_hi", [P, H, 4, D8], F32R), place("wq_lo", [P, H, 4, D8], F32R)]
        wk = [place("wk_hi", [P, H, 4, D8], F32R), place("wk_lo", [P, H, 4, D8], F32R)]
        wv = [place("wv_hi", [P, P], F32R), place("wv_lo", [P, P], F32R)]
        wo = place("wo", [P, P])
        bo = place("bo", [1, P])
        bq2 = place("bq2", [64, H, 4, D8], F32R)
        b_raw = place("b_raw", [P, 3, P])
        w2 = [place("w2_hi", [P, 3, P], F32R), place("w2_lo", [P, 3, P], F32R)]
        b_bq = place("b_bq", [64, P])
        b_bq2 = place("b_bq2", [64, P], F32R)
        rraw = place("rraw", [P, 16])
        rwt = [place("rw_hi", [P, 16], F32R), place("rw_lo", [P, 16], F32R)]
        emb = place("emb", [E, 3, D])
        emb_s = place("emb_s", [E, 4])
        rowb = place("rowb", [P, E])
        b2rep = place("b2rep", [GB * E, D])
        b2m = place("b2m", [GB * E, GB, D])
        b1 = place("b1", [P, E * NC_HID])
        rmsw = place("rmsw", [P, 1])
        cw = place("cw", [P, GB, E])
        cT = place("cT", [GB * E, P])
        rt = place("rt", [P, 12, GB, E])
        rs = place("rs", [P, 12, GB])
        raw = [place("raw0", [P, WCH // 2]), place("raw1", [P, WCH // 2])]
        lregion = [top[0], top[0]]
        l1w = [place("l1w_hi", [P, 4, INNER], F32R, lregion), place("l1w_lo", [P, 4, INNER], F32R, lregion)]
        lend = lregion[1]
        lregion = [top[0], lend]
        v8 = place("v8", [SK, GB * H * P + P], F32, lregion)
        top[0] = lregion[1]

        wregion = [top[0], top[0]]
        wb = [place("wb_hi", [P, 8, WCH // 2], F32R, wregion), place("wb_lo", [P, 8, WCH // 2], F32R, wregion)]
        wend = wregion[1]
        wregion = [top[0], wend]
        wo1 = place("wo1", [P, C1, D], F32, wregion)
        q1 = place("q1", [P, C1, GT], F32, wregion)
        k1 = place("k1", [P, C1, GB, SP], F32, wregion)
        v1 = place("v1", [SK, GB, H, D64], F32, wregion)
        assert wregion[0] <= wend
        wregion = [top[0], wend]
        wf = place("wf", [P, 4, P], F32R, wregion)
        wp = place("wp", [P, 4, P], F32, wregion)
        wfr = place("wfr", [P, 4, P], F32, wregion)
        wpr = place("wpr", [P, 4, P], F32, wregion)
        lnw = place("lnw", [P, 4], F32, wregion)
        lnb = place("lnb", [P, 4], F32, wregion)
        ta = place("ta", [P, 16], F32, wregion)
        top[0] = wend

        rden = place("rden", [P, H])
        s0 = top[0]
        s = [s0, s0]
        prob = place("prob", [SK, 4, 512], F32, s)
        sh = [place("sh0", [P, 4, 4, SK], F32, s), place("sh1", [P, 4, 4, SK], F32, s)]
        top_s = place("top_s", [P, H], F32, s)
        den = place("den", [P, H], F32, s)
        rd = [place("rd0", [P, H], F32, s), place("rd1", [P, H], F32, s)]
        sa = s[0]
        ctok = place("ctok", [SK, B, DC], F32, s)
        s = [sa, s[1]]
        q = place("q", [P, HG, GB, P], F32R, s)
        k = place("k", [P, HG, GB, SP], F32R, s)
        kbd = [place("kbd0", [P, HG, HG, SP], F32R, s), place("kbd1", [P, HG, HG, SP], F32R, s)]
        oT8 = place("oT8", [P, P], F32, s)
        s = [sa, s[1]]
        oT = place("oT", [P, C1, P], F32, s)
        s = [sa, s[1]]
        q2 = [place("q2_hi", [P, GT], F32R, s), place("q2_lo", [P, GT], F32R, s)]
        k2 = [place("k2_hi", [P, GB, SP], F32R, s), place("k2_lo", [P, GB, SP], F32R, s)]
        v2 = place("v2", [SK, GB, D + 1], F32, s)
        nm2 = place("nm2", [P, GB], F32, s)
        nT2 = place("nT2", [GB, P], F32, s)
        s = [s0, s[1]]
        hf = place("hf", [P, 4, 512], F32, s)
        hhi = [place("hhi0", [P, 4, 512], F32R, s), place("hhi1", [P, 4, 512], F32R, s)]
        hlo = [place("hlo0", [P, 4, 512], F32R, s), place("hlo1", [P, 4, 512], F32R, s)]
        s = [s0, s[1]]
        hg = place("hg", [P, GB, HID], F32, s)
        hgT = place("hgT", [P, 2, 4, P], F32, s)
        assert s[1] <= nc.sbuf_usable_end, (s[1], nc.sbuf_usable_end)

        ld = sems("loaded", "const", "x", "xrest", "ctx", "gate", "a", "r", "raw0", "raw1", "l1raw", "l1", "b", "l3")
        su = sems("setup", "braw", "zero", "dve", "tanh", "pe", "scratch", "plink", "vlink")
        fr = sems("front", "link", "var", "rstd", "xn", "xt", "hi", "lo")
        h8 = sems("heads8", "w", "ctx", "mm", "hi", "lo", "v_mm", "v", "kbd", "s", "max", "sub", "exp", "den", "rden",
                  "prob", "t", "pT", "o", "oT", "y", "x", "link")
        ff = sems("experts", "w_mm", "w_ss", "w_rt", "w", "r", "nn", "rn", "d", "tanh", "c", "ct_mm", "ct", "b_mm", "xb",
                  "h", "act", "split", "o", "x", "link", "link1")
        h64 = sems("heads64", "ctx", "qmm", "kmm", "vmm", "q", "k", "v", "s", "max", "sub", "exp", "den", "rden",
                   "prob", "t", "pT", "o", "oT", "y", "x", "link")
        h1 = sems("head128", "w", "ctx", "qmm", "qhi", "q", "kmm", "khi", "k", "vmm", "v", "s", "max", "t", "nT",
                  "st", "exp", "o", "x", "big", "link")
        mx = sems("mixed", "w", "r", "d", "e", "c", "ct_mm", "ct", "b_mm", "xb", "o", "half", "x", "link")
        tn = sems("ternary", "sum", "gamma", "w", "wT_mm", "wT", "h", "act", "var", "rstd", "norm", "t_mm", "t",
                  "y", "x", "link")
        wr = sems("split", "big", "l1")
        stored = sem("stored")

        block = ctx.enter_context(nc.Block())

        def row(ap):
            return ap.rearrange("(o n) -> o n", o=1)

        def f32(ap):
            return ap.bitcast(F32)

        def done(kind):
            return {"h8": (h8.x, B), "ff": (ff.x, NG * E), "h64": (h64.x, B), "mx": (mx.half, 8 * NG),
                    "h1": (h1.x, NG), "tn": (tn.x, NG)}[kind]

        def wait_done(eng, kind, runs):
            s_, n_ = done(kind)
            eng.wait_ge(s_, n_ * runs)

        def next_group(g):
            return 0 if isinstance(g, int) else (g + 1) % NG

        class Link:

            def __init__(self, eng, s_, per, step=0):
                self.eng, self.sem, self.per, self.step, self.n = eng, s_, per, step, 0

            def mark(self, ins):
                self.n += 1
                ins.then_inc(self.sem, 1)

            def wait(self, back=0):
                assert self.n > back
                self.eng.wait_ge(self.sem, self.step * self.per + self.n - back)

            def link(self, ins):
                self.mark(ins)
                self.wait()

            def end(self):
                assert self.n == self.per, (self.n, self.per)

        N_A = 9

        @block.sync
        def _(sp):
            def load_heads8(layer):
                n = f"L{layer}_xattn_"
                c = "w" if layer == 0 else "W"
                sp.dma_start(a_raw[:, 0, :], a[n + c + "q"]).then_inc(ld.a, 16)
                sp.dma_start(a_raw[0:DC, 1, :], a[n + c + "k"]).then_inc(ld.a, 16)
                sp.dma_start(a_raw[DC:DC + 1, 1, :], row(a[n + "bk"])).then_inc(ld.a, 16)
                sp.dma_start(a_raw[0:DC, 2, :], a[n + c + "v"]).then_inc(ld.a, 16)
                sp.dma_start(a_raw[DC:DC + 1, 2, :], row(a[n + "bv"])).then_inc(ld.a, 16)
                sp.dma_start(a_raw[:, 3, :], a[n + c + "o"]).then_inc(ld.a, 16)
                sp.dma_start(a_bq[0:1, :], row(a[n + "bq"])).then_inc(ld.a, 16)
                sp.dma_start(a_bq[32:33, :], row(a[n + "bq"])).then_inc(ld.a, 16)
                sp.dma_start(a_bo[:, :], row(a[n + "bo"])).then_inc(ld.a, 16)

            def load_experts(layer, i):
                w1 = a[f"L{layer}_ffn_W1"].rearrange("e d h -> d e h")
                w2 = a[f"L{layer}_ffn_W2"].rearrange("e (c p) d -> p (e c) d", p=P)
                src = w1[:, 2 * i:2 * i + 2, :] if i < 4 else w2[:, 8 * i - 32:8 * i - 24, :]
                n = 2 if i < 4 else 8
                sp.dma_start(raw[i % 2][:, :].rearrange("p (e h) -> p e h", e=n), src)\
                  .then_inc((ld.raw0, ld.raw1)[i % 2], 16)

            def load_b2(name):
                for t in range(GB):
                    sp.dma_start(b2rep[E * t:E * t + E, :], a[name]).then_inc(ld.r, 16)

            sp.dma_start(const[:, :], a["const"]).then_inc(ld.const, 16)
            xd = a["x"].rearrange("b t d -> t b d")
            sp.dma_start(x[:, 0:GB, :], xd[:, 0:GB, :]).then_inc(ld.x, 16)
            sp.dma_start(ctok[:, :, :], a["ctx_768"].rearrange("b s d -> s b d")).then_inc(ld.ctx, 16)
            sp.wait_ge(su.braw, 1)
            load_heads8(0)
            sp.dma_start(x[:, GB:B, :], xd[:, GB:B, :]).then_inc(ld.xrest, 16)
            sp.dma_start(tg[:, 0, :], row(a["g_xattn"]).to_broadcast([P, 4])).then_inc(ld.gate, 16)
            sp.dma_start(tg[:, 1, :], row(a["g_ffn"]).to_broadcast([P, 4])).then_inc(ld.gate, 16)
            sp.dma_start(emb[:, 0, :], a["L0_ffn_uzman_embeddings"]).then_inc(ld.r, 16)
            sp.dma_start(rowb[:, :], row(a["L0_ffn_onbellek_durumu"]).to_broadcast([P, E])).then_inc(ld.r, 16)
            sp.dma_start(b1[:, :], a["L0_b1"]).then_inc(ld.r, 16)
            load_b2("L0_ffn_b2")
            for i in range(8):
                if i >= 2:
                    sp.wait_ge(wr.big, i - 1)
                load_experts(0, i)
            sp.wait_ge(wr.big, 7)
            sp.dma_start(raw[0][:, :], a["L1_xattn_Wq"]).then_inc(ld.l1raw, 16)
            for i, n in enumerate(("L1_xattn_Wk", "L1_xattn_Wv")):
                sp.wait_ge(wr.l1, i + 1)
                sp.dma_start(raw[0][0:DC, :], a[n]).then_inc(ld.l1raw, 16)
            sp.wait_ge(wr.l1, 3)
            sp.dma_start(raw[0][:, :].rearrange("p (e h) -> p e h", e=E),
                         a["L1_ffn_expert_w"].rearrange("e d h -> d e h")).then_inc(ld.l1raw, 16)
            wait_done(sp, "ff", 1)
            sp.dma_start(wo1[:, :, :], a["L1_xattn_Wo"].rearrange("(c p) d -> p c d", p=P)).then_inc(ld.l1, 16)
            sp.dma_start(bo[:, :], row(a["L1_xattn_bo"])).then_inc(ld.l1, 16)
            sp.dma_start(rraw[:, 0:E], a["L1_ffn_gate_w"]).then_inc(ld.r, 16)
            sp.dma_start(rowb[:, :], row(a["L1_ffn_gate_b"]).to_broadcast([P, E])).then_inc(ld.r, 16)
            load_b2("L1_ffn_expert_b")
            sp.dma_start(b_raw[:, 0, :], a["L2_xattn_Wq"]).then_inc(ld.b, 16)
            for j, n in ((1, "k"), (2, "v")):
                sp.dma_start(b_raw[0:DC, j, :], a["L2_xattn_W" + n]).then_inc(ld.b, 16)
                sp.dma_start(b_raw[DC:DC + 1, j, :], row(a["L2_xattn_b" + n])).then_inc(ld.b, 16)
            sp.dma_start(b_bq[0:1, :], row(a["L2_xattn_bq"])).then_inc(ld.b, 16)
            sp.dma_start(b_bq[32:33, :], row(a["L2_xattn_bq"])).then_inc(ld.b, 16)
            load_heads8(3)
            sp.dma_start(rmsw[:, :], a["L2_ffn_rms_w"].rearrange("(p o) -> p o", o=1)).then_inc(ld.b, 16)
            sp.wait_ge(wr.l1, 4)
            for i in range(8):
                if i >= 2:
                    sp.wait_ge(h1.big, i - 1)
                if i == 2:
                    wait_done(sp, "mx", 1)
                    sp.dma_start(emb[:, 0, :], a["L2_ffn_gate_w"]).then_inc(ld.r, 16)
                    sp.dma_start(b1[:, :], a["L2_b1"]).then_inc(ld.r, 16)
                    load_b2("L2_ffn_b2")
                load_experts(2, i)
            wait_done(sp, "ff", 2)
            sp.dma_start(wfr[:, :, :], a["L3_ffn_W_fc"].rearrange("(c p) d -> p c d", p=P)).then_inc(ld.l3, 16)
            sp.dma_start(wpr[:, :, :], a["L3_ffn_W_proj"].rearrange("d (c p) -> d c p", p=P)).then_inc(ld.l3, 16)
            sp.dma_start(lnw[:, :], a["ln_w"]).then_inc(ld.l3, 16)
            sp.dma_start(lnb[:, :], a["ln_b"]).then_inc(ld.l3, 16)
            od = out.rearrange("b t d -> t b d")
            for g in range(NG):
                sp.wait_ge(tn.x, g + 1)
                sp.dma_start(od[:, GB * g:GB * g + GB, :], x[:, GB * g:GB * g + GB, :]).then_inc(stored, 16)
            sp.wait_ge(stored, 16 * NG)

        @block.gpsimd
        def _(pool):
            def rsqrt_front(n):
                pool.wait_ge(fr.var, n + 1)
                pool.tensor_tensor(rstd[:, :], vv[:, :], const[:, C_HALF:C_HALF + GB], ALU.pow).then_inc(fr.rstd, 1)

            def split_chunk(src, rows, hi, lo, links, done_, count):
                pool.tensor_copy(hi, src).then_inc(su.plink, 1)
                pool.wait_ge(su.plink, links)
                pool.tensor_tensor(lo, src, f32(hi), ALU.subtract).then_inc(done_, 1)

            def keys(G, b):
                if b == 0:
                    pool.wait_ge(h8.lo, 8 * G + 8)
                if b >= 2:
                    pool.wait_ge(h8.s, 4 * (4 * G + b - 1))
                kb = f32(k[:, :, b, :]).unsqueeze(2).to_broadcast([P, HG, HG, SP])
                m = const[:, C_MASK:C_MASK + HG].unsqueeze(1).unsqueeze(3).to_broadcast([P, HG, HG, SP])
                pool.tensor_tensor(kbd[b % 2][:, :, :, :], kb, m, ALU.mult).then_inc(h8.kbd, 1)

            def normalise(hs, G, b):
                for half in range(2):
                    pool.wait_ge(hs.rden, 2 * (4 * G + b) + half + 1)
                    e_ = sh[b % 2][:, 2 * half:2 * half + 2, :, :].rearrange("p u h t -> p (u h) t")
                    r_ = rd[b % 2][:, 8 * half:8 * half + 8].unsqueeze(2).to_broadcast([P, 8, SK])
                    pool.tensor_tensor(e_, e_, r_, ALU.mult).then_inc(hs.prob, 1)

            def values_scratch():
                pool.memset(v8[:, :], 0.0).then_inc(su.scratch, 1)

            pool.memset(a_bq[:, :], 0.0).then_inc(su.braw, 1)
            pool.memset(b_bq[:, :], 0.0).then_inc(su.zero, 1)
            pool.memset(ctxT[0:DC, :, SK:SP], 0.0).then_inc(su.zero, 1)
            pool.wait_ge(su.zero, 2)
            pool.memset(ctxT[DC:DC + 1, :, :], 1.0).then_inc(su.zero, 1)
            pool.wait_ge(su.zero, 3)
            for t in (*wq, *wk):
                pool.memset(f32(t[:, :, :, :]), 0.0).then_inc(su.zero, 1)
            pool.memset(f32(bq2[:, :, :, :]), 0.0).then_inc(su.zero, 1)
            pool.memset(f32(ones2[:, :]), 1.0).then_inc(su.zero, 1)
            pool.wait_ge(ld.const, 16)
            rsqrt_front(0)
            values_scratch()
            for g in range(NG):
                rsqrt_front(g + 1)
                keys(g, 0)
                for b in range(GB):
                    if b < GB - 1:
                        keys(g, b + 1)
                    normalise(h8, g, b)
                    if b < 2:
                        i = 2 * g + b
                        pool.wait_ge((ld.raw0, ld.raw1)[b], 16 * (g + 1))
                        split_chunk(raw[b][:, :], P, wb[0][:, i, :], wb[1][:, i, :], i + 1, wr.big, i + 1)
            pool.wait_ge(ff.w_ss, 1)
            pool.tensor_tensor(emb_s[:, 1:2], emb_s[:, 0:1], const[0:E, C_PLUS:C_PLUS + 1], ALU.pow).then_inc(ff.w_rt, 1)
            for g in range(NG):
                pool.wait_ge(ff.nn, g + 1)
                pool.tensor_tensor(rs[:, 1, :], rs[:, 0, :], const[:, C_PLUS:C_PLUS + GB], ALU.pow).then_inc(ff.rn, 1)
                rsqrt_front(NG + g + 1)
                rows = DC if g in (1, 2) else P
                pool.wait_ge(ld.l1raw, 16 * (g + 1))
                split_chunk(raw[0][0:rows, :], rows, l1w[0][0:rows, g, :], l1w[1][0:rows, g, :], 8 + g + 1, wr.l1, g + 1)
            with pool.Fori(0, NG) as g:
                rsqrt_front(g + 2 * NG + 1)
                for b in range(GB):
                    normalise(h64, g, b)
            with pool.Fori(0, NG) as g:
                rsqrt_front(g + 3 * NG + 1)
            wait_done(pool, "mx", 1)
            pool.memset(v2[:, :, D:D + 1], 1.0).then_inc(su.scratch, 1)
            values_scratch()
            with pool.Fori(0, NG) as g:
                rsqrt_front(g + 4 * NG + 1)
            with pool.Fori(0, NG) as g:
                rsqrt_front(g + 5 * NG + 1)
            with pool.Fori(0, NG) as g:
                rsqrt_front(g + 6 * NG + 1)
                keys(g + NG, 0)
                for b in range(GB):
                    if b < GB - 1:
                        keys(g + NG, b + 1)
                    normalise(h8, g + NG, b)
            with pool.Fori(0, NG) as g:
                rsqrt_front(g + 7 * NG + 1)
                pool.wait_ge(tn.var, g + 1)
                pool.tensor_tensor(ta[:, 4:8], ta[:, 0:4], const[:, C_HALF:C_HALF + GB], ALU.pow).then_inc(tn.rstd, 1)

        @block.scalar
        def _(act):
            def copy(o_, i_, **kw):
                return act.activation(o_, i_, ACT.Copy, **kw)

            def front(n):
                act.wait_ge(fr.xt, n + 1)
                copy(xhi[:, :], ps[:, 7, :]).then_inc(fr.hi, 1)

            def attend(hs, G, scale, outputs):
                def exps(i, units):
                    for u in units:
                        act.wait_ge(hs.sub, 4 * (4 * G + i) + u + 1)
                        e_ = sh[i % 2][:, u, :, :].rearrange("p h t -> p (h t)")
                        act.activation(e_, e_, ACT.Exp, scale=scale).then_inc(hs.exp, 1)

                for i in range(GB + 2):
                    if i >= 2:
                        outputs(i - 2)
                    if i < GB:
                        exps(i, (0, 1))
                    if 1 <= i <= GB:
                        for u in range(4):
                            act.wait_ge(hs.t, 4 * (4 * G + i - 1) + u + 1)
                            copy(prob[:, u, :], ps[0:SK, 2 + u, :]).then_inc(hs.pT, 1)
                    if i < GB:
                        exps(i, (2, 3))

            def heads8(run, phase):
                with act.Fori(0, NG) as g:
                    G = g + NG * run
                    for u in range(8):
                        act.wait_ge(h8.mm, 8 * G + u + 1)
                        bank = ps[:, u % 6, :]
                        if u < 4:
                            copy(q[:, u, :, :].rearrange("p b t -> p (b t)"), bank,
                                 scale=const[:, C_CQ:C_CQ + 1]).then_inc(h8.hi, 1)
                        else:
                            copy(k[:, u - 4, :, :].rearrange("p b t -> p (b t)"), bank[:, 0:GB * SP],
                                 scale=const[:, C_CK:C_CK + 1]).then_inc(h8.hi, 1)
                    front(g + NG * phase + 1)
                    act.wait_ge(h8.v_mm, G + 1)
                    for b in range(GB):
                        blocks = v8[:, b * H * P:b * H * P + H * (P + D8)].rearrange("p (h w) -> p h w", w=P + D8)
                        ins = copy(blocks[:, :, 0:D8], ps[0:SK, 6, b * P:b * P + P].rearrange("p (h d) -> p h d", h=H))
                    ins.then_inc(h8.v, 1)

                    def outputs(b):
                        act.wait_ge(h8.o, 4 * G + b + 1)
                        copy(oT8[:, :], ps[:, 6, 0:P]).then_inc(h8.oT, 1)

                    attend(h8, G, D8 ** -0.5, outputs)

            def experts(run, phase, func):
                with act.Fori(0, NG) as g:
                    G = g + NG * run
                    if run:
                        act.wait_ge(ff.d, G + 1)
                        act.activation(rt[:, 3, :, :], rt[:, 2, :, :], ACT.Tanh, scale=0.5).then_inc(ff.tanh, 1)
                    else:
                        act.wait_ge(ff.d, G + 1)
                        act.activation(rs[:, 9, :], rs[:, 8, :], ACT.Tanh, scale=0.5).then_inc(ff.tanh, 1)
                    for u in range(E * NC_HID):
                        if u >= 4:
                            act.wait_ge(ff.split, 32 * G + u - 3)
                        act.wait_ge(ff.h, 32 * G + u + 1)
                        act.activation(hf[:, u % 4, :], ps[:, u % 4, :], func, bias=b1[:, u:u + 1])\
                           .then_inc(ff.act, 1)
                    front(g + NG * phase + 1)

            def heads64():
                with act.Fori(0, NG) as g:
                    for c in range(C1):
                        act.wait_ge(h64.qmm, 8 * g + c + 1)
                        copy(q1[:, c, :], ps[:, c % 4, :]).then_inc(h64.q, 1)
                    for i in range(2 * GB):
                        act.wait_ge(h64.vmm, 8 * g + i + 1)
                        copy(v1[:, i // 2, 8 * (i % 2):8 * (i % 2) + 8, :].rearrange("p h d -> p (h d)"),
                             ps[0:SK, i % 4, :]).then_inc(h64.v, 1)
                    front(g + 2 * NG + 1)

                    def outputs(b):
                        for half in range(2):
                            act.wait_ge(h64.o, 2 * (4 * g + b) + half + 1)
                            copy(oT[:, 4 * half:4 * half + 4, :].rearrange("p c t -> p (c t)"), ps[:, 6 + half, :])\
                                .then_inc(h64.oT, 1)

                    attend(h64, g, D64 ** -0.5, outputs)

            def mixed():
                with act.Fori(0, NG) as g:
                    act.wait_ge(mx.d, g + 1)
                    act.activation(rt[:, 3, :, :], rt[:, 2, :, :], ACT.Exp).then_inc(mx.e, 1)
                    front(g + 3 * NG + 1)

            def head128():
                with act.Fori(0, NG) as g:
                    act.wait_ge(h1.qmm, g + 1)
                    copy(q2[0][:, :], ps[:, 0, :]).then_inc(h1.qhi, 1)
                    act.wait_ge(h1.kmm, g + 1)
                    copy(k2[0][:, :, :].rearrange("p b t -> p (b t)"), ps[:, 1, 0:GB * SP]).then_inc(h1.khi, 1)
                    act.wait_ge(h1.vmm, g + 1)
                    copy(v2[:, :, 0:D], ps[0:SK, 2, :].rearrange("p (b d) -> p b d", b=GB)).then_inc(h1.v, 1)
                    front(g + 4 * NG + 1)
                    act.wait_ge(h1.st, g + 1)
                    act.activation(prob[:, 0, :], ps[0:SK, 5, :], ACT.Exp).then_inc(h1.exp, 1)

            def ternary():
                with act.Fori(0, NG) as g:
                    for t in range(GB):
                        act.wait_ge(tn.h, 4 * g + t + 1)
                        act.activation(hg[:, t, :], ps[:, t, :], ACT.Gelu).then_inc(tn.act, 1)
                    front(g + 7 * NG + 1)
                    for t in range(GB):
                        act.wait_ge(tn.t_mm, 4 * g + t + 1)
                        for c in range(NC_HID):
                            ins = act.activation(hgT[:, t % 2, c, :], ps[:, 4 + t % 2, c * P:c * P + P], ACT.Identity,
                                                 scale=lnw[:, c:c + 1], bias=lnb[:, c:c + 1])
                        ins.then_inc(tn.t, 1)

            act.wait_ge(ld.gate, 32)
            act.activation(tg[:, :, :], tg[:, :, :], ACT.Tanh).then_inc(su.tanh, 1)
            front(0)
            heads8(0, 0)
            act.wait_ge(ld.r, 16 * 7)
            experts(0, 1, ACT.Gelu)
            heads64()
            mixed()
            head128()
            act.wait_ge(ld.r, 16 * 19)
            experts(1, 5, ACT.Silu)
            heads8(1, 6)
            act.wait_ge(ld.l3, 64)
            ternary()

        @block.tensor
        def _(pe):
            def split3(o_, w_, m_, stop=True):
                pe.matmul(o_, w_[0], m_[0], start=True, stop=False)
                pe.matmul(o_, w_[1], m_[0], start=False, stop=False)
                return pe.matmul(o_, w_[0], m_[1], start=False, stop=stop)

            xT = (xhi[:, :], xlo[:, :])

            def front(n):
                pe.wait_ge(fr.xn, n + 1)
                for t in range(GB):
                    ins = pe.transpose(ps[:, 7, t * P:t * P + P], xn[:, t, :], idn)
                ins.then_inc(fr.xt, 1)

            def tokens(src, t):
                return tuple(p_[:, t * P:t * P + P] for p_ in src)

            def attend(hs, G, scores, values, project):
                for i in range(GB + 2):
                    n = 4 * (4 * G + i)
                    if i < GB:
                        for u in (0, 1):
                            if i:
                                pe.wait_ge(hs.sub, n - 2 + u + 1)
                            scores(i, u).then_inc(hs.s, 1)
                    if i >= 2:
                        project(i - 2)
                    if 1 <= i <= GB:
                        for u in range(4):
                            if u % 2 == 0:
                                pe.wait_ge(hs.prob, 2 * (4 * G + i - 1) + u // 2 + 1)
                            if i >= 2:
                                pe.wait_ge(hs.pT, n - 8 + u + 1)
                            for h_ in range(4):
                                ins = pe.transpose(ps[0:SK, 2 + u, h_ * P:h_ * P + P], sh[(i - 1) % 2][:, u, h_, :], idn)
                            ins.then_inc(hs.t, 1)
                    if i < GB:
                        for u in (2, 3):
                            pe.wait_ge(hs.sub, n + u - 1)
                            scores(i, u).then_inc(hs.s, 1)
                    if 1 <= i <= GB:
                        pe.wait_ge(hs.pT, n)
                        if i >= 2:
                            pe.wait_ge(hs.x, 4 * G + i - 1)
                        values(i - 1)

            def heads8(run, phase):
                wait_done(pe, "ff", 2) if run else None
                pe.wait_ge(su.scratch, 3 if run else 1)
                pe.wait_ge(h8.w, run + 1)
                with pe.Fori(0, NG) as g:
                    G = g + NG * run
                    pe.wait_ge(fr.lo, g + NG * phase + 1)
                    pe.wait_ge(h8.ctx, G + 1)
                    for u in range(8):
                        if u >= 6:
                            pe.wait_ge(h8.lo, 8 * G + u - 5)
                        cols = slice(4 * (u % 4), 4 * (u % 4) + 4)
                        if u < 4:
                            o_ = ps[:, u % 6, :]
                            wt = tuple(w_[:, cols, :, :].rearrange("p h r d -> p (h r d)") for w_ in wq)
                            split3(o_, wt, xT, stop=False)
                            pe.matmul(o_, bq2[:, cols, :, :].rearrange("p h r d -> p (h r d)"), ones2[:, :],
                                      start=False, stop=True).then_inc(h8.mm, 1)
                        else:
                            wt = tuple(w_[0:DC + 1, cols, :, :].rearrange("p h r d -> p (h r d)") for w_ in wk)
                            split3(ps[:, u % 6, 0:GB * SP], wt,
                                   tuple(c_[0:DC + 1, :, :].rearrange("p b t -> p (b t)") for c_ in (chi, clo)))\
                                .then_inc(h8.mm, 1)
                    front(g + NG * phase + 1)
                    for b in range(GB):
                        ins = split3(ps[0:SK, 6, b * P:b * P + P], tuple(c_[0:DC + 1, b, 0:SK] for c_ in (chi, clo)),
                                     tuple(w_[0:DC + 1, :] for w_ in wv))
                    ins.then_inc(h8.v_mm, 1)
                    pe.wait_ge(h8.lo, 8 * G + 8)
                    pe.wait_ge(h8.v, G + 1)

                    def scores(b, u):
                        if u == 0:
                            pe.wait_ge(h8.kbd, 4 * G + b + 1)
                        return pe.matmul(ps[:, u % 2, 0:HG * SP], q[:, u, b, :],
                                         kbd[b % 2][:, u, :, :].rearrange("p h t -> p (h t)"), start=True, stop=True)

                    def values(b):
                        for h in range(H):
                            ins = pe.matmul(ps[:, 6, 0:P], v8[:, (b * H + h) * P:(b * H + h + 1) * P],
                                            prob[:, h // 4, (h % 4) * P:(h % 4) * P + P],
                                            start=(h == 0), stop=(h == H - 1))
                        ins.then_inc(h8.o, 1)

                    def project(b):
                        pe.wait_ge(h8.oT, 4 * G + b + 1)
                        pe.matmul(ps[:, 6, 0:P], oT8[:, :], wo[:, :], start=True, stop=False)
                        pe.matmul(ps[:, 6, 0:P], const[0:1, C_ONE:C_ONE + P], bo[:, :], start=False, stop=True)\
                            .then_inc(h8.y, 1)

                    attend(h8, G, scores, values, project)

            def mix_rows(s_c, s_ct_mm, s_ct, s_b_mm, G, between):
                pe.wait_ge(s_c, G + 1)
                pe.transpose(ps[0:GB * E, 6, 0:P], cw[:, :, :].rearrange("p t e -> p (t e)"), idn).then_inc(s_ct_mm, 1)
                between()
                pe.wait_ge(s_ct, G + 1)
                pe.matmul(ps[:, 6, :], cT[:, :], b2m[:, :, :].rearrange("p t d -> p (t d)"), start=True, stop=True)\
                    .then_inc(s_b_mm, 1)

            def experts(run, phase):
                wait_done(pe, "h1" if run else "h8", 1)
                if run:
                    pe.wait_ge(ld.r, 16 * 19)
                else:
                    pe.wait_ge(ff.w_ss, 2)
                for j in range(1 if run else 2):
                    ins = pe.transpose(ps[:, 6, 8 * j:8 * j + E], emb[:, 2 * j, :], const[0:E, C_ID:C_ID + E])
                ins.then_inc(ff.w_mm, 1)
                pe.wait_ge(ff.w, run + 1)
                if run:
                    pe.wait_ge(h1.big, 8)
                else:
                    pe.wait_ge(wr.big, 8)
                with pe.Fori(0, NG) as g:
                    G = g + NG * run
                    pe.wait_ge(fr.lo, g + NG * phase + 1)
                    n = E if run else 2 * E
                    for t in range(GB):
                        ins = split3(ps[:, 6, t * 16:t * 16 + n], tokens(xT, t), tuple(w_[:, 0:n] for w_ in rwt))
                    ins.then_inc(ff.r, 1)

                    def up(e):
                        for c in range(NC_HID):
                            u = e * NC_HID + c
                            if u >= 4:
                                pe.wait_ge(ff.act, 32 * G + u - 3)
                            split3(ps[:, u % 4, :],
                                   tuple(w_[:, e // 2, (u % 8) * P:(u % 8) * P + P] for w_ in wb), xT)\
                                .then_inc(ff.h, 1)

                    def down(e):
                        pe.wait_ge(ff.split, 32 * G + 4 * e + 4)
                        if e >= 2:
                            pe.wait_ge(ff.x, 8 * G + e - 1)
                        for t in range(GB):
                            o_ = ps[:, 4 + e % 2, t * P:t * P + P]
                            for c in range(NC_HID):
                                hh = hhi[e % 2][:, c, t * P:t * P + P]
                                hl = hlo[e % 2][:, c, t * P:t * P + P]
                                w_ = [z[:, 4 + e // 2, (4 * (e % 2) + c) * P:(4 * (e % 2) + c) * P + P] for z in wb]
                                pe.matmul(o_, hh, w_[0], start=(c == 0), stop=False)
                                pe.matmul(o_, hh, w_[1], start=False, stop=False)
                                ins = pe.matmul(o_, hl, w_[0], start=False, stop=(c == NC_HID - 1))
                        ins.then_inc(ff.o, 1)

                    up(0)
                    mix_rows(ff.c, ff.ct_mm, ff.ct, ff.b_mm, G, lambda: up(1))
                    down(0)
                    for e in range(2, E):
                        up(e)
                        if e < E - 1:
                            down(e - 1)
                    front(g + NG * phase + 1)
                    down(E - 2)
                    down(E - 1)

            def heads64():
                wait_done(pe, "ff", 1)
                pe.wait_ge(ld.l1, 32)
                pe.wait_ge(wr.l1, 4)
                with pe.Fori(0, NG) as g:
                    pe.wait_ge(fr.lo, g + 2 * NG + 1)
                    pe.wait_ge(h64.ctx, g + 1)
                    ct = tuple(c_[0:DC, :, :].rearrange("p b t -> p (b t)") for c_ in (chi, clo))
                    for c in range(C1):
                        if c >= 4:
                            pe.wait_ge(h64.q, 8 * g + c - 3)
                        split3(ps[:, c % 4, :], tuple(w_[:, 0, c * P:c * P + P] for w_ in l1w), xT).then_inc(h64.qmm, 1)
                        if c >= 2:
                            pe.wait_ge(h64.k, 8 * g + c - 1)
                        split3(ps[:, 4 + c % 2, 0:GB * SP], tuple(w_[0:DC, 1, c * P:c * P + P] for w_ in l1w), ct)\
                            .then_inc(h64.kmm, 1)
                    front(g + 2 * NG + 1)
                    for i in range(2 * GB):
                        if i < 4:
                            pe.wait_ge(h64.q, 8 * g + 5 + i)
                        else:
                            pe.wait_ge(h64.v, 8 * g + i - 3)
                        split3(ps[0:SK, i % 4, :], tuple(c_[0:DC, i // 2, 0:SK] for c_ in (chi, clo)),
                               tuple(w_[0:DC, 2, 512 * (i % 2):512 * (i % 2) + 512] for w_ in l1w)).then_inc(h64.vmm, 1)
                    pe.wait_ge(h64.k, 8 * g + 8)
                    pe.wait_ge(h64.v, 8 * g + 8)
                    pe.wait_ge(fr.lo, g + 2 * NG + 2)

                    def scores(b, u):
                        half, par = u // 2, u % 2
                        for i in range(4):
                            c = 4 * half + i
                            ins = pe.matmul(ps[:, par, i * SP:i * SP + SK],
                                            q1[64 * par:64 * par + 64, c, b * P:b * P + P],
                                            k1[64 * par:64 * par + 64, c, b, 0:SK], start=True, stop=True)
                        return ins

                    def values(b):
                        for c in range(C1):
                            for par in range(2):
                                ins = pe.matmul(ps[64 * par:64 * par + 64, 6 + c // 4, (c % 4) * P:(c % 4) * P + P],
                                                v1[:, b, 2 * c + par, :],
                                                prob[:, 2 * (c // 4) + par, (c % 4) * P:(c % 4) * P + P],
                                                start=True, stop=True)
                            if c % 4 == 3:
                                ins.then_inc(h64.o, 1)

                    def project(b):
                        pe.wait_ge(h64.oT, 2 * (4 * g + b) + 2)
                        for c in range(C1):
                            pe.matmul(ps[:, 6, 0:P], oT[:, c, :], wo1[:, c, :], start=(c == 0), stop=False)
                        pe.matmul(ps[:, 6, 0:P], const[0:1, C_ONE:C_ONE + P], bo[:, :], start=False, stop=True)\
                            .then_inc(h64.y, 1)

                    attend(h64, g, scores, values, project)

            def mixed():
                wait_done(pe, "h64", 1)
                pe.wait_ge(mx.w, 1)
                with pe.Fori(0, NG) as g:
                    pe.wait_ge(fr.lo, g + 3 * NG + 1)
                    for t in range(GB):
                        ins = split3(ps[:, 6, t * 16:t * 16 + E], tokens(xT, t), tuple(w_[:, 0:E] for w_ in rwt))
                    ins.then_inc(mx.r, 1)

                    def half_(i):
                        for t in range(GB):
                            if i:
                                pe.wait_ge(mx.half, 8 * g + t + 1)
                            split3(ps[:, t, :], tokens(xT, t),
                                   tuple(w_[:, 3, 512 * i:512 * i + 512] for w_ in l1w)).then_inc(mx.o, 1)

                    mix_rows(mx.c, mx.ct_mm, mx.ct, mx.b_mm, g, lambda: half_(0))
                    half_(1)
                    front(g + 3 * NG + 1)

            def head128():
                wait_done(pe, "mx", 1)
                pe.wait_ge(h1.w, 1)
                pe.wait_ge(su.scratch, 2)
                with pe.Fori(0, NG) as g:
                    pe.wait_ge(fr.lo, g + 4 * NG + 1)
                    pe.wait_ge(h1.ctx, g + 1)
                    split3(ps[:, 0, :], tuple(w_[:, 0, :] for w_ in w2), xT, stop=False)
                    pe.matmul(ps[:, 0, :], b_bq2[:, :], ones2[:, :], start=False, stop=True).then_inc(h1.qmm, 1)
                    split3(ps[:, 1, 0:GB * SP], tuple(w_[0:DC + 1, 1, :] for w_ in w2),
                           tuple(c_[0:DC + 1, :, :].rearrange("p b t -> p (b t)") for c_ in (chi, clo)))\
                        .then_inc(h1.kmm, 1)
                    for b in range(GB):
                        ins = split3(ps[0:SK, 2, b * P:b * P + P], tuple(c_[0:DC + 1, b, 0:SK] for c_ in (chi, clo)),
                                     tuple(w_[0:DC + 1, 2, :] for w_ in w2))
                    ins.then_inc(h1.vmm, 1)
                    front(g + 4 * NG + 1)
                    pe.wait_ge(h1.q, g + 1)
                    pe.wait_ge(h1.k, g + 1)
                    for b in range(GB):
                        ins = split3(ps[:, 3, b * SP:b * SP + SP], tokens([q_[:, :] for q_ in q2], b),
                                     tuple(k_[:, b, :] for k_ in k2))
                    ins.then_inc(h1.s, 1)
                    pe.wait_ge(h1.max, g + 1)
                    pe.transpose(ps[0:GB, 4, 0:P], nm2[:, :], idn).then_inc(h1.t, 1)
                    pe.wait_ge(h1.nT, g + 1)
                    for b in range(GB):
                        o_ = ps[0:SK, 5, b * P:b * P + P]
                        split3(o_, tuple(k_[:, b, 0:SK] for k_ in k2), tokens([q_[:, :] for q_ in q2], b), stop=False)
                        ins = pe.matmul(o_, const[0:GB, C_SELB + b * SK:C_SELB + b * SK + SK], nT2[:, :],
                                        start=False, stop=True)
                    ins.then_inc(h1.st, 1)
                    pe.wait_ge(h1.exp, g + 1)
                    pe.wait_ge(h1.v, g + 1)
                    for b in range(GB):
                        ins = pe.matmul(ps[:, (6, 0)[b // 2], (b % 2) * (D + 1):(b % 2 + 1) * (D + 1)],
                                        prob[:, 0, b * P:b * P + P], v2[:, b, :], start=True, stop=True)
                        if b % 2:
                            ins.then_inc(h1.o, 1)

            def ternary():
                wait_done(pe, "h8", 2)
                pe.wait_ge(tn.sum, 1)
                pe.matmul(ps[:, 2, 0:2], const[:, C_ONE:C_ONE + P], ta[:, 8:10], start=True, stop=True)\
                    .then_inc(tn.gamma, 1)
                pe.wait_ge(tn.w, 1)
                for j, w_ in enumerate((wfr, wpr)):
                    for c in range(4):
                        ins = pe.transpose(ps[:, j, c * P:c * P + P], w_[:, c, :], idn)
                    ins.then_inc(tn.wT_mm, 1)
                pe.wait_ge(tn.wT, 2)
                with pe.Fori(0, NG) as g:
                    pe.wait_ge(fr.lo, g + 7 * NG + 1)
                    for t in range(GB):
                        w_ = wf[:, :, :].rearrange("p c h -> p (c h)")
                        pe.matmul(ps[:, t, :], xhi[:, t * P:t * P + P], w_, start=True, stop=False)
                        pe.matmul(ps[:, t, :], xlo[:, t * P:t * P + P], w_, start=False, stop=True).then_inc(tn.h, 1)
                    front(g + 7 * NG + 1)
                    for t in range(GB + 1):
                        if t < GB:
                            pe.wait_ge(tn.norm, 4 * g + t + 1)
                            if t >= 2:
                                pe.wait_ge(tn.t, 4 * g + t - 1)
                            for c in range(NC_HID):
                                ins = pe.transpose(ps[:, 4 + t % 2, c * P:c * P + P], hg[:, t, c * P:c * P + P], idn)
                            ins.then_inc(tn.t_mm, 1)
                        if t >= 1:
                            pe.wait_ge(tn.t, 4 * g + t)
                            for c in range(NC_HID):
                                ins = pe.matmul(ps[:, 6, (t - 1) * P:t * P], hgT[:, (t - 1) % 2, c, :], wp[:, c, :],
                                                start=(c == 0), stop=(c == NC_HID - 1))
                    ins.then_inc(tn.y, 1)

            pe.wait_ge(ld.const, 16)
            pe.wait_ge(ld.ctx, 16)
            for b in range(B):
                ins = pe.transpose(ps[0:DC, b // 4, (b % 4) * SP:(b % 4) * SP + SK], ctok[:, b, :],
                                   const[0:SK, C_ID:C_ID + SK])
            ins.then_inc(su.pe, 1)
            front(0)
            pe.wait_ge(su.dve, 4)
            pe.wait_ge(su.zero, 9)
            heads8(0, 0)
            experts(0, 1)
            heads64()
            mixed()
            head128()
            experts(1, 5)
            heads8(1, 6)
            ternary()

        @block.vector
        def _(dve):
            def over(ap, n=E):
                return ap.unsqueeze(2).to_broadcast([P, GB, n])

            def along(col, n=E):
                return const[:, col:col + n].unsqueeze(1).to_broadcast([P, GB, n])

            def group(t_, g, w=1):
                return t_[:, bass.ds(g, w), :]

            def variance(lk, s_, n, mean, var):
                lk.wait()
                lk.mark(dve.tensor_tensor(fs[:, 0, :], s_[:, :, 1], s_[:, :, 4], ALU.add))
                lk.mark(dve.tensor_tensor(fs[:, 1, :], s_[:, :, 1], s_[:, :, 4], ALU.subtract))
                lk.mark(dve.tensor_tensor(fs[:, 2, :], s_[:, :, 2], s_[:, :, 5], ALU.add))
                lk.wait()
                lk.mark(dve.tensor_scalar(mean, fs[:, 0, :], 0.5, None, ALU.mult))
                lk.mark(dve.tensor_tensor(fs[:, 3, :], fs[:, 1, :], fs[:, 1, :], ALU.mult))
                lk.mark(dve.tensor_scalar(fs[:, 4, :], fs[:, 2, :], 1.0 / n, None, ALU.mult))
                lk.wait()
                lk.link(dve.scalar_tensor_tensor(out=var, in0=fs[:, 3, :], scalar=0.25, in1=fs[:, 4, :],
                                                 op0=ALU.mult, op1=ALU.add))

            def front_a(gn, n):
                lk = Link(dve, fr.link, 11, n)
                for t in range(GB):
                    lk.mark(dve.bn_stats(st[:, t, :], x[:, bass.ds(gn * GB + t, 1), :].rearrange("p o d -> p (o d)")))
                variance(lk, st, D, mv[:, :, 0], mv[:, :, 1])
                dve.tensor_scalar(vv[:, :], mv[:, :, 1], const[:, bass.ds(n + C_NA, 1)], const[:, bass.ds(n + C_NB, 1)],
                                  ALU.mult, ALU.add).then_inc(fr.var, 1)
                lk.end()

            def front_b(gn, n):
                dve.wait_ge(fr.rstd, n + 1)
                for t in range(GB):
                    ins = dve.tensor_scalar(xn[:, t, :], x[:, bass.ds(gn * GB + t, 1), :].rearrange("p o d -> p (o d)"),
                                            mv[:, t, 0:1], rstd[:, t:t + 1], ALU.subtract, ALU.mult)
                ins.then_inc(fr.xn, 1)

            def front_c(n):
                dve.wait_ge(fr.hi, n + 1)
                dve.tensor_tensor(xlo[:, :], ps[:, 7, :], f32(xhi[:, :]), ALU.subtract).then_inc(fr.lo, 1)

            def stage(lk, g, rows, s_):
                c_ = ctxT[0:rows, bass.ds(g * GB, GB), :]
                lk.mark(dve.tensor_copy(chi[0:rows, :, :], c_))
                lk.wait()
                dve.tensor_tensor(clo[0:rows, :, :], c_, f32(chi[0:rows, :, :]), ALU.subtract).then_inc(s_, 1)

            sl = Link(dve, su.vlink, 0)

            def add_to_x(tile_, w, in_, scalar, s_):
                xt = x[:, bass.ds(tile_, w), :].rearrange("p o d -> p (o d)")
                dve.scalar_tensor_tensor(out=xt, in0=in_, scalar=scalar, in1=xt, op0=ALU.mult, op1=ALU.add).then_inc(s_, 1)

            def attend(hs, lk, G, add):
                for i in range(GB + 2):
                    if i < GB:
                        n = 4 * (4 * G + i)
                        for pair in range(2):
                            for u in (2 * pair, 2 * pair + 1):
                                dve.wait_ge(hs.s, n + u + 1)
                                s_ = ps[:, u % 2, 0:4 * SP].rearrange("p (h t) -> p h t", h=4)[:, :, 0:SK]
                                dve.tensor_reduce(top_s[:, 4 * u:4 * u + 4].unsqueeze(2), s_, AX.X, ALU.max)\
                                   .then_inc(hs.max, 1)
                            for u in (2 * pair, 2 * pair + 1):
                                s_ = ps[:, u % 2, 0:4 * SP].rearrange("p (h t) -> p h t", h=4)[:, :, 0:SK]
                                dve.wait_ge(hs.max, n + u + 1)
                                dve.tensor_tensor(sh[i % 2][:, u, :, :], s_,
                                                  top_s[:, 4 * u:4 * u + 4].unsqueeze(2).to_broadcast([P, 4, SK]),
                                                  ALU.subtract).then_inc(hs.sub, 1)
                            if pair == 0 and i >= 2:
                                add(i - 2)
                        for half in range(2):
                            dve.wait_ge(hs.exp, n + 2 * half + 2)
                            e_ = sh[i % 2][:, 2 * half:2 * half + 2, :, :].rearrange("p u h t -> p (u h) t")
                            dve.tensor_reduce(den[:, 8 * half:8 * half + 8].unsqueeze(2), e_, AX.X, ALU.add)\
                               .then_inc(hs.den, 1)
                            dve.wait_ge(hs.den, 2 * (4 * G + i) + half + 1)
                            dve.reciprocal(rd[i % 2][:, 8 * half:8 * half + 8], den[:, 8 * half:8 * half + 8])\
                               .then_inc(hs.rden, 1)
                    else:
                        add(i - 2)

            def heads8_weights(run):
                def rep(ap, rows):
                    return ap[0:rows, :].rearrange("p (h d) -> p h d", h=H).unsqueeze(2).to_broadcast([rows, H, 3, D8])
                dve.wait_ge(ld.a, 16 * N_A * (run + 1))
                dve.wait_ge(su.zero, 9)
                K1 = DC + 1
                sl.mark(dve.tensor_copy(wq[0][:, :, 0:3, :], rep(a_raw[:, 0, :], P)))
                sl.mark(dve.tensor_copy(wk[0][0:K1, :, 0:3, :], rep(a_raw[:, 1, :], K1)))
                sl.mark(dve.tensor_copy(wv[0][0:K1, :], a_raw[0:K1, 2, :]))
                sl.mark(dve.tensor_copy(bq2[:, :, 0:3, :], rep(a_bq[:, :], 64)))
                sl.mark(dve.tensor_copy(wo[:, :], a_raw[:, 3, :]))
                sl.mark(dve.tensor_copy(bo[:, :], a_bo[:, :]))
                sl.wait()
                dve.tensor_tensor(wq[1][:, :, 0:3, :], rep(a_raw[:, 0, :], P), f32(wq[0][:, :, 0:3, :]), ALU.subtract)
                dve.tensor_tensor(wk[1][0:K1, :, 0:3, :], rep(a_raw[:, 1, :], K1), f32(wk[0][0:K1, :, 0:3, :]),
                                  ALU.subtract)
                dve.tensor_tensor(wv[1][0:K1, :], a_raw[0:K1, 2, :], f32(wv[0][0:K1, :]), ALU.subtract)
                dve.tensor_tensor(bq2[32:64, :, 0:3, :], rep(a_bq[:, :], 64)[32:64], f32(bq2[32:64, :, 0:3, :]),
                                  ALU.subtract).then_inc(h8.w, 1)

            def heads8(run, phase):
                layer = 3 * run
                heads8_weights(run)
                with dve.Fori(0, NG) as g:
                    G = g + NG * run
                    n = g + NG * phase + 1
                    gn = next_group(g)
                    lk = Link(dve, h8.link, 1, G)
                    stage(lk, g, DC + 1, h8.ctx)
                    front_a(gn, n)
                    for u in range(8):
                        dve.wait_ge(h8.hi, 8 * G + u + 1)
                        t_, m, w = (q, C_MQ, GT) if u < 4 else (k, C_MK, GB * SP)
                        t_ = t_[:, u % 4, :, :].rearrange("p b t -> p (b t)")
                        dve.scalar_tensor_tensor(out=t_, in0=ps[:, u % 6, 0:w], scalar=const[:, m:m + 1], in1=f32(t_),
                                                 op0=ALU.mult, op1=ALU.add).then_inc(h8.lo, 1)
                        if u == 3:
                            front_b(gn, n)
                    front_c(n)

                    def add(b):
                        dve.wait_ge(h8.y, 4 * G + b + 1)
                        add_to_x(g * GB + b, 1, ps[:, 6, 0:P], tg[:, 0, layer:layer + 1], h8.x)

                    attend(h8, lk, G, add)
                    lk.end()

            def second_biases(s_):
                dve.tensor_tensor(b2m[:, :, :], b2rep[:, :].unsqueeze(1).to_broadcast([GB * E, GB, D]),
                                  const[0:GB * E, C_TM:C_TM + GB].unsqueeze(2).to_broadcast([GB * E, GB, D]),
                                  ALU.mult).then_inc(s_, 1)

            def split_small(hi, lo, src):
                sl.link(dve.tensor_copy(hi, src))
                return dve.tensor_tensor(lo, src, f32(hi), ALU.subtract)

            def first_best(lk, s_, best, hit, tie, one):
                lk.link(dve.tensor_reduce(best, s_, AX.X, ALU.max))
                lk.link(dve.tensor_tensor(hit, s_, over(best), ALU.is_equal))
                lk.link(dve.tensor_tensor(hit, hit, along(C_DOWN), ALU.mult))
                lk.link(dve.tensor_reduce(tie, hit, AX.X, ALU.max))
                lk.link(dve.tensor_tensor(one, hit, over(tie), ALU.is_equal))

            def route_top2(lk, G, gate):
                R = [rt[:, i, :, :] for i in range(12)]
                S = [rs[:, i, :] for i in range(12)]
                dve.wait_ge(ff.rn, G + 1)
                lk.link(dve.tensor_scalar(S[4], S[1], 1e-8, None, ALU.add))
                lk.link(dve.reciprocal(S[5], S[4]))
                dve.wait_ge(ff.r, G + 1)
                o_ = ps[:, 6, 0:GB * 16].rearrange("p (t e) -> p t e", e=16)
                lk.mark(dve.tensor_tensor(R[0], o_[:, :, E:2 * E], over(S[5]), ALU.mult))
                lk.mark(dve.tensor_copy(R[2], o_[:, :, 0:E]))
                lk.wait()
                lk.mark(dve.tensor_tensor(R[1], R[0], rowb[:, :].unsqueeze(1).to_broadcast([P, GB, E]), ALU.add))
                lk.link(dve.tensor_reduce(S[6], R[2], AX.X, ALU.min))
                lk.link(dve.tensor_tensor(R[3], R[2], over(S[6]), ALU.is_equal))
                lk.link(dve.tensor_tensor(R[4], R[3], along(C_UP), ALU.mult))
                lk.link(dve.tensor_reduce(S[7], R[4], AX.X, ALU.max))
                lk.link(dve.tensor_tensor(R[5], R[4], over(S[7]), ALU.is_equal))
                lk.link(dve.scalar_tensor_tensor(out=R[6], in0=R[5], scalar=-1e30, in1=R[1], op0=ALU.mult, op1=ALU.add))
                first_best(lk, R[6], S[10], R[7], S[11], R[9])
                lk.link(dve.scalar_tensor_tensor(out=R[10], in0=R[9], scalar=-3e30, in1=R[6], op0=ALU.mult, op1=ALU.add))
                first_best(lk, R[10], S[6], R[3], S[7], R[11])
                dve.tensor_tensor(S[8], S[6], S[10], ALU.subtract).then_inc(ff.d, 1)
                dve.wait_ge(ff.tanh, G + 1)
                lk.mark(dve.tensor_scalar(S[2], S[9], 0.5, 0.5, ALU.mult, ALU.add))
                lk.link(dve.tensor_scalar(S[3], S[9], -0.5, 0.5, ALU.mult, ALU.add))
                lk.mark(dve.tensor_tensor(R[7], R[9], over(S[3]), ALU.mult))
                lk.link(dve.tensor_tensor(R[8], R[11], over(S[2]), ALU.mult))
                lk.link(dve.tensor_tensor(R[0], R[7], R[8], ALU.add))
                dve.tensor_scalar(cw[:, :, :], R[0], gate, None, ALU.mult).then_inc(ff.c, 1)

            def route_top1(lk, G, gate):
                R = [rt[:, i, :, :] for i in range(12)]
                S = [rs[:, i, :] for i in range(12)]
                dve.wait_ge(ff.r, G + 1)
                o_ = ps[:, 6, 0:GB * 16].rearrange("p (t e) -> p t e", e=16)
                lk.link(dve.tensor_copy(R[0], o_[:, :, 0:E]))
                first_best(lk, R[0], S[0], R[1], S[1], R[5])
                dve.tensor_tensor(R[2], R[0], over(S[0]), ALU.subtract).then_inc(ff.d, 1)
                dve.wait_ge(ff.tanh, G + 1)
                lk.mark(dve.tensor_scalar(R[6], R[3], 1.0, None, ALU.add))
                lk.link(dve.tensor_scalar(R[7], R[3], -1.0, 1.0, ALU.mult, ALU.add))
                lk.link(dve.reciprocal(R[8], R[7]))
                lk.link(dve.tensor_tensor(R[9], R[6], R[8], ALU.mult))
                lk.link(dve.tensor_reduce(S[2], R[9], AX.X, ALU.add))
                lk.link(dve.reciprocal(S[3], S[2]))
                lk.link(dve.tensor_tensor(R[10], R[5], over(S[3]), ALU.mult))
                dve.tensor_scalar(cw[:, :, :], R[10], gate, None, ALU.mult).then_inc(ff.c, 1)

            def experts(run, phase):
                layer = 2 * run
                LK2, LK1 = 60, 45
                gate = tg[:, 1, layer:layer + 1]
                dve.wait_ge(ld.r, 16 * (19 if run else 7))
                n_ = E if run else 2 * E
                if not run:
                    sl.link(dve.tensor_tensor(emb[:, 1, :], emb[:, 0, :], emb[:, 0, :], ALU.mult))
                    dve.tensor_reduce(emb_s[:, 0:1], emb[:, 1, :], AX.X, ALU.add).then_inc(ff.w_ss, 1)
                    dve.wait_ge(ff.w_rt, 1)
                    sl.link(dve.tensor_scalar(emb_s[:, 2:3], emb_s[:, 1:2], 1e-8, None, ALU.add))
                    sl.link(dve.reciprocal(emb_s[:, 3:4], emb_s[:, 2:3]))
                    dve.tensor_scalar(emb[:, 2, :], emb[:, 0, :], emb_s[:, 3:4], None, ALU.mult).then_inc(ff.w_ss, 1)
                    sl.link(dve.tensor_scalar(rowb[:, :], rowb[:, :], 0.1, None, ALU.mult))
                dve.wait_ge(ff.w_mm, run + 1)
                if run:
                    sl.link(dve.tensor_scalar(rraw[:, 0:n_], ps[:, 6, 0:n_], rmsw[:, 0:1], None, ALU.mult))
                else:
                    sl.link(dve.tensor_copy(rraw[:, 0:n_], ps[:, 6, 0:n_]))
                split_small(rwt[0][:, 0:n_], rwt[1][:, 0:n_], rraw[:, 0:n_])
                second_biases(ff.w)
                with dve.Fori(0, NG) as g:
                    G = g + NG * run
                    n = g + NG * phase + 1
                    gn = next_group(g)
                    lk = Link(dve, (ff.link, ff.link1)[run], (LK2, LK1)[run], g)
                    if not run:
                        lk.link(dve.tensor_tensor(rs[:, 2, :], mv[:, :, 1], rstd[:, :], ALU.mult))
                        dve.scalar_tensor_tensor(out=rs[:, 0, :], in0=rs[:, 2, :], scalar=float(D), in1=rstd[:, :],
                                                 op0=ALU.mult, op1=ALU.mult).then_inc(ff.nn, 1)
                    front_a(gn, n)
                    (route_top1 if run else route_top2)(lk, G, gate)

                    def split(e):
                        if e >= 2:
                            dve.wait_ge(ff.o, 8 * G + e - 1)
                        for c in range(NC_HID + 1):
                            u = NC_HID * e + c
                            if c < NC_HID:
                                dve.wait_ge(ff.act, 32 * G + u + 1)
                                lk.mark(dve.tensor_copy(hhi[e % 2][:, c, :], hf[:, u % 4, :]))
                            if c:
                                lk.wait(back=1 if c < NC_HID else 0)
                                dve.tensor_tensor(hlo[e % 2][:, c - 1, :], hf[:, (u - 1) % 4, :],
                                                  f32(hhi[e % 2][:, c - 1, :]), ALU.subtract).then_inc(ff.split, 1)

                    def add(e):
                        dve.wait_ge(ff.o, 8 * G + e + 1)
                        if e:
                            dve.wait_ge(ff.x, 8 * G + e)
                        else:
                            dve.wait_ge(ff.xb, G + 1)
                        for t in range(GB):
                            xt = x[:, bass.ds(g * GB + t, 1), :].rearrange("p o d -> p (o d)")
                            ins = dve.scalar_tensor_tensor(out=xt, in0=ps[:, 4 + e % 2, t * P:t * P + P],
                                                           scalar=cw[:, t, e:e + 1], in1=xt, op0=ALU.mult, op1=ALU.add)
                        ins.then_inc(ff.x, 1)

                    split(0)
                    dve.wait_ge(ff.ct_mm, G + 1)
                    dve.tensor_copy(cT[:, :], ps[0:GB * E, 6, 0:P]).then_inc(ff.ct, 1)
                    split(1)
                    add_rows(g, ff.b_mm, G, ff.xb)
                    front_b(gn, n)
                    add(0)
                    for e in range(2, E):
                        split(e)
                        if e == E - 1:
                            front_c(n)
                        add(e - 1)
                    add(E - 1)
                    lk.end()

            def add_rows(g, s_mm, G, s_):
                dve.wait_ge(s_mm, G + 1)
                xt = x[:, bass.ds(g * GB, GB), :].rearrange("p t d -> p (t d)")
                dve.tensor_tensor(xt, xt, ps[:, 6, :], ALU.add).then_inc(s_, 1)

            def heads64():
                with dve.Fori(0, NG) as g:
                    n = g + 2 * NG + 1
                    gn = next_group(g)
                    lk = Link(dve, h64.link, 1, g)
                    stage(lk, g, DC, h64.ctx)
                    front_a(gn, n)
                    for c in range(C1):
                        dve.wait_ge(h64.kmm, 8 * g + c + 1)
                        dve.tensor_copy(k1[:, c, :, :].rearrange("p b t -> p (b t)"), ps[:, 4 + c % 2, 0:GB * SP])\
                           .then_inc(h64.k, 1)
                        if c == 1:
                            front_b(gn, n)
                    front_c(n)

                    def add(b):
                        dve.wait_ge(h64.y, 4 * g + b + 1)
                        add_to_x(g * GB + b, 1, ps[:, 6, 0:P], tg[:, 0, 1:2], h64.x)

                    attend(h64, lk, g, add)
                    lk.end()

            def mixed():
                dve.wait_ge(ld.r, 16 * 13)
                split_small(rwt[0][:, 0:E], rwt[1][:, 0:E], rraw[:, 0:E])
                second_biases(mx.w)
                R = [rt[:, i, :, :] for i in range(12)]
                S = [rs[:, i, :] for i in range(12)]
                with dve.Fori(0, NG) as g:
                    n = g + 3 * NG + 1
                    gn = next_group(g)
                    lk = Link(dve, mx.link, 36, g)
                    front_a(gn, n)
                    dve.wait_ge(mx.r, g + 1)
                    o_ = ps[:, 6, 0:GB * 16].rearrange("p (t e) -> p t e", e=16)[:, :, 0:E]
                    lk.link(dve.tensor_tensor(R[0], o_, rowb[:, :].unsqueeze(1).to_broadcast([P, GB, E]), ALU.add))
                    lk.link(dve.tensor_reduce(S[0], R[0], AX.X, ALU.max))
                    dve.tensor_tensor(R[2], R[0], over(S[0]), ALU.subtract).then_inc(mx.d, 1)
                    front_b(gn, n)
                    dve.wait_ge(mx.e, g + 1)
                    lk.link(dve.tensor_reduce(S[1], R[3], AX.X, ALU.add))
                    lk.link(dve.reciprocal(S[2], S[1]))
                    lk.link(dve.tensor_tensor(R[4], R[3], over(S[2]), ALU.mult))
                    lk.link(dve.tensor_scalar(R[5], R[4], 0.1, None, ALU.is_ge))
                    lk.link(dve.tensor_tensor(R[6], R[4], R[5], ALU.mult))
                    lk.link(dve.tensor_reduce(S[3], R[6], AX.X, ALU.add))
                    lk.link(dve.tensor_scalar(S[4], S[3], 0.0, None, ALU.is_equal))
                    lk.link(dve.tensor_tensor(S[5], S[3], S[4], ALU.add))
                    lk.link(dve.reciprocal(S[6], S[5]))
                    lk.link(dve.tensor_tensor(R[7], R[6], over(S[6]), ALU.mult))
                    dve.tensor_scalar(cw[:, :, :], R[7], tg[:, 1, 1:2], None, ALU.mult).then_inc(mx.c, 1)
                    dve.wait_ge(mx.ct_mm, g + 1)
                    dve.tensor_copy(cT[:, :], ps[0:GB * E, 6, 0:P]).then_inc(mx.ct, 1)
                    add_rows(g, mx.b_mm, g, mx.xb)
                    for i in range(2):
                        for e in range(4):
                            for t in range(GB):
                                if e == 0:
                                    dve.wait_ge(mx.o, 8 * g + 4 * i + t + 1)
                                    if i:
                                        dve.wait_ge(mx.half, 8 * g + t + 1)
                                    else:
                                        dve.wait_ge(mx.xb, g + 1)
                                else:
                                    lk.wait(back=3 - t if e == 3 else 3)
                                xt = x[:, bass.ds(g * GB + t, 1), :].rearrange("p o d -> p (o d)")
                                ins = dve.scalar_tensor_tensor(out=xt, in0=ps[:, t, e * P:e * P + P],
                                                               scalar=cw[:, t, 4 * i + e:4 * i + e + 1], in1=xt,
                                                               op0=ALU.mult, op1=ALU.add)
                                if e < 3:
                                    lk.mark(ins)
                                else:
                                    ins.then_inc(mx.half, 1)
                    front_c(n)
                    lk.end()

            def head128():
                dve.wait_ge(ld.b, 16 * 8)
                K1 = DC + 1
                sl.mark(dve.tensor_copy(w2[0][:, 0, :], b_raw[:, 0, :]))
                sl.mark(dve.tensor_copy(w2[0][0:K1, 1:3, :], b_raw[0:K1, 1:3, :]))
                sl.mark(dve.tensor_copy(b_bq2[:, :], b_bq[:, :]))
                sl.link(dve.memset(scal[:, :], 1.0))
                sl.mark(dve.tensor_copy(scal[:, 0:4], rmsw[:, 0:1].to_broadcast([P, 4])))
                dve.tensor_tensor(w2[1][:, 0, :], b_raw[:, 0, :], f32(w2[0][:, 0, :]), ALU.subtract)
                dve.tensor_tensor(w2[1][0:K1, 1:3, :], b_raw[0:K1, 1:3, :], f32(w2[0][0:K1, 1:3, :]), ALU.subtract)
                dve.tensor_tensor(b_bq2[32:64, :], b_bq[32:64, :], f32(b_bq2[32:64, :]), ALU.subtract).then_inc(h1.w, 1)
                sl.wait()
                with dve.Fori(0, NG) as g:
                    n = g + 4 * NG + 1
                    gn = next_group(g)
                    lk = Link(dve, h1.link, 8, g)
                    stage(lk, g, K1, h1.ctx)
                    front_a(gn, n)
                    dve.wait_ge(h1.qhi, g + 1)
                    dve.tensor_tensor(q2[1][:, :], ps[:, 0, :], f32(q2[0][:, :]), ALU.subtract).then_inc(h1.q, 1)
                    dve.wait_ge(h1.khi, g + 1)
                    dve.tensor_tensor(k2[1][:, :, :].rearrange("p b t -> p (b t)"), ps[:, 1, 0:GB * SP],
                                      f32(k2[0][:, :, :]).rearrange("p b t -> p (b t)"), ALU.subtract).then_inc(h1.k, 1)
                    front_b(gn, n)
                    dve.wait_ge(h1.s, g + 1)
                    dve.tensor_reduce(nm2[:, :].unsqueeze(2),
                                      ps[:, 3, 0:GB * SP].rearrange("p (b t) -> p b t", b=GB)[:, :, 0:SK],
                                      AX.X, ALU.max, negate=True).then_inc(h1.max, 1)
                    dve.wait_ge(h1.t, g + 1)
                    dve.tensor_copy(nT2[:, :], ps[0:GB, 4, 0:P]).then_inc(h1.nT, 1)
                    front_c(n)
                    for b in range(2):
                        i = g * 2 + b
                        hi, lo = (t_[:, bass.ds(i, 1), :].rearrange("p o n -> p (o n)") for t_ in wb)
                        dve.wait_ge((ld.raw0, ld.raw1)[b], 16 * (g + NG + 1))
                        lk.link(dve.tensor_scalar(raw[b][:, :], raw[b][:, :], scal[:, bass.ds(i, 1)], None, ALU.mult))
                        lk.link(dve.tensor_scalar(hi, raw[b][:, :], 1.0, None, ALU.mult))
                        dve.tensor_tensor(lo, raw[b][:, :], f32(hi), ALU.subtract).then_inc(h1.big, 1)
                    for i in range(2):
                        dve.wait_ge(h1.o, 2 * g + i + 1)
                        lk.mark(dve.reciprocal(rden[:, 2 * i:2 * i + 2].unsqueeze(2),
                                               ps[:, (6, 0)[i], 0:2 * (D + 1)].rearrange("p (b d) -> p b d", b=2)[:, :, D:D + 1]))
                    lk.wait()
                    lk.link(dve.tensor_scalar(rden[:, 4:8], rden[:, 0:4], tg[:, 0, 2:3], None, ALU.mult))
                    for b in range(GB):
                        xt = x[:, bass.ds(g * GB + b, 1), :].rearrange("p o d -> p (o d)")
                        o_ = ps[:, (6, 0)[b // 2], (b % 2) * (D + 1):(b % 2) * (D + 1) + D]
                        ins = dve.scalar_tensor_tensor(out=xt, in0=o_, scalar=rden[:, 4 + b:5 + b], in1=xt,
                                                       op0=ALU.mult, op1=ALU.add)
                    ins.then_inc(h1.x, 1)
                    lk.end()

            def ternary():
                dve.wait_ge(ld.l3, 64)
                for j, w_ in enumerate((wfr, wpr)):
                    ins = dve.tensor_reduce(ta[:, 8 + j:9 + j], w_[:, :, :].rearrange("p c d -> p (c d)"), AX.X, ALU.add,
                                            apply_absolute_value=True)
                ins.then_inc(tn.sum, 1)
                dve.wait_ge(tn.gamma, 1)
                sl.link(dve.tensor_scalar(ta[:, 10:12], ps[:, 2, 0:2], 1.0 / (HID * D), 1e-6, ALU.mult, ALU.add))
                sl.mark(dve.tensor_scalar(ta[:, 12:14], ta[:, 10:12], 0.5, None, ALU.mult))
                sl.link(dve.tensor_scalar(ta[:, 14:16], ta[:, 10:12], -0.5, None, ALU.mult))
                for j, w_ in enumerate((wfr, wpr)):
                    wv_ = w_[:, :, :].rearrange("p c d -> p (c d)")
                    sl.link(dve.tensor_scalar(hg[:, j, :], wv_, ta[:, 14 + j:15 + j], None, ALU.is_lt))
                    ins = dve.scalar_tensor_tensor(out=wv_, in0=wv_, scalar=ta[:, 12 + j:13 + j], in1=hg[:, j, :],
                                                   op0=ALU.is_gt, op1=ALU.subtract)
                ins.then_inc(tn.w, 1)
                dve.wait_ge(tn.wT_mm, 1)
                dve.tensor_copy(wf[:, :, :].rearrange("p c h -> p (c h)"), ps[:, 0, :]).then_inc(tn.wT, 1)
                dve.wait_ge(tn.wT_mm, 2)
                dve.tensor_copy(wp[:, :, :].rearrange("p c h -> p (c h)"), ps[:, 1, :]).then_inc(tn.wT, 1)
                with dve.Fori(0, NG) as g:
                    n = g + 7 * NG + 1
                    gn = next_group(g)
                    lk = Link(dve, tn.link, 11, g)
                    front_a(gn, n)
                    front_b(gn, n)
                    for t in range(GB):
                        dve.wait_ge(tn.act, 4 * g + t + 1)
                        lk.mark(dve.bn_stats(st[:, t, :], hg[:, t, :]))
                    variance(lk, st, HID, mh[:, 0, :], mh[:, 1, :])
                    dve.tensor_scalar(ta[:, 0:4], mh[:, 1, :], 1e-5, None, ALU.add).then_inc(tn.var, 1)
                    dve.wait_ge(tn.rstd, g + 1)
                    for t in range(GB):
                        dve.tensor_scalar(hg[:, t, :], hg[:, t, :], mh[:, 0, t:t + 1], ta[:, 4 + t:5 + t],
                                          ALU.subtract, ALU.mult).then_inc(tn.norm, 1)
                    front_c(n)
                    dve.wait_ge(tn.y, g + 1)
                    add_to_x(g * GB, GB, ps[:, 6, :], tg[:, 1, 3:4], tn.x)
                    lk.end()

            dve.wait_ge(ld.const, 16)
            dve.wait_ge(ld.x, 16)
            front_a(0, 0)
            front_b(0, 0)
            dve.wait_ge(su.zero, 4)
            dve.wait_ge(su.pe, 1)
            for i in range(4):
                o_ = ps[0:DC, i, 0:GB * SP].rearrange("p (b t) -> p b t", b=GB)[:, :, 0:SK]
                dve.tensor_copy(ctxT[0:DC, GB * i:GB * i + GB, 0:SK], o_).then_inc(su.dve, 1)
            front_c(0)
            dve.wait_ge(su.dve, 4)
            dve.wait_ge(ld.xrest, 16)
            dve.wait_ge(su.tanh, 1)
            heads8(0, 0)
            experts(0, 1)
            heads64()
            mixed()
            head128()
            experts(1, 5)
            heads8(1, 6)
            ternary()


_PASS = ["x", "ctx_768", "g_xattn", "g_ffn",
         "L0_xattn_wq", "L0_xattn_bq", "L0_xattn_wk", "L0_xattn_bk", "L0_xattn_wv", "L0_xattn_bv", "L0_xattn_wo",
         "L0_xattn_bo", "L0_ffn_uzman_embeddings", "L0_ffn_W1", "L0_ffn_b1", "L0_ffn_W2", "L0_ffn_b2",
         "L0_ffn_onbellek_durumu", "L1_xattn_Wq", "L1_xattn_Wk", "L1_xattn_Wv", "L1_xattn_Wo", "L1_xattn_bo",
         "L1_ffn_gate_w", "L1_ffn_gate_b", "L1_ffn_expert_w", "L1_ffn_expert_b", "L2_xattn_Wq", "L2_xattn_bq",
         "L2_xattn_Wk", "L2_xattn_bk", "L2_xattn_Wv", "L2_xattn_bv", "L2_ffn_rms_w", "L2_ffn_gate_w", "L2_ffn_W1",
         "L2_ffn_b1", "L2_ffn_W2", "L2_ffn_b2", "L3_xattn_Wq", "L3_xattn_bq", "L3_xattn_Wk", "L3_xattn_bk",
         "L3_xattn_Wv", "L3_xattn_bv", "L3_xattn_Wo", "L3_xattn_bo", "L3_ffn_W_fc", "L3_ffn_ln_w", "L3_ffn_ln_b",
         "L3_ffn_W_proj"]


def kernel(**inputs):
    import concourse.bacc as bacc
    import concourse.bass_utils as bass_utils

    nc = bacc.Bacc("TRN2", target_bir_lowering=False, num_devices=1)
    arrays, args = {}, {}
    given = {n: np.ascontiguousarray(inputs[n]) for n in _PASS}
    for n, src in (("L0_b1", "L0_ffn_b1"), ("L2_b1", "L2_ffn_b1"), ("ln_w", "L3_ffn_ln_w"), ("ln_b", "L3_ffn_ln_b")):
        given[n] = np.ascontiguousarray(np.asarray(inputs[src]).reshape(-1, P).T)
    given["const"] = constants()
    for n, v in given.items():
        arrays[f"in_{n}"] = v
        args[n] = nc.dram_tensor(f"in_{n}", v.shape, mybir.dt.from_np(v.dtype), kind="ExternalInput").ap()
    o = nc.dram_tensor("out_0", (B, P, D), F32, kind="ExternalOutput").ap()
    build(nc, args, o)
    r = bass_utils.run_bass_kernel_spmd(nc, [arrays], core_ids=[0])
    return r.results[0]["out_0"]
```

```python
from contextlib import ExitStack

import concourse.bass as bass
import numpy as np
from concourse import mybir

F32 = mybir.dt.float32
F32R = mybir.dt.float32r
ALU = mybir.AluOpType
ACT = mybir.ActivationFunctionType
AX = mybir.AxisListType

P = 128
B = 16
D = 128
SK = 77
SP = 78
DC = 96
GB = 4
NG = B // GB
GT = GB * P
H = 16
D8 = 8
HG = 4
D64 = 64
INNER = H * D64
C1 = INNER // P
E = 8
HID = 512
NC_HID = HID // P
WCH = 2048

DVE_HI = (0, 2)

BANKS8 = (0, 1, 2, 3, 4, 5, 2, 3)

C_ID = 0
C_CQ, C_MQ, C_CK, C_MK = 128, 129, 130, 131
C_MASK = 132
C_NA = 136
C_NB = C_NA + 33
C_UP = C_NB + 33
C_DOWN = C_UP + E
C_HALF = C_DOWN + E
C_TM = C_HALF + GB
C_ONE = C_TM + GB
C_PLUS = C_ONE + P
C_SELB = C_PLUS + GB
NCONST = C_SELB + GB * SK


def constants():
    c = np.zeros((P, NCONST), np.float32)
    c[:, C_ID:C_ID + P] = np.eye(P)
    role = (np.arange(P) % 32) // D8
    c[:, C_CQ] = np.where(role == 1, -1, 1)
    c[:, C_MQ] = role == 1
    c[:, C_CK] = np.where(role == 2, -1, 1)
    c[:, C_MK] = role == 2
    for j in range(HG):
        c[32 * j:32 * j + 32, C_MASK + j] = 1
    c[:, C_NA:C_NA + 33] = 1.0
    c[:, C_NB:C_NB + 33] = 1e-5
    c[:, C_NA + 20:C_NA + 24] = 1.0 + 1e-6
    c[:, C_NB + 20:C_NB + 24] = 1e-11
    c[:, C_UP:C_UP + E] = np.arange(1, E + 1)
    c[:, C_DOWN:C_DOWN + E] = np.arange(E, 0, -1)
    c[:, C_HALF:C_HALF + GB] = -0.5
    for t in range(GB):
        c[E * t:E * t + E, C_TM + t] = 1
        c[t, C_SELB + t * SK:C_SELB + t * SK + SK] = 1
    c[:, C_ONE:C_ONE + P] = 1
    c[:, C_PLUS:C_PLUS + GB] = 0.5
    return c


def build(nc, a, out):
    ctx = ExitStack()
    with ctx:
        def sem(name):
            return ctx.enter_context(nc.semaphore(name))

        def sems(prefix, *names):
            return type(prefix, (), {n: sem(f"{prefix}_{n}") for n in names})

        ps = ctx.enter_context(nc.psum_tensor("banks", [P, 8, 512], F32))

        top = [(nc.sbuf_base + 63) // 64 * 64]

        def place(name, shape, dt=F32, at=None):
            size = int(np.prod(shape[1:])) * 4
            offset = top[0] if at is None else at[0]
            t = nc.alloc_sbuf_tensor_at(name, shape, dt, offset=offset)
            size = (size + 63) // 64 * 64
            if at is None:
                top[0] += size
            else:
                at[0] += size
                at[1] = max(at[1], at[0])
            return t

        const = place("const", [P, NCONST])
        x = place("x", [P, B, D])
        xn = place("xn", [P, GB, D])
        xhi = place("xhi", [P, GT], F32R)
        xlo = place("xlo", [P, GT], F32R)
        ctxT = place("ctxT", [P, B, SP])
        chi = place("chi", [P, GB, SP], F32R)
        clo = place("clo", [P, GB, SP], F32R)
        tg = place("tg", [P, 2, 4])
        st = place("st", [P, GB, 6])
        mv = place("mv", [P, GB, 2])
        vv = place("vv", [P, GB])
        rstd = place("rstd", [P, GB])
        fs = place("fs", [P, 5, GB])
        mh = place("mh", [P, 2, GB])
        scal = place("scal", [P, 8])
        ones2 = place("ones2", [64, GT], F32R)
        idn = const[:, C_ID:C_ID + P]

        a_raw = place("a_raw", [P, 4, P])
        a_bq = place("a_bq", [64, P])
        a_bo = place("a_bo", [1, P])
        wq = [place("wq_hi", [P, H, 4, D8], F32R), place("wq_lo", [P, H, 4, D8], F32R)]
        wk = [place("wk_hi", [P, H, 4, D8], F32R), place("wk_lo", [P, H, 4, D8], F32R)]
        wv = [place("wv_hi", [P, P], F32R), place("wv_lo", [P, P], F32R)]
        wo = place("wo", [P, P])
        bo = place("bo", [1, P])
        bq2 = place("bq2", [64, H, 4, D8], F32R)
        b_raw = place("b_raw", [P, 3, P])
        w2 = [place("w2_hi", [P, 3, P], F32R), place("w2_lo", [P, 3, P], F32R)]
        b_bq = place("b_bq", [64, P])
        b_bq2 = place("b_bq2", [64, P], F32R)
        rraw = place("rraw", [P, 16])
        rwt = [place("rw_hi", [P, 16], F32R), place("rw_lo", [P, 16], F32R)]
        emb = place("emb", [E, 3, D])
        emb_s = place("emb_s", [E, 4])
        rowb = place("rowb", [P, E])
        b2rep = place("b2rep", [GB * E, D])
        b2m_at = [top[0], top[0]]
        b2m = place("b2m", [GB * E, GB, D])
        b1 = place("b1", [P, E * NC_HID])
        rmsw = place("rmsw", [P, 1])
        cw = place("cw", [P, GB, E])
        cT = place("cT", [GB * E, P])
        cwT = [nc.alloc_sbuf_tensor_at("cwT_hi", [E, GT], F32R, offset=b2m_at[0]), place("cwT_lo", [E, GT], F32R)]
        sel = place("sel", [E, E], F32R)
        b2T = place("b2T", [P, E])
        rt = place("rt", [P, 12, GB, E])
        rs = place("rs", [P, 12, GB])
        raw = [place("raw0", [P, WCH // 2])]
        xf = nc.alloc_sbuf_tensor_at("xf", [P, GT], F32, offset=top[0])
        raw.append(place("raw1", [P, WCH // 2]))
        lregion = [top[0], top[0]]
        l1w = [place("l1w_hi", [P, 4, INNER], F32R, lregion), place("l1w_lo", [P, 4, INNER], F32R, lregion)]
        lend = lregion[1]
        lregion = [top[0], lend]
        v8 = place("v8", [P, GB * H * P + P], F32, lregion)
        top[0] = lregion[1]

        wregion = [top[0], top[0]]
        wb = [place("wb_hi", [P, 8, WCH // 2], F32R, wregion), place("wb_lo", [P, 8, WCH // 2], F32R, wregion)]
        wend = wregion[1]
        wregion = [top[0], wend]
        wo1 = place("wo1", [P, C1, D], F32, wregion)
        q1 = place("q1", [P, C1, GT], F32, wregion)
        k1 = place("k1", [P, C1, GB, 2, SP], F32, wregion)
        v1 = place("v1", [P, GB, H, D64], F32, wregion)
        assert wregion[0] <= wend
        wregion = [top[0], wend]
        wf = place("wf", [P, 4, P], F32R, wregion)
        wp = place("wp", [P, 4, P], F32, wregion)
        wfr = place("wfr", [P, 4, P], F32, wregion)
        wpr = place("wpr", [P, 4, P], F32, wregion)
        lnw = place("lnw", [P, 4], F32, wregion)
        lnb = place("lnb", [P, 4], F32, wregion)
        ta = place("ta", [P, 16], F32, wregion)
        top[0] = wend

        rden = place("rden", [P, H])
        s0 = top[0]
        s = [s0, s0]
        prob = place("prob", [P, 4, 512], F32, s)
        sh = [place("sh0", [P, 4, 4, SK], F32, s), place("sh1", [P, 4, 4, SK], F32, s)]
        top_s = place("top_s", [P, H], F32, s)
        den = place("den", [P, H], F32, s)
        rd = [place("rd0", [P, H], F32, s), place("rd1", [P, H], F32, s)]
        sa = s[0]
        ctok = place("ctok", [SK, B, DC], F32, s)
        s = [sa, s[1]]
        q = place("q", [P, HG, GB, P], F32R, s)
        k = place("k", [P, HG, GB, SP], F32R, s)
        kbd = [place("kbd0", [P, HG, HG, SP], F32R, s), place("kbd1", [P, HG, HG, SP], F32R, s)]
        oT8 = place("oT8", [P, P], F32, s)
        s = [sa, s[1]]
        oT = place("oT", [P, C1, P], F32, s)
        s = [sa, s[1]]
        q2 = [[place(f"q2_{part}{i}", [P, GT], F32R, s) for part in ("hi", "lo")] for i in range(2)]
        k2 = [[place(f"k2_{part}{i}", [P, GB, SP], F32R, s) for part in ("hi", "lo")] for i in range(2)]
        v2 = [place(f"v2_{i}", [SK, GB, D + 1], F32, s) for i in range(2)]
        nm2 = place("nm2", [P, GB], F32, s)
        nT2 = place("nT2", [GB, P], F32, s)
        s = [s0, s[1]]
        hf = place("hf", [P, 4, 512], F32, s)
        acc = place("acc", [P, GT], F32, s)
        yw = [place("yw0", [P, GT], F32, s), place("yw1", [P, GT], F32, s)]
        hhi = [place("hhi0", [P, 4, 512], F32R, s), place("hhi1", [P, 4, 512], F32R, s)]
        hlo = [place("hlo0", [P, 4, 512], F32R, s), place("hlo1", [P, 4, 512], F32R, s)]
        s = [s0, s[1]]
        hg = [place("hg0", [P, GB, HID], F32, s), place("hg1", [P, GB, HID], F32, s)]
        hgT = place("hgT", [P, 2, 4, P], F32, s)
        assert s[1] <= nc.sbuf_usable_end, (s[1], nc.sbuf_usable_end)

        ld = sems("loaded", "const", "x", "xrest", "ctx", "gate", "a", "r", "raw0", "raw1", "l1raw", "l1", "b", "l3")
        su = sems("setup", "braw", "zero", "dve", "tanh", "pe", "scratch", "plink", "vlink", "hi")
        fr = sems("front", "link", "var", "rstd", "xn", "xt", "hi", "lo")
        h8 = sems("heads8", "w", "ctx", "mm", "hi", "lo", "v_mm", "v", "kbd", "s", "max", "sub", "exp", "den", "rden",
                  "prob", "t", "pT", "o", "oT", "y", "x", "link")
        ff = sems("experts", "w_mm", "w_ss", "w_rt", "w", "r", "read", "read_hi", "xf", "sq", "nn", "rn", "d", "tanh", "c", "ct_mm", "ct",
                  "h", "act", "hi", "split", "o", "y", "yw", "acc", "sum", "x", "link", "link1", "link2", "link3")
        h64 = sems("heads64", "ctx", "qmm", "kmm", "vmm", "q", "k", "v", "s", "max", "sub", "exp", "den", "rden",
                   "prob", "t", "pT", "o", "oT", "y", "x", "link")
        h1 = sems("head128", "w", "ctx", "qmm", "qhi", "q", "kmm", "khi", "k", "vmm", "v", "s", "max", "t", "nT",
                  "st", "exp", "o", "x", "big", "link", "link2")
        mx = sems("mixed", "w", "r", "d", "e", "c", "ct_mm", "ct", "b_mm", "xb", "o", "half", "x", "link", "link2")
        tn = sems("ternary", "sum", "gamma", "w", "wT_mm", "wT", "h", "act", "var", "rstd", "norm", "t_mm", "t",
                  "y", "x", "link")
        wr = sems("split", "big", "l1")
        stored = sem("stored")

        block = ctx.enter_context(nc.Block())

        def row(ap):
            return ap.rearrange("(o n) -> o n", o=1)

        def f32(ap):
            return ap.bitcast(F32)

        def done(kind):
            return {"h8": (h8.x, B), "ff": (ff.x, NG), "h64": (h64.x, B), "mx": (mx.half, 8 * NG),
                    "h1": (h1.x, NG), "tn": (tn.x, NG)}[kind]

        def wait_done(eng, kind, runs):
            s_, n_ = done(kind)
            eng.wait_ge(s_, n_ * runs)

        def next_group(g):
            return (g + 1) % NG

        class Link:

            def __init__(self, eng, s_, per, step=0):
                self.eng, self.sem, self.per, self.step, self.n = eng, s_, per, step, 0

            def mark(self, ins):
                self.n += 1
                ins.then_inc(self.sem, 1)

            def wait(self, back=0):
                assert self.n > back
                self.eng.wait_ge(self.sem, self.step * self.per + self.n - back)

            def link(self, ins):
                self.mark(ins)
                self.wait()

            def end(self):
                assert self.n == self.per, (self.n, self.per)

        N_A = 9

        @block.sync
        def _(sp):
            def load_heads8(layer):
                n = f"L{layer}_xattn_"
                c = "w" if layer == 0 else "W"
                sp.dma_start(a_raw[:, 0, :], a[n + c + "q"]).then_inc(ld.a, 16)
                sp.dma_start(a_raw[0:DC, 1, :], a[n + c + "k"]).then_inc(ld.a, 16)
                sp.dma_start(a_raw[DC:DC + 1, 1, :], row(a[n + "bk"])).then_inc(ld.a, 16)
                sp.dma_start(a_raw[0:DC, 2, :], a[n + c + "v"]).then_inc(ld.a, 16)
                sp.dma_start(a_raw[DC:DC + 1, 2, :], row(a[n + "bv"])).then_inc(ld.a, 16)
                sp.dma_start(a_raw[:, 3, :], a[n + c + "o"]).then_inc(ld.a, 16)
                sp.dma_start(a_bq[0:1, :], row(a[n + "bq"])).then_inc(ld.a, 16)
                sp.dma_start(a_bq[32:33, :], row(a[n + "bq"])).then_inc(ld.a, 16)
                sp.dma_start(a_bo[:, :], row(a[n + "bo"])).then_inc(ld.a, 16)

            def load_experts(layer, i):
                w1 = a[f"L{layer}_ffn_W1"].rearrange("e d h -> d e h")
                w2 = a[f"L{layer}_ffn_W2"].rearrange("e (c p) d -> p (e c) d", p=P)
                src = w1[:, 2 * i:2 * i + 2, :] if i < 4 else w2[:, 8 * i - 32:8 * i - 24, :]
                n = 2 if i < 4 else 8
                sp.dma_start(raw[i % 2][:, :].rearrange("p (e h) -> p e h", e=n), src)\
                  .then_inc((ld.raw0, ld.raw1)[i % 2], 16)

            sp.dma_start(const[:, :], a["const"]).then_inc(ld.const, 16)
            xd = a["x"].rearrange("b t d -> t b d")
            sp.dma_start(x[:, 0:GB, :], xd[:, 0:GB, :]).then_inc(ld.x, 16)
            sp.dma_start(ctok[:, :, :], a["ctx_768"].rearrange("b s d -> s b d")).then_inc(ld.ctx, 16)
            sp.wait_ge(su.braw, 1)
            load_heads8(0)
            sp.dma_start(x[:, GB:B, :], xd[:, GB:B, :]).then_inc(ld.xrest, 16)
            sp.dma_start(tg[:, 0, :], row(a["g_xattn"]).to_broadcast([P, 4])).then_inc(ld.gate, 16)
            sp.dma_start(tg[:, 1, :], row(a["g_ffn"]).to_broadcast([P, 4])).then_inc(ld.gate, 16)
            sp.dma_start(emb[:, 0, :], a["L0_ffn_uzman_embeddings"]).then_inc(ld.r, 16)
            sp.dma_start(rowb[:, :], row(a["L0_ffn_onbellek_durumu"]).to_broadcast([P, E])).then_inc(ld.r, 16)
            sp.dma_start(b1[:, :], a["L0_b1"]).then_inc(ld.r, 16)
            sp.dma_start(b2T[:, :], a["L0_b2"]).then_inc(ld.r, 16)
            for i in range(8):
                if i >= 2:
                    sp.wait_ge(wr.big, i - 1)
                load_experts(0, i)
            sp.wait_ge(wr.big, 7)
            sp.dma_start(raw[0][:, :], a["L1_xattn_Wq"]).then_inc(ld.l1raw, 16)
            for i, n in enumerate(("L1_xattn_Wk", "L1_xattn_Wv")):
                sp.wait_ge(wr.l1, i + 1)
                sp.dma_start(raw[0][0:DC, :], a[n]).then_inc(ld.l1raw, 16)
            sp.wait_ge(wr.l1, 3)
            sp.dma_start(raw[0][:, :].rearrange("p (e h) -> p e h", e=E),
                         a["L1_ffn_expert_w"].rearrange("e d h -> d e h")).then_inc(ld.l1raw, 16)
            wait_done(sp, "ff", 1)
            sp.dma_start(wo1[:, :, :], a["L1_xattn_Wo"].rearrange("(c p) d -> p c d", p=P)).then_inc(ld.l1, 16)
            sp.dma_start(bo[:, :], row(a["L1_xattn_bo"])).then_inc(ld.l1, 16)
            sp.dma_start(rraw[:, 0:E], a["L1_ffn_gate_w"]).then_inc(ld.r, 16)
            sp.dma_start(rowb[:, :], row(a["L1_ffn_gate_b"]).to_broadcast([P, E])).then_inc(ld.r, 16)
            for t in range(GB):
                sp.dma_start(b2rep[E * t:E * t + E, :], a["L1_ffn_expert_b"]).then_inc(ld.r, 16)
            sp.dma_start(b_raw[:, 0, :], a["L2_xattn_Wq"]).then_inc(ld.b, 16)
            for j, n in ((1, "k"), (2, "v")):
                sp.dma_start(b_raw[0:DC, j, :], a["L2_xattn_W" + n]).then_inc(ld.b, 16)
                sp.dma_start(b_raw[DC:DC + 1, j, :], row(a["L2_xattn_b" + n])).then_inc(ld.b, 16)
            sp.dma_start(b_bq[0:1, :], row(a["L2_xattn_bq"])).then_inc(ld.b, 16)
            sp.dma_start(b_bq[32:33, :], row(a["L2_xattn_bq"])).then_inc(ld.b, 16)
            load_heads8(3)
            sp.dma_start(rmsw[:, :], a["L2_ffn_rms_w"].rearrange("(p o) -> p o", o=1)).then_inc(ld.b, 16)
            sp.wait_ge(wr.l1, 4)
            for i in range(8):
                if i >= 2:
                    sp.wait_ge(h1.big, i - 1)
                if i == 2:
                    wait_done(sp, "mx", 1)
                    sp.dma_start(emb[:, 0, :], a["L2_ffn_gate_w"]).then_inc(ld.r, 16)
                    sp.dma_start(b1[:, :], a["L2_b1"]).then_inc(ld.r, 16)
                    sp.dma_start(b2T[:, :], a["L2_b2"]).then_inc(ld.r, 16)
                load_experts(2, i)
            wait_done(sp, "ff", 2)
            sp.dma_start(wfr[:, :, :], a["L3_ffn_W_fc"].rearrange("(c p) d -> p c d", p=P)).then_inc(ld.l3, 16)
            sp.dma_start(wpr[:, :, :], a["L3_ffn_W_proj"].rearrange("d (c p) -> d c p", p=P)).then_inc(ld.l3, 16)
            sp.dma_start(lnw[:, :], a["ln_w"]).then_inc(ld.l3, 16)
            sp.dma_start(lnb[:, :], a["ln_b"]).then_inc(ld.l3, 16)
            od = out.rearrange("b t d -> t b d")
            for g in range(NG):
                sp.wait_ge(tn.x, g + 1)
                sp.dma_start(od[:, GB * g:GB * g + GB, :], x[:, GB * g:GB * g + GB, :]).then_inc(stored, 16)
            sp.wait_ge(stored, 16 * NG)

        @block.gpsimd
        def _(pool):
            def rsqrt_front(n):
                pool.wait_ge(fr.var, n + 1)
                pool.tensor_tensor(rstd[:, :], vv[:, :], const[:, C_HALF:C_HALF + GB], ALU.pow).then_inc(fr.rstd, 1)

            def split_chunk(src, rows, hi, lo, links, done_, count):
                pool.tensor_copy(hi, src).then_inc(su.plink, 1)
                pool.wait_ge(su.plink, links)
                pool.tensor_tensor(lo, src, f32(hi), ALU.subtract).then_inc(done_, 1)

            def keys(G, b):
                if b == 0:
                    pool.wait_ge(h8.lo, 8 * G + 4)
                if b >= 2:
                    pool.wait_ge(h8.s, 4 * (4 * G + b - 1))
                kb = f32(k[:, :, b, :]).unsqueeze(2).to_broadcast([P, HG, HG, SP])
                m = const[:, C_MASK:C_MASK + HG].unsqueeze(1).unsqueeze(3).to_broadcast([P, HG, HG, SP])
                pool.tensor_tensor(kbd[b % 2][:, :, :, :], kb, m, ALU.mult).then_inc(h8.kbd, 1)

            def normalise(hs, G, b):
                for half in range(2):
                    pool.wait_ge(hs.rden, 2 * (4 * G + b) + half + 1)
                    e_ = sh[b % 2][:, 2 * half:2 * half + 2, :, :].rearrange("p u h t -> p (u h) t")
                    r_ = rd[b % 2][:, 8 * half:8 * half + 8].unsqueeze(2).to_broadcast([P, 8, SK])
                    pool.tensor_tensor(e_, e_, r_, ALU.mult).then_inc(hs.prob, 1)

            def prob_scratch():
                pool.memset(prob[:, :, :], 0.0).then_inc(su.scratch, 1)

            def values_scratch():
                pool.memset(v8[:, :], 0.0).then_inc(su.scratch, 1)

            pool.memset(a_bq[:, :], 0.0).then_inc(su.braw, 1)
            pool.memset(b_bq[:, :], 0.0).then_inc(su.zero, 1)
            pool.memset(ctxT[0:DC, :, SK:SP], 0.0).then_inc(su.zero, 1)
            pool.wait_ge(su.zero, 2)
            pool.memset(ctxT[DC:DC + 1, :, :], 1.0).then_inc(su.zero, 1)
            pool.wait_ge(su.zero, 3)
            for t in (*wq, *wk):
                pool.memset(f32(t[:, :, :, :]), 0.0).then_inc(su.zero, 1)
            pool.memset(f32(bq2[:, :, :, :]), 0.0).then_inc(su.zero, 1)
            pool.memset(f32(ones2[:, :]), 1.0).then_inc(su.zero, 1)
            pool.wait_ge(ld.const, 16)
            rsqrt_front(0)
            prob_scratch()
            values_scratch()
            for g in range(NG):
                rsqrt_front(g + 1)
                keys(g, 0)
                for b in range(GB):
                    if b < GB - 1:
                        keys(g, b + 1)
                    normalise(h8, g, b)
                    if b < 2:
                        i = 2 * g + b
                        pool.wait_ge(su.hi, i + 1)
                        pool.tensor_tensor(wb[1][:, i, :], raw[b][:, :], f32(wb[0][:, i, :]), ALU.subtract)\
                            .then_inc(wr.big, 1)
            pool.wait_ge(ff.w_ss, 1)
            pool.tensor_tensor(emb_s[:, 1:2], emb_s[:, 0:1], const[0:E, C_PLUS:C_PLUS + 1], ALU.pow).then_inc(ff.w_rt, 1)
            def lengths(n):
                pool.wait_ge(ff.nn, n + 1)
                pool.tensor_tensor(rs[:, 1, :], rs[:, 0, :], const[:, C_PLUS:C_PLUS + GB], ALU.pow).then_inc(ff.rn, 1)

            def gather(G, experts_):
                for e in experts_:
                    pool.wait_ge(ff.yw, 8 * G + e + 1)
                    if e > 1:
                        pool.wait_ge(ff.acc, 7 * G + e - 1)
                    pool.tensor_tensor(acc[:, :], acc[:, :], yw[e % 2][:, :], ALU.add).then_inc(ff.acc, 1)

            lengths(0)
            for g in range(NG):
                rows = DC if g in (1, 2) else P
                pool.wait_ge(ld.l1raw, 16 * (g + 1))
                split_chunk(raw[0][0:rows, :], rows, l1w[0][0:rows, g, :], l1w[1][0:rows, g, :], g + 1, wr.l1, g + 1)
                rsqrt_front(NG + g + 1)
                gather(g, (1,))
                lengths(g + 1)
                gather(g, (2, 3, 4, 5, 6, 7))
            wait_done(pool, "ff", 1)
            pool.memset(k1[:, :, :, :, :], 0.0).then_inc(su.scratch, 1)
            for g in range(NG):
                rsqrt_front(g + 2 * NG + 1)
                if g == 0:
                    prob_scratch()
                    pool.memset(v1[:, :, :, :], 0.0).then_inc(su.scratch, 1)
                for b in range(GB):
                    normalise(h64, g, b)
            with pool.Fori(0, NG) as g:
                rsqrt_front(g + 3 * NG + 1)
            wait_done(pool, "mx", 1)
            for i in range(2):
                ins = pool.memset(v2[i][:, :, D:D + 1], 1.0)
            ins.then_inc(su.scratch, 1)
            values_scratch()
            with pool.Fori(0, NG) as g:
                rsqrt_front(g + 4 * NG + 1)
            with pool.Fori(0, NG) as g:
                rsqrt_front(g + 5 * NG + 1)
                gather(g + NG, range(1, E))
            wait_done(pool, "ff", 2)
            prob_scratch()
            with pool.Fori(0, NG) as g:
                rsqrt_front(g + 6 * NG + 1)
                keys(g + NG, 0)
                for b in range(GB):
                    if b < GB - 1:
                        keys(g + NG, b + 1)
                    normalise(h8, g + NG, b)
            for g in range(NG):
                if g < NG - 1:
                    rsqrt_front(g + 7 * NG + 1)
                pool.wait_ge(tn.var, g + 1)
                pool.tensor_tensor(ta[:, 4:8], ta[:, 0:4], const[:, C_HALF:C_HALF + GB], ALU.pow).then_inc(tn.rstd, 1)

        @block.scalar
        def _(act):
            def copy(o_, i_, **kw):
                return act.activation(o_, i_, ACT.Copy, **kw)

            def front(n):
                act.wait_ge(fr.xt, n + 1)
                copy(xhi[:, :], ps[:, 7, :]).then_inc(fr.hi, 1)

            def attend(hs, G, scale, outputs, own_values, chunk=None):
                def exps(i, units):
                    for u in units:
                        act.wait_ge(hs.sub, 4 * (4 * G + i) + u + 1)
                        e_ = sh[i % 2][:, u, :, :].rearrange("p h t -> p (h t)")
                        act.activation(e_, e_, ACT.Exp, scale=scale).then_inc(hs.exp, 1)

                for i in range(GB + 2):
                    if i >= 2:
                        outputs(G, i - 2)
                    if i < GB:
                        exps(i, (0, 1))
                    if i == 0:
                        own_values(G, 0)
                    if 1 <= i <= GB:
                        for u in range(4):
                            act.wait_ge(hs.t, 4 * (4 * G + i - 1) + u + 1)
                            copy(prob[0:SK, u, :], ps[0:SK, 2 + u, :]).then_inc(hs.pT, 1)
                    if i < GB:
                        if i < 2 and chunk:
                            act.wait_ge((ld.raw0, ld.raw1)[i], 16 * (G + 1))
                        exps(i, (2, 3))
                        if i < 2 and chunk:
                            chunk(G, i)
                    if i == 0:
                        own_values(G, 1)

            def heads8(run, phase):
                def prepare(g):
                    G = g + NG * run
                    for u in range(8):
                        act.wait_ge(h8.mm, 8 * G + u + 1)
                        bank = ps[:, BANKS8[u], :]
                        if u >= 4:
                            copy(q[:, u - 4, :, :].rearrange("p b t -> p (b t)"), bank,
                                 scale=const[:, C_CQ:C_CQ + 1]).then_inc(h8.hi, 1)
                        else:
                            copy(k[:, u, :, :].rearrange("p b t -> p (b t)"), bank[:, 0:GB * SP],
                                 scale=const[:, C_CK:C_CK + 1]).then_inc(h8.hi, 1)
                    front(g + NG * phase + 1)

                def own_values(G, part):
                    if part:
                        return
                    act.wait_ge(h8.v_mm, G + 1)
                    for b in range(GB):
                        blocks = v8[:, b * H * P:b * H * P + H * (P + D8)].rearrange("p (h w) -> p h w", w=P + D8)
                        ins = copy(blocks[0:SK, :, 0:D8],
                                   ps[0:SK, 6, b * P:b * P + P].rearrange("p (h d) -> p h d", h=H))
                    ins.then_inc(h8.v, 1)

                def outputs(G, b):
                    act.wait_ge(h8.o, 4 * G + b + 1)
                    copy(oT8[:, :], ps[:, 6, 0:P]).then_inc(h8.oT, 1)

                def chunk(g, b):
                    hi = wb[0][:, bass.ds(g * 2 + b, 1), :].rearrange("p o n -> p (o n)")
                    copy(hi, raw[b][:, :]).then_inc(su.hi, 1)

                chunk_ = None if run else chunk
                prepare(0)
                with act.Fori(0, NG - 1) as g:
                    attend(h8, g + NG * run, D8 ** -0.5, outputs, own_values, chunk_)
                    prepare(g + 1)
                attend(h8, NG - 1 + NG * run, D8 ** -0.5, outputs, own_values, chunk_)

            def experts(run, phase, func):
                def tanh(n):
                    act.wait_ge(ff.d, n + 1)
                    t_ = (rt[:, 3, :, :], rt[:, 2, :, :]) if run else (rs[:, 9, :], rs[:, 8, :])
                    act.activation(t_[0], t_[1], ACT.Tanh, scale=0.5).then_inc(ff.tanh, 1)

                def hidden(G, e):
                    for c in range(NC_HID):
                        u = e * NC_HID + c
                        act.wait_ge(ff.h, 32 * G + u + 1)
                        if c not in DVE_HI:
                            act.activation(hhi[e % 2][:, c, :], ps[:, u % 4, :], func, bias=b1[:, u:u + 1])
                        if e or not isinstance(G, int):
                            act.wait_ge(ff.split, 32 * G + u - 3)
                        act.activation(hf[:, u % 4, :], ps[:, u % 4, :], func, bias=b1[:, u:u + 1])\
                           .then_inc(ff.act, 1)

                def output(G, e):
                    act.wait_ge(ff.o, 8 * G + e + 1)
                    if e >= 3:
                        act.wait_ge(ff.acc, 7 * G + e - 2)
                    act.activation(yw[e % 2][:, :] if e else acc[:, :], ps[:, 4 + e % 2, :], ACT.Identity,
                                   bias=b2T[:, e:e + 1]).then_inc(ff.y, 1)

                def group(g, last):
                    G = g + NG * run
                    for e in range(1, E):
                        if e >= 2:
                            output(G, e - 2)
                        if e == 6:
                            act.wait_ge(fr.xt, g + NG * phase + 2)
                            copy(xf[:, :], ps[:, 7, :]).then_inc(ff.xf, 1)
                        hidden(G, e)
                    act.wait_ge(ff.xf, G + 1)
                    copy(xhi[:, :], xf[:, :]).then_inc(fr.hi, 1)
                    output(G, E - 2)
                    output(G, E - 1)
                    tanh(g + run * (NG + 1) + 1)
                    if not last:
                        hidden(G + 1, 0)

                tanh(run * (NG + 1))
                hidden(NG * run, 0)
                with act.Fori(0, NG - 1) as g:
                    group(g, False)
                group(NG - 1, True)

            def heads64():
                def prepare(g):
                    for c in range(C1):
                        act.wait_ge(h64.qmm, 8 * g + c + 1)
                        copy(q1[:, c, :], ps[:, c % 4, :]).then_inc(h64.q, 1)
                    front(g + 2 * NG + 1)

                def own_values(g, part):
                    for i in range(4 * part, 4 * part + 4):
                        act.wait_ge(h64.vmm, 8 * g + i + 1)
                        copy(v1[0:SK, i // 2, 8 * (i % 2):8 * (i % 2) + 8, :].rearrange("p h d -> p (h d)"),
                             ps[0:SK, 2 + i % 4, :]).then_inc(h64.v, 1)

                def outputs(g, b):
                    for half in range(2):
                        act.wait_ge(h64.o, 2 * (4 * g + b) + half + 1)
                        copy(oT[:, 4 * half:4 * half + 4, :].rearrange("p c t -> p (c t)"), ps[:, 6 + half, :])\
                            .then_inc(h64.oT, 1)

                prepare(0)
                with act.Fori(0, NG - 1) as g:
                    attend(h64, g, D64 ** -0.5, outputs, own_values)
                    prepare(g + 1)
                attend(h64, NG - 1, D64 ** -0.5, outputs, own_values)

            def mixed():
                def exp(g):
                    act.wait_ge(mx.d, g + 1)
                    act.activation(rt[:, 3, :, :], rt[:, 2, :, :], ACT.Exp).then_inc(mx.e, 1)

                exp(0)
                with act.Fori(0, NG) as g:
                    front(g + 3 * NG + 1)
                    exp(g + 1)

            def head128():
                for g in range(NG + 1):
                    if g < NG:
                        i = g % 2
                        act.wait_ge(h1.qmm, g + 1)
                        copy(q2[i][0][:, :], ps[:, 0, :]).then_inc(h1.qhi, 1)
                        act.wait_ge(h1.kmm, g + 1)
                        copy(k2[i][0][:, :, :].rearrange("p b t -> p (b t)"), ps[:, 1, 0:GB * SP]).then_inc(h1.khi, 1)
                        act.wait_ge(h1.vmm, g + 1)
                        copy(v2[i][:, :, 0:D], ps[0:SK, 2, :].rearrange("p (b d) -> p b d", b=GB)).then_inc(h1.v, 1)
                    if g:
                        act.wait_ge(h1.st, g)
                        act.activation(prob[0:SK, 0, :], ps[0:SK, 5, :], ACT.Exp).then_inc(h1.exp, 1)
                    if g < NG:
                        front(g + 4 * NG + 1)

            def ternary():
                def hidden(g):
                    for t in range(GB):
                        act.wait_ge(tn.h, 4 * g + t + 1)
                        act.activation(hg[g % 2][:, t, :], ps[:, t, :], ACT.Gelu).then_inc(tn.act, 1)

                hidden(0)
                for g in range(NG):
                    for t in range(GB):
                        act.wait_ge(tn.t_mm, 4 * g + t + 1)
                        for c in range(NC_HID):
                            ins = act.activation(hgT[:, t % 2, c, :], ps[:, 4 + t % 2, c * P:c * P + P], ACT.Identity,
                                                 scale=lnw[:, c:c + 1], bias=lnb[:, c:c + 1])
                        ins.then_inc(tn.t, 1)
                        if t == 1 and g < NG - 1:
                            front(g + 7 * NG + 1)
                    if g < NG - 1:
                        hidden(g + 1)

            act.wait_ge(ld.gate, 32)
            act.activation(tg[:, :, :], tg[:, :, :], ACT.Tanh).then_inc(su.tanh, 1)
            front(0)
            heads8(0, 0)
            act.wait_ge(ld.r, 16 * 4)
            experts(0, 1, ACT.Gelu)
            heads64()
            mixed()
            head128()
            act.wait_ge(ld.r, 16 * 13)
            experts(1, 5, ACT.Silu)
            heads8(1, 6)
            act.wait_ge(ld.l3, 64)
            ternary()

        @block.tensor
        def _(pe):
            def split3(o_, w_, m_, stop=True):
                pe.matmul(o_, w_[0], m_[0], start=True, stop=False)
                pe.matmul(o_, w_[1], m_[0], start=False, stop=False)
                return pe.matmul(o_, w_[0], m_[1], start=False, stop=stop)

            xT = (xhi[:, :], xlo[:, :])

            def front(n):
                pe.wait_ge(fr.xn, n + 1)
                for t in range(GB):
                    ins = pe.transpose(ps[:, 7, t * P:t * P + P], xn[:, t, :], idn)
                ins.then_inc(fr.xt, 1)

            def tokens(src, t):
                return tuple(p_[:, t * P:t * P + P] for p_ in src)

            def attend(hs, G, scores, own_values, values, project, prepare=None):
                for i in range(GB + 2):
                    n = 4 * (4 * G + i)
                    if i < GB:
                        for u in (0, 1):
                            if i:
                                pe.wait_ge(hs.sub, n - 2 + u + 1)
                            scores(G, i, u).then_inc(hs.s, 1)
                    if i == 0:
                        own_values(G, 0)
                    if i > GB and prepare:
                        prepare(lambda: project(G, i - 2))
                    elif i > GB:
                        project(G, i - 2)
                    if 1 <= i <= GB:
                        for u in range(4):
                            if u == 2 and i >= 2:
                                project(G, i - 2)
                            if u % 2 == 0:
                                pe.wait_ge(hs.prob, 2 * (4 * G + i - 1) + u // 2 + 1)
                            if i >= 2:
                                pe.wait_ge(hs.pT, n - 8 + u + 1)
                            for h_ in range(4):
                                ins = pe.transpose(ps[0:SK, 2 + u, h_ * P:h_ * P + P], sh[(i - 1) % 2][:, u, h_, :], idn)
                            ins.then_inc(hs.t, 1)
                    if i < GB:
                        for u in (2, 3):
                            pe.wait_ge(hs.sub, n + u - 1)
                            scores(G, i, u).then_inc(hs.s, 1)
                    if i == 0:
                        own_values(G, 1)
                    if 1 <= i <= GB:
                        if i >= 2:
                            pe.wait_ge(hs.x, 4 * G + i - 1)
                        values(G, i - 1)

            def heads8(run, phase):
                wait_done(pe, "ff", 2) if run else None
                pe.wait_ge(su.scratch, 8 if run else 2)
                pe.wait_ge(h8.w, run + 1)

                def blocks(g, between):
                    G = g + NG * run
                    pe.wait_ge(fr.lo, g + NG * phase + 1)
                    pe.wait_ge(h8.ctx, G + 1)
                    for u in range(8):
                        if u == 4:
                            between()
                        if u >= 6:
                            pe.wait_ge(h8.lo, 8 * G + u - 3)
                        cols = slice(4 * (u % 4), 4 * (u % 4) + 4)
                        if u >= 4:
                            o_ = ps[:, BANKS8[u], :]
                            wt = tuple(w_[:, cols, :, :].rearrange("p h r d -> p (h r d)") for w_ in wq)
                            split3(o_, wt, xT, stop=False)
                            pe.matmul(o_, bq2[:, cols, :, :].rearrange("p h r d -> p (h r d)"), ones2[:, :],
                                      start=False, stop=True).then_inc(h8.mm, 1)
                        else:
                            wt = tuple(w_[0:DC + 1, cols, :, :].rearrange("p h r d -> p (h r d)") for w_ in wk)
                            split3(ps[:, BANKS8[u], 0:GB * SP], wt,
                                   tuple(c_[0:DC + 1, :, :].rearrange("p b t -> p (b t)") for c_ in (chi, clo)))\
                                .then_inc(h8.mm, 1)

                def own_values(G, part):
                    if part:
                        return
                    for b in range(GB):
                        ins = split3(ps[0:SK, 6, b * P:b * P + P], tuple(c_[0:DC + 1, b, 0:SK] for c_ in (chi, clo)),
                                     tuple(w_[0:DC + 1, :] for w_ in wv))
                    ins.then_inc(h8.v_mm, 1)

                def scores(G, b, u):
                    if b == 0:
                        pe.wait_ge(h8.lo, 8 * G + 5 + u)
                    if u == 0:
                        pe.wait_ge(h8.kbd, 4 * G + b + 1)
                    return pe.matmul(ps[:, u % 2, 0:HG * SP], q[:, u, b, :],
                                     kbd[b % 2][:, u, :, :].rearrange("p h t -> p (h t)"), start=True, stop=True)

                def values(G, b):
                    if b == 0:
                        pe.wait_ge(h8.v, G + 1)
                    for h in range(H):
                        if h % 4 == 0:
                            pe.wait_ge(h8.pT, 4 * (4 * G + b) + h // 4 + 1)
                        ins = pe.matmul(ps[:, 6, 0:P], v8[:, (b * H + h) * P:(b * H + h + 1) * P],
                                        prob[:, h // 4, (h % 4) * P:(h % 4) * P + P],
                                        start=(h == 0), stop=(h == H - 1))
                    ins.then_inc(h8.o, 1)

                def project(G, b):
                    pe.wait_ge(h8.oT, 4 * G + b + 1)
                    pe.matmul(ps[:, 6, 0:P], oT8[:, :], wo[:, :], start=True, stop=False)
                    pe.matmul(ps[:, 6, 0:P], const[0:1, C_ONE:C_ONE + P], bo[:, :], start=False, stop=True)\
                        .then_inc(h8.y, 1)

                blocks(0, lambda: None)
                front(NG * phase + 1)
                with pe.Fori(0, NG - 1) as g:
                    G = g + NG * run
                    attend(h8, G, scores, own_values, values, project, lambda between: blocks(g + 1, between))
                    front(g + NG * phase + 2)
                    pe.wait_ge(h8.x, 4 * G + 4)
                attend(h8, NG - 1 + NG * run, scores, own_values, values, project)

            def experts(run, phase):
                wait_done(pe, "h1" if run else "h8", 1)
                if run:
                    pe.wait_ge(ld.r, 16 * 13)
                else:
                    pe.wait_ge(ff.w_ss, 2)
                for j in range(1 if run else 2):
                    ins = pe.transpose(ps[:, 6, 8 * j:8 * j + E], emb[:, 2 * j, :], const[0:E, C_ID:C_ID + E])
                ins.then_inc(ff.w_mm, 1)
                pe.wait_ge(ff.w, run + 1)
                if run:
                    pe.wait_ge(h1.big, 8)
                else:
                    pe.wait_ge(wr.big, 8)

                def logits(n_):
                    pe.wait_ge(fr.lo, n_ + 1)
                    n = E if run else 2 * E
                    for t in range(GB):
                        ins = split3(ps[:, 7, t * 16:t * 16 + n], tokens(xT, t), tuple(w_[:, 0:n] for w_ in rwt))
                    ins.then_inc(ff.r, 1)

                def logits_ahead(G):
                    pe.wait_ge(ff.xf, G + 1)
                    n = E if run else 2 * E
                    for t in range(GB):
                        ins = pe.matmul(ps[:, 7, t * 16:t * 16 + n], xf[:, t * P:t * P + P], rraw[:, 0:n],
                                        start=True, stop=True)
                    ins.then_inc(ff.r, 1)

                logits(NG * phase)

                def up(G, e, ahead=False):
                    for c in range(NC_HID):
                        u = e * NC_HID + c
                        if u >= 4:
                            pe.wait_ge(ff.act, 32 * G + u - 3)
                        elif ahead and c == 3:
                            pe.wait_ge(ff.yw, 8 * G)
                        split3(ps[:, u % 4, :],
                               tuple(w_[:, e // 2, (u % 8) * P:(u % 8) * P + P] for w_ in wb), xT)\
                            .then_inc(ff.h, 1)

                def down(G, e):
                    bank = 6
                    if e == E - 1:
                        bank = 3
                        pe.wait_ge(ff.split, 32 * G + 4 * e + 4)
                    elif e:
                        pe.wait_ge(ff.yw, 8 * G + e)
                    for j in range(2):
                        pe.matmul(ps[:, bank, :], sel[:, e:e + 1].to_broadcast([E, P]), cwT[j][:, :],
                                  start=(j == 0), stop=(j == 1))
                    pe.wait_ge(ff.split, 32 * G + 4 * e + 4)
                    if e >= 2:
                        pe.wait_ge(ff.y, 8 * G + e - 1)
                    o_ = ps[:, 4 + e % 2, :]
                    for c in range(NC_HID):
                        w_ = [z[:, 4 + e // 2, (4 * (e % 2) + c) * P:(4 * (e % 2) + c) * P + P] for z in wb]
                        pe.matmul(o_, w_[0], hhi[e % 2][:, c, :], start=(c == 0), stop=False)
                        pe.matmul(o_, w_[1], hhi[e % 2][:, c, :], start=False, stop=False)
                        ins = pe.matmul(o_, w_[0], hlo[e % 2][:, c, :], start=False, stop=(c == NC_HID - 1))
                    ins.then_inc(ff.o, 1)

                def group(g, last):
                    G = g + NG * run
                    R = g + (NG + 1) * run
                    pe.wait_ge(ff.c, R + 1)
                    for t in range(GB):
                        ins = pe.transpose(ps[0:E, 6, t * P:t * P + P], cw[:, t, :], idn)
                    ins.then_inc(ff.ct_mm, 1)
                    up(G, 1)
                    pe.wait_ge(ff.ct, G + 1)
                    for e in range(E):
                        down(G, e)
                        if e < E - 2:
                            up(G, e + 2)
                        if e == 3:
                            front(g + NG * phase + 1)
                        if e == 4:
                            logits_ahead(G)
                    if not last:
                        pe.wait_ge(fr.lo, g + NG * phase + 2)
                        up(G + 1, 0, ahead=True)
                    pe.wait_ge(ff.acc, 7 * G + 7)
                    pe.wait_ge(ff.read, R + 2)
                    for t in range(GB):
                        ins = pe.transpose(ps[:, 7, t * P:t * P + P], acc[:, t * P:t * P + P], idn)
                    ins.then_inc(ff.sum, 1)

                up(NG * run, 0)
                with pe.Fori(0, NG - 1) as g:
                    group(g, False)
                group(NG - 1, True)

            def heads64():
                wait_done(pe, "ff", 1)
                pe.wait_ge(ld.l1, 32)
                pe.wait_ge(wr.l1, 4)

                def blocks(g, between):
                    pe.wait_ge(fr.lo, g + 2 * NG + 1)
                    ct = tuple(c_[0:DC, :, :].rearrange("p b t -> p (b t)") for c_ in (chi, clo))
                    for c in range(C1):
                        if c >= 4:
                            pe.wait_ge(h64.q, 8 * g + c - 3)
                        split3(ps[:, c % 4, :], tuple(w_[:, 0, c * P:c * P + P] for w_ in l1w), xT).then_inc(h64.qmm, 1)
                        if c == 0:
                            pe.wait_ge(h64.ctx, g + 1)
                        if c >= 2:
                            pe.wait_ge(h64.k, 8 * g + c - 1)
                        split3(ps[:, 4 + c % 2, 0:GB * SP], tuple(w_[0:DC, 1, c * P:c * P + P] for w_ in l1w), ct)\
                            .then_inc(h64.kmm, 1)
                    between()

                def own_values(g, part):
                    pe.wait_ge(su.scratch, 5)
                    for i in range(4 * part, 4 * part + 4):
                        if i >= 4:
                            pe.wait_ge(h64.v, 8 * g + i - 3)
                        split3(ps[0:SK, 2 + i % 4, :], tuple(c_[0:DC, i // 2, 0:SK] for c_ in (chi, clo)),
                               tuple(w_[0:DC, 2, 512 * (i % 2):512 * (i % 2) + 512] for w_ in l1w)).then_inc(h64.vmm, 1)

                def scores(g, b, u):
                    if b == 0 and u == 0:
                        pe.wait_ge(h64.k, 8 * g + 8)
                        pe.wait_ge(h64.q, 8 * g + 8)
                        pe.wait_ge(fr.lo, g + 2 * NG + 2)
                    if b == 1 and u == 0:
                        pe.wait_ge(h64.v, 8 * g + 8)
                    for i in range(2):
                        ins = pe.matmul(ps[:, u % 2, 2 * i * SP:2 * (i + 1) * SP], q1[:, 2 * u + i, b * P:b * P + P],
                                        k1[:, 2 * u + i, b, :, :].rearrange("p h t -> p (h t)"), start=True, stop=True)
                    return ins

                def values(g, b):
                    for c in range(C1):
                        if c % 2 == 0:
                            pe.wait_ge(h64.pT, 4 * (4 * g + b) + c // 2 + 1)
                        for par in range(2):
                            ins = pe.matmul(ps[64 * par:64 * par + 64, 6 + c // 4, (c % 4) * P:(c % 4) * P + P],
                                            v1[:, b, 2 * c + par, :],
                                            prob[:, c // 2, (2 * (c % 2) + par) * P:(2 * (c % 2) + par + 1) * P],
                                            start=True, stop=True)
                        if c % 4 == 3:
                            ins.then_inc(h64.o, 1)

                def project(g, b):
                    pe.wait_ge(h64.oT, 2 * (4 * g + b) + 2)
                    for c in range(C1):
                        pe.matmul(ps[:, 6, 0:P], oT[:, c, :], wo1[:, c, :], start=(c == 0), stop=False)
                    pe.matmul(ps[:, 6, 0:P], const[0:1, C_ONE:C_ONE + P], bo[:, :], start=False, stop=True)\
                        .then_inc(h64.y, 1)

                blocks(0, lambda: None)
                front(2 * NG + 1)
                with pe.Fori(0, NG - 1) as g:
                    attend(h64, g, scores, own_values, values, project, lambda between: blocks(g + 1, between))
                    front(g + 2 * NG + 2)
                attend(h64, NG - 1, scores, own_values, values, project)

            def mixed():
                wait_done(pe, "h64", 1)
                pe.wait_ge(mx.w, 1)

                def logits(g):
                    pe.wait_ge(fr.lo, g + 3 * NG + 1)
                    for t in range(GB):
                        ins = split3(ps[:, 7, t * 16:t * 16 + E], tokens(xT, t), tuple(w_[:, 0:E] for w_ in rwt))
                    ins.then_inc(mx.r, 1)

                logits(0)
                with pe.Fori(0, NG) as g:
                    pe.wait_ge(mx.c, g + 1)
                    pe.transpose(ps[0:GB * E, 6, 0:P], cw[:, :, :].rearrange("p t e -> p (t e)"), idn)\
                        .then_inc(mx.ct_mm, 1)
                    for u in range(2 * GB):
                        i, t = u // GB, u % GB
                        if u == GB:
                            pe.wait_ge(mx.ct, g + 1)
                            pe.matmul(ps[:, 6, :], cT[:, :], b2m[:, :, :].rearrange("p t d -> p (t d)"), start=True,
                                      stop=True).then_inc(mx.b_mm, 1)
                        if u >= 6:
                            pe.wait_ge(mx.half, 8 * g + u - 5)
                        split3(ps[:, u % 6, :], tokens(xT, t), tuple(w_[:, 3, 512 * i:512 * i + 512] for w_ in l1w))\
                            .then_inc(mx.o, 1)
                    front(g + 3 * NG + 1)
                    logits(g + 1)

            def head128():
                wait_done(pe, "mx", 1)
                pe.wait_ge(h1.w, 1)
                pe.wait_ge(su.scratch, 7)
                for g in range(NG + 1):
                    m, i = g - 1, (g - 1) % 2
                    q_, k_ = q2[i], k2[i]
                    if g:
                        pe.wait_ge(h1.q, g)
                        pe.wait_ge(h1.k, g)
                        for b in range(GB):
                            ins = split3(ps[:, 3, b * SP:b * SP + SP], tokens([z[:, :] for z in q_], b),
                                         tuple(z[:, b, :] for z in k_))
                        ins.then_inc(h1.s, 1)
                    if g < NG:
                        pe.wait_ge(fr.lo, g + 4 * NG + 1)
                        pe.wait_ge(h1.ctx, g + 1)
                        split3(ps[:, 0, :], tuple(w_[:, 0, :] for w_ in w2), xT, stop=False)
                        pe.matmul(ps[:, 0, :], b_bq2[:, :], ones2[:, :], start=False, stop=True).then_inc(h1.qmm, 1)
                        split3(ps[:, 1, 0:GB * SP], tuple(w_[0:DC + 1, 1, :] for w_ in w2),
                               tuple(c_[0:DC + 1, :, :].rearrange("p b t -> p (b t)") for c_ in (chi, clo)))\
                            .then_inc(h1.kmm, 1)
                        if g:
                            pe.wait_ge(h1.v, g)
                        for b in range(GB):
                            ins = split3(ps[0:SK, 2, b * P:b * P + P], tuple(c_[0:DC + 1, b, 0:SK] for c_ in (chi, clo)),
                                         tuple(w_[0:DC + 1, 2, :] for w_ in w2))
                        ins.then_inc(h1.vmm, 1)
                    if g:
                        if m:
                            pe.wait_ge(h1.x, m)
                        pe.wait_ge(h1.max, g)
                        pe.transpose(ps[0:GB, 4, 0:P], nm2[:, :], idn).then_inc(h1.t, 1)
                        pe.wait_ge(h1.nT, g)
                        for b in range(GB):
                            o_ = ps[0:SK, 5, b * P:b * P + P]
                            split3(o_, tuple(z[:, b, 0:SK] for z in k_), tokens([z[:, :] for z in q_], b), stop=False)
                            ins = pe.matmul(o_, const[0:GB, C_SELB + b * SK:C_SELB + b * SK + SK], nT2[:, :],
                                            start=False, stop=True)
                        ins.then_inc(h1.st, 1)
                    if g < NG:
                        front(g + 4 * NG + 1)
                    if g:
                        pe.wait_ge(h1.exp, g)
                        for b in range(GB):
                            ins = pe.matmul(ps[:, (6, 4)[b // 2], (b % 2) * (D + 1):(b % 2 + 1) * (D + 1)],
                                            prob[0:SK, 0, b * P:b * P + P], v2[i][:, b, :], start=True, stop=True)
                            if b % 2:
                                ins.then_inc(h1.o, 1)

            def ternary():
                wait_done(pe, "h8", 2)
                pe.wait_ge(tn.sum, 1)
                pe.matmul(ps[:, 2, 0:2], const[:, C_ONE:C_ONE + P], ta[:, 8:10], start=True, stop=True)\
                    .then_inc(tn.gamma, 1)
                pe.wait_ge(tn.w, 1)
                for j, w_ in enumerate((wfr, wpr)):
                    for c in range(4):
                        ins = pe.transpose(ps[:, j, c * P:c * P + P], w_[:, c, :], idn)
                    ins.then_inc(tn.wT_mm, 1)
                pe.wait_ge(tn.wT, 2)

                def hidden(g):
                    pe.wait_ge(fr.lo, g + 7 * NG + 1)
                    w_ = wf[:, :, :].rearrange("p c h -> p (c h)")
                    for t in range(GB):
                        pe.matmul(ps[:, t, :], xhi[:, t * P:t * P + P], w_, start=True, stop=False)
                        pe.matmul(ps[:, t, :], xlo[:, t * P:t * P + P], w_, start=False, stop=True).then_inc(tn.h, 1)

                hidden(0)
                for g in range(NG):
                    for t in range(GB + 1):
                        if t == GB and g < NG - 1:
                            hidden(g + 1)
                        if t < GB:
                            pe.wait_ge(tn.norm, 4 * g + t + 1)
                            if 4 * g + t >= 2:
                                pe.wait_ge(tn.t, 4 * g + t - 1)
                            for c in range(NC_HID):
                                ins = pe.transpose(ps[:, 4 + t % 2, c * P:c * P + P], hg[g % 2][:, t, c * P:c * P + P],
                                                   idn)
                            ins.then_inc(tn.t_mm, 1)
                        if t == 1:
                            if g < NG - 1:
                                front(g + 7 * NG + 1)
                            if g:
                                pe.wait_ge(tn.x, g)
                        if t >= 1:
                            pe.wait_ge(tn.t, 4 * g + t)
                            for c in range(NC_HID):
                                ins = pe.matmul(ps[:, 6, (t - 1) * P:t * P], hgT[:, (t - 1) % 2, c, :], wp[:, c, :],
                                                start=(c == 0), stop=(c == NC_HID - 1))
                    ins.then_inc(tn.y, 1)

            pe.wait_ge(ld.const, 16)
            pe.wait_ge(ld.ctx, 16)
            for b in range(B):
                ins = pe.transpose(ps[0:DC, b // 4, (b % 4) * SP:(b % 4) * SP + SK], ctok[:, b, :],
                                   const[0:SK, C_ID:C_ID + SK])
            ins.then_inc(su.pe, 1)
            front(0)
            pe.wait_ge(su.dve, 4)
            pe.wait_ge(su.zero, 9)
            heads8(0, 0)
            experts(0, 1)
            heads64()
            mixed()
            head128()
            experts(1, 5)
            heads8(1, 6)
            ternary()

        @block.vector
        def _(dve):
            def over(ap, n=E):
                return ap.unsqueeze(2).to_broadcast([P, GB, n])

            def along(col, n=E):
                return const[:, col:col + n].unsqueeze(1).to_broadcast([P, GB, n])

            def group(t_, g, w=1):
                return t_[:, bass.ds(g, w), :]

            def variance(lk, s_, n, mean, var):
                lk.wait()
                lk.mark(dve.tensor_tensor(fs[:, 0, :], s_[:, :, 1], s_[:, :, 4], ALU.add))
                lk.mark(dve.tensor_tensor(fs[:, 1, :], s_[:, :, 1], s_[:, :, 4], ALU.subtract))
                lk.mark(dve.tensor_tensor(fs[:, 2, :], s_[:, :, 2], s_[:, :, 5], ALU.add))
                lk.wait()
                lk.mark(dve.tensor_scalar(mean, fs[:, 0, :], 0.5, None, ALU.mult))
                lk.mark(dve.tensor_tensor(fs[:, 3, :], fs[:, 1, :], fs[:, 1, :], ALU.mult))
                lk.mark(dve.tensor_scalar(fs[:, 4, :], fs[:, 2, :], 1.0 / n, None, ALU.mult))
                lk.wait()
                lk.link(dve.scalar_tensor_tensor(out=var, in0=fs[:, 3, :], scalar=0.25, in1=fs[:, 4, :],
                                                 op0=ALU.mult, op1=ALU.add))

            def front_a(gn, n):
                lk = Link(dve, fr.link, 11, n)
                for t in range(GB):
                    lk.mark(dve.bn_stats(st[:, t, :], x[:, bass.ds(gn * GB + t, 1), :].rearrange("p o d -> p (o d)")))
                variance(lk, st, D, mv[:, :, 0], mv[:, :, 1])
                dve.tensor_scalar(vv[:, :], mv[:, :, 1], const[:, bass.ds(n + C_NA, 1)], const[:, bass.ds(n + C_NB, 1)],
                                  ALU.mult, ALU.add).then_inc(fr.var, 1)
                lk.end()

            def front_b(gn, n):
                dve.wait_ge(fr.rstd, n + 1)
                for t in range(GB):
                    ins = dve.tensor_scalar(xn[:, t, :], x[:, bass.ds(gn * GB + t, 1), :].rearrange("p o d -> p (o d)"),
                                            mv[:, t, 0:1], rstd[:, t:t + 1], ALU.subtract, ALU.mult)
                ins.then_inc(fr.xn, 1)

            def front_c(n):
                dve.wait_ge(fr.hi, n + 1)
                dve.tensor_tensor(xlo[:, :], ps[:, 7, :], f32(xhi[:, :]), ALU.subtract).then_inc(fr.lo, 1)

            def stage(lk, g, rows, s_):
                c_ = ctxT[0:rows, bass.ds(g * GB, GB), :]
                lk.mark(dve.tensor_copy(chi[0:rows, :, :], c_))
                lk.wait()
                dve.tensor_tensor(clo[0:rows, :, :], c_, f32(chi[0:rows, :, :]), ALU.subtract).then_inc(s_, 1)

            sl = Link(dve, su.vlink, 0)

            def add_to_x(tile_, w, in_, scalar, s_):
                xt = x[:, bass.ds(tile_, w), :].rearrange("p o d -> p (o d)")
                dve.scalar_tensor_tensor(out=xt, in0=in_, scalar=scalar, in1=xt, op0=ALU.mult, op1=ALU.add).then_inc(s_, 1)

            def attend(hs, G, add, prepare=None):
                for i in range(GB + 2):
                    if i < GB:
                        n = 4 * (4 * G + i)
                        for pair in range(2):
                            for u in (2 * pair, 2 * pair + 1):
                                dve.wait_ge(hs.s, n + u + 1)
                                s_ = ps[:, u % 2, 0:4 * SP].rearrange("p (h t) -> p h t", h=4)[:, :, 0:SK]
                                dve.tensor_reduce(top_s[:, 4 * u:4 * u + 4].unsqueeze(2), s_, AX.X, ALU.max)\
                                   .then_inc(hs.max, 1)
                            for u in (2 * pair, 2 * pair + 1):
                                s_ = ps[:, u % 2, 0:4 * SP].rearrange("p (h t) -> p h t", h=4)[:, :, 0:SK]
                                dve.wait_ge(hs.max, n + u + 1)
                                dve.tensor_tensor(sh[i % 2][:, u, :, :], s_,
                                                  top_s[:, 4 * u:4 * u + 4].unsqueeze(2).to_broadcast([P, 4, SK]),
                                                  ALU.subtract).then_inc(hs.sub, 1)
                            if pair == 0 and i >= 2:
                                add(G, i - 2)
                            dve.wait_ge(hs.exp, n + 2 * pair + 2)
                            e_ = sh[i % 2][:, 2 * pair:2 * pair + 2, :, :].rearrange("p u h t -> p (u h) t")
                            dve.tensor_reduce(den[:, 8 * pair:8 * pair + 8].unsqueeze(2), e_, AX.X, ALU.add)\
                               .then_inc(hs.den, 1)
                            dve.wait_ge(hs.den, 2 * (4 * G + i) + pair + 1)
                            dve.reciprocal(rd[i % 2][:, 8 * pair:8 * pair + 8], den[:, 8 * pair:8 * pair + 8])\
                               .then_inc(hs.rden, 1)
                    else:
                        if i > GB and prepare:
                            prepare(lambda: add(G, i - 2))
                        else:
                            add(G, i - 2)

            def heads8_weights(run):
                def rep(ap, rows):
                    return ap[0:rows, :].rearrange("p (h d) -> p h d", h=H).unsqueeze(2).to_broadcast([rows, H, 3, D8])
                dve.wait_ge(ld.a, 16 * N_A * (run + 1))
                dve.wait_ge(su.zero, 9)
                K1 = DC + 1
                sl.mark(dve.tensor_copy(wq[0][:, :, 0:3, :], rep(a_raw[:, 0, :], P)))
                sl.mark(dve.tensor_copy(wk[0][0:K1, :, 0:3, :], rep(a_raw[:, 1, :], K1)))
                sl.mark(dve.tensor_copy(wv[0][0:K1, :], a_raw[0:K1, 2, :]))
                sl.mark(dve.tensor_copy(bq2[:, :, 0:3, :], rep(a_bq[:, :], 64)))
                sl.mark(dve.tensor_copy(wo[:, :], a_raw[:, 3, :]))
                sl.mark(dve.tensor_copy(bo[:, :], a_bo[:, :]))
                sl.wait()
                dve.tensor_tensor(wq[1][:, :, 0:3, :], rep(a_raw[:, 0, :], P), f32(wq[0][:, :, 0:3, :]), ALU.subtract)
                dve.tensor_tensor(wk[1][0:K1, :, 0:3, :], rep(a_raw[:, 1, :], K1), f32(wk[0][0:K1, :, 0:3, :]),
                                  ALU.subtract)
                dve.tensor_tensor(wv[1][0:K1, :], a_raw[0:K1, 2, :], f32(wv[0][0:K1, :]), ALU.subtract)
                dve.tensor_tensor(bq2[32:64, :, 0:3, :], rep(a_bq[:, :], 64)[32:64], f32(bq2[32:64, :, 0:3, :]),
                                  ALU.subtract).then_inc(h8.w, 1)

            def heads8(run, phase):
                layer = 3 * run
                heads8_weights(run)

                def blocks(g, between):
                    G = g + NG * run
                    n = g + NG * phase + 1
                    gn = next_group(g)
                    lk = Link(dve, h8.link, 1, G)
                    stage(lk, g, DC + 1, h8.ctx)
                    lk.end()
                    front_a(gn, n)
                    for u in range(8):
                        dve.wait_ge(h8.hi, 8 * G + u + 1)
                        t_, m, w = (q, C_MQ, GT) if u >= 4 else (k, C_MK, GB * SP)
                        t_ = t_[:, u % 4, :, :].rearrange("p b t -> p (b t)")
                        dve.scalar_tensor_tensor(out=t_, in0=ps[:, BANKS8[u], 0:w], scalar=const[:, m:m + 1], in1=f32(t_),
                                                 op0=ALU.mult, op1=ALU.add).then_inc(h8.lo, 1)
                        if u == 3:
                            front_b(gn, n)
                            between()

                def add(G, b):
                    dve.wait_ge(h8.y, 4 * G + b + 1)
                    add_to_x((G - NG * run) * GB + b, 1, ps[:, 6, 0:P], tg[:, 0, layer:layer + 1], h8.x)

                blocks(0, lambda: None)
                front_c(NG * phase + 1)
                with dve.Fori(0, NG - 1) as g:
                    attend(h8, g + NG * run, add, lambda between: blocks(g + 1, between))
                    front_c(g + NG * phase + 2)
                attend(h8, NG - 1 + NG * run, add)

            def second_biases(s_):
                dve.tensor_tensor(b2m[:, :, :], b2rep[:, :].unsqueeze(1).to_broadcast([GB * E, GB, D]),
                                  const[0:GB * E, C_TM:C_TM + GB].unsqueeze(2).to_broadcast([GB * E, GB, D]),
                                  ALU.mult).then_inc(s_, 1)

            def split_small(hi, lo, src):
                sl.link(dve.tensor_copy(hi, src))
                return dve.tensor_tensor(lo, src, f32(hi), ALU.subtract)

            def first_best(lk, s_, best, hit, tie, one):
                lk.link(dve.tensor_reduce(best, s_, AX.X, ALU.max))
                lk.link(dve.tensor_tensor(hit, s_, over(best), ALU.is_equal))
                lk.link(dve.tensor_tensor(hit, hit, along(C_DOWN), ALU.mult))
                lk.link(dve.tensor_reduce(tie, hit, AX.X, ALU.max))
                lk.link(dve.tensor_tensor(one, hit, over(tie), ALU.is_equal))

            def route_top2(lk, n, part):
                R = [rt[:, i, :, :] for i in range(12)]
                S = [rs[:, i, :] for i in range(12)]
                if part == 0:
                    dve.wait_ge(ff.r, n + 1)
                    o_ = ps[:, 7, 0:GB * 16].rearrange("p (t e) -> p t e", e=16)
                    dve.tensor_copy(R[2], o_[:, :, 0:E])
                    dve.tensor_copy(R[1], o_[:, :, E:2 * E]).then_inc(ff.read, 1)
                    dve.wait_ge(ff.rn, n + 1)
                    lk.link(dve.tensor_scalar(S[4], S[1], 1e-8, None, ALU.add))
                    lk.link(dve.reciprocal(S[5], S[4]))
                    dve.wait_ge(ff.read, n + 1)
                    lk.link(dve.tensor_tensor(R[0], R[1], over(S[5]), ALU.mult))
                    lk.mark(dve.tensor_tensor(R[1], R[0], rowb[:, :].unsqueeze(1).to_broadcast([P, GB, E]), ALU.add))
                    lk.link(dve.tensor_reduce(S[6], R[2], AX.X, ALU.min))
                    lk.link(dve.tensor_tensor(R[3], R[2], over(S[6]), ALU.is_equal))
                    lk.link(dve.tensor_tensor(R[4], R[3], along(C_UP), ALU.mult))
                    lk.link(dve.tensor_reduce(S[7], R[4], AX.X, ALU.max))
                elif part == 1:
                    lk.link(dve.tensor_tensor(R[5], R[4], over(S[7]), ALU.is_equal))
                    lk.link(dve.scalar_tensor_tensor(out=R[6], in0=R[5], scalar=-1e30, in1=R[1], op0=ALU.mult,
                                                     op1=ALU.add))
                    first_best(lk, R[6], S[10], R[7], S[11], R[9])
                else:
                    lk.link(dve.scalar_tensor_tensor(out=R[10], in0=R[9], scalar=-3e30, in1=R[6], op0=ALU.mult,
                                                     op1=ALU.add))
                    first_best(lk, R[10], S[6], R[3], S[7], R[11])
                    dve.tensor_tensor(S[8], S[6], S[10], ALU.subtract).then_inc(ff.d, 1)

            def weigh_top2(lk, n, gate):
                R = [rt[:, i, :, :] for i in range(12)]
                S = [rs[:, i, :] for i in range(12)]
                dve.wait_ge(ff.tanh, n + 1)
                lk.mark(dve.tensor_scalar(S[2], S[9], 0.5, 0.5, ALU.mult, ALU.add))
                lk.link(dve.tensor_scalar(S[3], S[9], -0.5, 0.5, ALU.mult, ALU.add))
                lk.mark(dve.tensor_tensor(R[7], R[9], over(S[3]), ALU.mult))
                lk.link(dve.tensor_tensor(R[8], R[11], over(S[2]), ALU.mult))
                lk.link(dve.tensor_tensor(R[0], R[7], R[8], ALU.add))
                dve.tensor_scalar(cw[:, :, :], R[0], gate, None, ALU.mult).then_inc(ff.c, 1)

            def route_top1(lk, n, part):
                R = [rt[:, i, :, :] for i in range(12)]
                S = [rs[:, i, :] for i in range(12)]
                if part == 0:
                    dve.wait_ge(ff.r, n + 1)
                    o_ = ps[:, 7, 0:GB * 16].rearrange("p (t e) -> p t e", e=16)
                    dve.tensor_copy(R[0], o_[:, :, 0:E]).then_inc(ff.read, 1)
                elif part == 1:
                    dve.wait_ge(ff.read, n + 1)
                    first_best(lk, R[0], S[0], R[1], S[1], R[5])
                else:
                    dve.tensor_tensor(R[2], R[0], over(S[0]), ALU.subtract).then_inc(ff.d, 1)

            def weigh_top1(lk, n, gate):
                R = [rt[:, i, :, :] for i in range(12)]
                S = [rs[:, i, :] for i in range(12)]
                dve.wait_ge(ff.tanh, n + 1)
                lk.mark(dve.tensor_scalar(R[6], R[3], 1.0, None, ALU.add))
                lk.link(dve.tensor_scalar(R[7], R[3], -1.0, 1.0, ALU.mult, ALU.add))
                lk.link(dve.reciprocal(R[8], R[7]))
                lk.link(dve.tensor_tensor(R[9], R[6], R[8], ALU.mult))
                lk.link(dve.tensor_reduce(S[2], R[9], AX.X, ALU.add))
                lk.link(dve.reciprocal(S[3], S[2]))
                lk.link(dve.tensor_tensor(R[10], R[5], over(S[3]), ALU.mult))
                dve.tensor_scalar(cw[:, :, :], R[10], gate, None, ALU.mult).then_inc(ff.c, 1)

            def experts(run, phase):
                layer = 2 * run
                gate = tg[:, 1, layer:layer + 1]
                dve.wait_ge(ld.r, 16 * (13 if run else 4))
                n_ = E if run else 2 * E
                if not run:
                    sl.link(dve.tensor_tensor(emb[:, 1, :], emb[:, 0, :], emb[:, 0, :], ALU.mult))
                    dve.tensor_reduce(emb_s[:, 0:1], emb[:, 1, :], AX.X, ALU.add).then_inc(ff.w_ss, 1)
                    dve.wait_ge(ff.w_rt, 1)
                    sl.link(dve.tensor_scalar(emb_s[:, 2:3], emb_s[:, 1:2], 1e-8, None, ALU.add))
                    sl.link(dve.reciprocal(emb_s[:, 3:4], emb_s[:, 2:3]))
                    dve.tensor_scalar(emb[:, 2, :], emb[:, 0, :], emb_s[:, 3:4], None, ALU.mult).then_inc(ff.w_ss, 1)
                    sl.link(dve.tensor_scalar(rowb[:, :], rowb[:, :], 0.1, None, ALU.mult))
                dve.wait_ge(ff.w_mm, run + 1)
                if run:
                    sl.link(dve.tensor_scalar(rraw[:, 0:n_], ps[:, 6, 0:n_], rmsw[:, 0:1], None, ALU.mult))
                else:
                    sl.link(dve.tensor_copy(rraw[:, 0:n_], ps[:, 6, 0:n_]))
                split_small(rwt[0][:, 0:n_], rwt[1][:, 0:n_], rraw[:, 0:n_])
                sl.wait()
                dve.tensor_copy(sel[:, :], const[0:E, C_ID:C_ID + E])\
                   .then_inc(ff.w, 1)

                def squares(n):
                    if not run:
                        dve.tensor_tensor(rs[:, 2, :], mv[:, :, 1], rstd[:, :], ALU.mult).then_inc(ff.sq, 1)
                        dve.wait_ge(ff.sq, n + 1)
                        dve.scalar_tensor_tensor(out=rs[:, 0, :], in0=rs[:, 2, :], scalar=float(D), in1=rstd[:, :],
                                                 op0=ALU.mult, op1=ALU.mult).then_inc(ff.nn, 1)

                def route(lk, n, part):
                    (route_top1 if run else route_top2)(lk, n, part)

                weigh = weigh_top1 if run else weigh_top2
                s_link = (ff.link, ff.link1)[run]
                s_link2 = (ff.link2, ff.link3)[run]
                PER, PER2 = ((21, 5), (5, 7))[run]
                squares(0)
                R0 = run * (NG + 1)
                lk = Link(dve, s_link, PER, 0)
                for part in range(3):
                    route(lk, R0, part)
                lk.end()
                lk = Link(dve, s_link2, PER2, 0)
                weigh(lk, R0, gate)
                lk.end()
                with dve.Fori(0, NG) as g:
                    G = g + NG * run
                    n = g + NG * phase + 1
                    gn = next_group(g)
                    R = g + (NG + 1) * run

                    def split(e):
                        if e >= 2:
                            dve.wait_ge(ff.o, 8 * G + e - 1)
                        for c in range(NC_HID):
                            u = NC_HID * e + c
                            dve.wait_ge(ff.act, 32 * G + u + 1)
                            if c in DVE_HI:
                                dve.tensor_copy(hhi[e % 2][:, c, :], hf[:, u % 4, :]).then_inc(ff.hi, 1)
                                dve.wait_ge(ff.hi, len(DVE_HI) * (8 * G + e) + DVE_HI.index(c) + 1)
                            dve.tensor_tensor(hlo[e % 2][:, c, :], hf[:, u % 4, :], f32(hhi[e % 2][:, c, :]),
                                              ALU.subtract).then_inc(ff.split, 1)

                    def weighted(e):
                        dve.wait_ge(ff.y, 8 * G + e + 1)
                        y_ = yw[e % 2] if e else acc
                        dve.tensor_tensor(y_[:, :], y_[:, :], ps[:, 3 if e == E - 1 else 6, :], ALU.mult).then_inc(ff.yw, 1)

                    split(0)
                    dve.wait_ge(ff.ct_mm, G + 1)
                    dve.tensor_copy(cwT[0][:, :], ps[0:E, 6, :]).then_inc(ff.read_hi, 1)
                    dve.wait_ge(ff.read_hi, G + 1)
                    dve.tensor_tensor(cwT[1][:, :], ps[0:E, 6, :], f32(cwT[0][:, :]), ALU.subtract).then_inc(ff.ct, 1)
                    split(1)
                    weighted(0)
                    lk = Link(dve, s_link, PER, g + 1)
                    for e in range(2, E):
                        split(e)
                        if e == 2:
                            front_a(gn, n)
                        if e == 3:
                            front_b(gn, n)
                            squares(g + 1)
                        if e == E - 1:
                            dve.wait_ge(fr.hi, n + 1)
                            dve.tensor_tensor(xlo[:, :], xf[:, :], f32(xhi[:, :]), ALU.subtract).then_inc(fr.lo, 1)
                        weighted(e - 1)
                        if e >= E - 2:
                            route(lk, R + 1, e - E + 2)
                    weighted(E - 1)
                    route(lk, R + 1, 2)
                    lk.end()
                    dve.wait_ge(ff.sum, G + 1)
                    xt = x[:, bass.ds(g * GB, GB), :].rearrange("p t d -> p (t d)")
                    dve.tensor_tensor(xt, xt, ps[:, 7, :], ALU.add).then_inc(ff.x, 1)
                    lk = Link(dve, s_link2, PER2, g + 1)
                    weigh(lk, R + 1, gate)
                    lk.end()

            def add_rows(g, s_mm, G, s_):
                dve.wait_ge(s_mm, G + 1)
                xt = x[:, bass.ds(g * GB, GB), :].rearrange("p t d -> p (t d)")
                dve.tensor_tensor(xt, xt, ps[:, 6, :], ALU.add).then_inc(s_, 1)

            def heads64():
                def blocks(g, between):
                    n = g + 2 * NG + 1
                    gn = next_group(g)
                    lk = Link(dve, h64.link, 1, g)
                    stage(lk, g, DC, h64.ctx)
                    lk.end()
                    front_a(gn, n)
                    for c in range(C1):
                        if c == 0:
                            dve.wait_ge(su.scratch, 3)
                        dve.wait_ge(h64.kmm, 8 * g + c + 1)
                        for par in range(2):
                            rows = slice(64 * par, 64 * par + 64)
                            ins = dve.tensor_copy(k1[rows, c, :, par, :],
                                                  ps[rows, 4 + c % 2, 0:GB * SP].rearrange("p (b t) -> p b t", b=GB))
                        ins.then_inc(h64.k, 1)
                        if c == 1:
                            front_b(gn, n)
                    between()

                def add(g, b):
                    dve.wait_ge(h64.y, 4 * g + b + 1)
                    add_to_x(g * GB + b, 1, ps[:, 6, 0:P], tg[:, 0, 1:2], h64.x)

                blocks(0, lambda: None)
                front_c(2 * NG + 1)
                with dve.Fori(0, NG - 1) as g:
                    attend(h64, g, add, lambda between: blocks(g + 1, between))
                    front_c(g + 2 * NG + 2)
                attend(h64, NG - 1, add)

            def mixed():
                dve.wait_ge(ld.r, 16 * 10)
                split_small(rwt[0][:, 0:E], rwt[1][:, 0:E], rraw[:, 0:E])
                second_biases(mx.w)
                R = [rt[:, i, :, :] for i in range(12)]
                S = [rs[:, i, :] for i in range(12)]

                def route(g):
                    lk = Link(dve, mx.link, 12, g)
                    dve.wait_ge(mx.r, g + 1)
                    o_ = ps[:, 7, 0:GB * 16].rearrange("p (t e) -> p t e", e=16)[:, :, 0:E]
                    lk.link(dve.tensor_tensor(R[0], o_, rowb[:, :].unsqueeze(1).to_broadcast([P, GB, E]), ALU.add))
                    lk.link(dve.tensor_reduce(S[0], R[0], AX.X, ALU.max))
                    dve.tensor_tensor(R[2], R[0], over(S[0]), ALU.subtract).then_inc(mx.d, 1)
                    dve.wait_ge(mx.e, g + 1)
                    lk.link(dve.tensor_reduce(S[1], R[3], AX.X, ALU.add))
                    lk.link(dve.reciprocal(S[2], S[1]))
                    lk.link(dve.tensor_tensor(R[4], R[3], over(S[2]), ALU.mult))
                    lk.link(dve.tensor_scalar(R[5], R[4], 0.1, None, ALU.is_ge))
                    lk.link(dve.tensor_tensor(R[6], R[4], R[5], ALU.mult))
                    lk.link(dve.tensor_reduce(S[3], R[6], AX.X, ALU.add))
                    lk.link(dve.tensor_scalar(S[4], S[3], 0.0, None, ALU.is_equal))
                    lk.link(dve.tensor_tensor(S[5], S[3], S[4], ALU.add))
                    lk.link(dve.reciprocal(S[6], S[5]))
                    lk.link(dve.tensor_tensor(R[7], R[6], over(S[6]), ALU.mult))
                    dve.tensor_scalar(cw[:, :, :], R[7], tg[:, 1, 1:2], None, ALU.mult).then_inc(mx.c, 1)
                    lk.end()

                route(0)
                with dve.Fori(0, NG) as g:
                    n = g + 3 * NG + 1
                    gn = next_group(g)
                    dve.wait_ge(mx.ct_mm, g + 1)
                    dve.tensor_copy(cT[:, :], ps[0:GB * E, 6, 0:P]).then_inc(mx.ct, 1)
                    front_a(gn, n)
                    lk = Link(dve, mx.link2, 24, g)
                    for i in range(2):
                        for e in range(4):
                            for t in range(GB):
                                if e == 0:
                                    dve.wait_ge(mx.o, 8 * g + 4 * i + t + 1)
                                    if i:
                                        dve.wait_ge(mx.xb, g + 1)
                                else:
                                    lk.wait(back=3 - t if e == 3 else 3)
                                xt = x[:, bass.ds(g * GB + t, 1), :].rearrange("p o d -> p (o d)")
                                ins = dve.scalar_tensor_tensor(out=xt, in0=ps[:, (GB * i + t) % 6, e * P:e * P + P],
                                                               scalar=cw[:, t, 4 * i + e:4 * i + e + 1], in1=xt,
                                                               op0=ALU.mult, op1=ALU.add)
                                if e < 3:
                                    lk.mark(ins)
                                else:
                                    ins.then_inc(mx.half, 1)
                        if i == 0:
                            front_b(gn, n)
                            dve.wait_ge(mx.half, 8 * g + 4)
                            add_rows(g, mx.b_mm, g, mx.xb)
                            front_c(n)
                    lk.end()
                    route(g + 1)

            def head128():
                dve.wait_ge(ld.b, 16 * 8)
                K1 = DC + 1
                sl.mark(dve.tensor_copy(w2[0][:, 0, :], b_raw[:, 0, :]))
                sl.mark(dve.tensor_copy(w2[0][0:K1, 1:3, :], b_raw[0:K1, 1:3, :]))
                sl.mark(dve.tensor_copy(b_bq2[:, :], b_bq[:, :]))
                sl.link(dve.memset(scal[:, :], 1.0))
                sl.mark(dve.tensor_copy(scal[:, 0:4], rmsw[:, 0:1].to_broadcast([P, 4])))
                dve.tensor_tensor(w2[1][:, 0, :], b_raw[:, 0, :], f32(w2[0][:, 0, :]), ALU.subtract)
                dve.tensor_tensor(w2[1][0:K1, 1:3, :], b_raw[0:K1, 1:3, :], f32(w2[0][0:K1, 1:3, :]), ALU.subtract)
                dve.tensor_tensor(b_bq2[32:64, :], b_bq[32:64, :], f32(b_bq2[32:64, :]), ALU.subtract).then_inc(h1.w, 1)
                sl.wait()
                for g in range(NG + 1):
                    n = g + 4 * NG + 1
                    gn = next_group(g)
                    if g < NG:
                        i = g % 2
                        lk = Link(dve, h1.link, 5, g)
                        if g:
                            dve.wait_ge(h1.vmm, g)
                        stage(lk, g, K1, h1.ctx)
                        front_a(gn, n)
                    if g:
                        dve.wait_ge(h1.s, g)
                        dve.tensor_reduce(nm2[:, :].unsqueeze(2),
                                          ps[:, 3, 0:GB * SP].rearrange("p (b t) -> p b t", b=GB)[:, :, 0:SK],
                                          AX.X, ALU.max, negate=True).then_inc(h1.max, 1)
                    if g < NG:
                        dve.wait_ge(h1.qhi, g + 1)
                        dve.tensor_tensor(q2[i][1][:, :], ps[:, 0, :], f32(q2[i][0][:, :]), ALU.subtract).then_inc(h1.q, 1)
                    if g:
                        dve.wait_ge(h1.t, g)
                        dve.tensor_copy(nT2[:, :], ps[0:GB, 4, 0:P]).then_inc(h1.nT, 1)
                    if g < NG:
                        dve.wait_ge(h1.khi, g + 1)
                        dve.tensor_tensor(k2[i][1][:, :, :].rearrange("p b t -> p (b t)"), ps[:, 1, 0:GB * SP],
                                          f32(k2[i][0][:, :, :]).rearrange("p b t -> p (b t)"), ALU.subtract)\
                           .then_inc(h1.k, 1)
                        front_b(gn, n)
                        for b in range(2):
                            c = g * 2 + b
                            hi, lo = wb[0][:, c, :], wb[1][:, c, :]
                            dve.wait_ge((ld.raw0, ld.raw1)[b], 16 * (g + NG + 1))
                            lk.link(dve.tensor_scalar(raw[b][:, :], raw[b][:, :], scal[:, c:c + 1], None, ALU.mult))
                            lk.link(dve.tensor_copy(hi, raw[b][:, :]))
                            dve.tensor_tensor(lo, raw[b][:, :], f32(hi), ALU.subtract).then_inc(h1.big, 1)
                        lk.end()
                        front_c(n)
                    if g:
                        lk = Link(dve, h1.link2, 3, g - 1)
                        for i in range(2):
                            dve.wait_ge(h1.o, 2 * (g - 1) + i + 1)
                            lk.mark(dve.reciprocal(rden[:, 2 * i:2 * i + 2].unsqueeze(2),
                                                   ps[:, (6, 4)[i], 0:2 * (D + 1)].rearrange("p (b d) -> p b d", b=2)[:, :, D:D + 1]))
                        lk.wait()
                        lk.link(dve.tensor_scalar(rden[:, 4:8], rden[:, 0:4], tg[:, 0, 2:3], None, ALU.mult))
                        lk.end()
                        for b in range(GB):
                            o_ = ps[:, (6, 4)[b // 2], (b % 2) * (D + 1):(b % 2) * (D + 1) + D]
                            xt = x[:, (g - 1) * GB + b, :]
                            ins = dve.scalar_tensor_tensor(out=xt, in0=o_, scalar=rden[:, 4 + b:5 + b], in1=xt,
                                                           op0=ALU.mult, op1=ALU.add)
                        ins.then_inc(h1.x, 1)

            def ternary():
                dve.wait_ge(ld.l3, 64)
                for j, w_ in enumerate((wfr, wpr)):
                    ins = dve.tensor_reduce(ta[:, 8 + j:9 + j], w_[:, :, :].rearrange("p c d -> p (c d)"), AX.X, ALU.add,
                                            apply_absolute_value=True)
                ins.then_inc(tn.sum, 1)
                dve.wait_ge(tn.gamma, 1)
                sl.link(dve.tensor_scalar(ta[:, 10:12], ps[:, 2, 0:2], 1.0 / (HID * D), 1e-6, ALU.mult, ALU.add))
                sl.mark(dve.tensor_scalar(ta[:, 12:14], ta[:, 10:12], 0.5, None, ALU.mult))
                sl.link(dve.tensor_scalar(ta[:, 14:16], ta[:, 10:12], -0.5, None, ALU.mult))
                for j, w_ in enumerate((wfr, wpr)):
                    wv_ = w_[:, :, :].rearrange("p c d -> p (c d)")
                    sl.link(dve.tensor_scalar(hg[0][:, j, :], wv_, ta[:, 14 + j:15 + j], None, ALU.is_lt))
                    ins = dve.scalar_tensor_tensor(out=wv_, in0=wv_, scalar=ta[:, 12 + j:13 + j], in1=hg[0][:, j, :],
                                                   op0=ALU.is_gt, op1=ALU.subtract)
                ins.then_inc(tn.w, 1)
                dve.wait_ge(tn.wT_mm, 1)
                dve.tensor_copy(wf[:, :, :].rearrange("p c h -> p (c h)"), ps[:, 0, :]).then_inc(tn.wT, 1)
                dve.wait_ge(tn.wT_mm, 2)
                dve.tensor_copy(wp[:, :, :].rearrange("p c h -> p (c h)"), ps[:, 1, :]).then_inc(tn.wT, 1)
                for g in range(NG):
                    n = g + 7 * NG + 1
                    gn = next_group(g)
                    if g < NG - 1:
                        front_a(gn, n)
                    lk = Link(dve, tn.link, 11, g)
                    for t in range(GB):
                        dve.wait_ge(tn.act, 4 * g + t + 1)
                        lk.mark(dve.bn_stats(st[:, t, :], hg[g % 2][:, t, :]))
                    variance(lk, st, HID, mh[:, 0, :], mh[:, 1, :])
                    dve.tensor_scalar(ta[:, 0:4], mh[:, 1, :], 1e-5, None, ALU.add).then_inc(tn.var, 1)
                    if g < NG - 1:
                        front_b(gn, n)
                    dve.wait_ge(tn.rstd, g + 1)
                    for t in range(GB):
                        dve.tensor_scalar(hg[g % 2][:, t, :], hg[g % 2][:, t, :], mh[:, 0, t:t + 1], ta[:, 4 + t:5 + t],
                                          ALU.subtract, ALU.mult).then_inc(tn.norm, 1)
                    if g < NG - 1:
                        front_c(n)
                    dve.wait_ge(tn.y, g + 1)
                    add_to_x(g * GB, GB, ps[:, 6, :], tg[:, 1, 3:4], tn.x)
                    lk.end()

            dve.wait_ge(ld.const, 16)
            dve.wait_ge(ld.x, 16)
            front_a(0, 0)
            front_b(0, 0)
            dve.wait_ge(su.zero, 4)
            dve.wait_ge(su.pe, 1)
            for i in range(4):
                o_ = ps[0:DC, i, 0:GB * SP].rearrange("p (b t) -> p b t", b=GB)[:, :, 0:SK]
                dve.tensor_copy(ctxT[0:DC, GB * i:GB * i + GB, 0:SK], o_).then_inc(su.dve, 1)
            front_c(0)
            dve.wait_ge(su.dve, 4)
            dve.wait_ge(ld.xrest, 16)
            dve.wait_ge(su.tanh, 1)
            heads8(0, 0)
            experts(0, 1)
            heads64()
            mixed()
            head128()
            experts(1, 5)
            heads8(1, 6)
            ternary()


_PASS = ["x", "ctx_768", "g_xattn", "g_ffn",
         "L0_xattn_wq", "L0_xattn_bq", "L0_xattn_wk", "L0_xattn_bk", "L0_xattn_wv", "L0_xattn_bv", "L0_xattn_wo",
         "L0_xattn_bo", "L0_ffn_uzman_embeddings", "L0_ffn_W1", "L0_ffn_b1", "L0_ffn_W2", "L0_ffn_b2",
         "L0_ffn_onbellek_durumu", "L1_xattn_Wq", "L1_xattn_Wk", "L1_xattn_Wv", "L1_xattn_Wo", "L1_xattn_bo",
         "L1_ffn_gate_w", "L1_ffn_gate_b", "L1_ffn_expert_w", "L1_ffn_expert_b", "L2_xattn_Wq", "L2_xattn_bq",
         "L2_xattn_Wk", "L2_xattn_bk", "L2_xattn_Wv", "L2_xattn_bv", "L2_ffn_rms_w", "L2_ffn_gate_w", "L2_ffn_W1",
         "L2_ffn_b1", "L2_ffn_W2", "L2_ffn_b2", "L3_xattn_Wq", "L3_xattn_bq", "L3_xattn_Wk", "L3_xattn_bk",
         "L3_xattn_Wv", "L3_xattn_bv", "L3_xattn_Wo", "L3_xattn_bo", "L3_ffn_W_fc", "L3_ffn_ln_w", "L3_ffn_ln_b",
         "L3_ffn_W_proj"]


def kernel(**inputs):
    import concourse.bacc as bacc
    import concourse.bass_utils as bass_utils

    nc = bacc.Bacc("TRN2", target_bir_lowering=False, num_devices=1)
    arrays, args = {}, {}
    given = {n: np.ascontiguousarray(inputs[n]) for n in _PASS}
    for n, src in (("L0_b1", "L0_ffn_b1"), ("L2_b1", "L2_ffn_b1"), ("ln_w", "L3_ffn_ln_w"), ("ln_b", "L3_ffn_ln_b")):
        given[n] = np.ascontiguousarray(np.asarray(inputs[src]).reshape(-1, P).T)
    for n in ("L0", "L2"):
        given[n + "_b2"] = np.ascontiguousarray(np.asarray(inputs[n + "_ffn_b2"]).T)
    given["const"] = constants()
    for n, v in given.items():
        arrays[f"in_{n}"] = v
        args[n] = nc.dram_tensor(f"in_{n}", v.shape, mybir.dt.from_np(v.dtype), kind="ExternalInput").ap()
    o = nc.dram_tensor("out_0", (B, P, D), F32, kind="ExternalOutput").ap()
    build(nc, args, o)
    r = bass_utils.run_bass_kernel_spmd(nc, [arrays], core_ids=[0])
    return r.results[0]["out_0"]
```
